# Optimizing a Trainium2 kernel written in Bass

```python
import numpy as np
import jax
import jax.numpy as jnp

def _softmax(x, axis=-1):
    return jax.nn.softmax(x, axis=axis)

def _gelu(x):
    return jax.nn.gelu(x, approximate=True)

def _silu(x):
    return jax.nn.silu(x)

def _sigmoid(x):
    return jax.nn.sigmoid(x)

def _layernorm(x, axis=-1, eps=1e-05):
    m = jnp.mean(x, axis=axis, keepdims=True)
    v = jnp.var(x, axis=axis, keepdims=True)
    return (x - m) / jnp.sqrt(v + eps)

def _scatter_add(tgt, idx, src, axis=0):
    return tgt.at[idx].add(src)

def _segment_sum(src, seg, n):
    return jax.ops.segment_sum(src, seg, n)
kernel_name = 'mk_flamingo_gated_d2_seqx_r4_3debd3'

def setup_inputs(seed: int=0):
    np.random.seed(seed)
    _w = jnp.asarray

    def _rec_inputs():
        import jax
        import jax.numpy as jnp
        _rk = jax.random.key(seed)
        x = 0.5 + 0.2887 * jax.random.normal(jax.random.fold_in(_rk, 1), (4, 512, 512), jnp.float32)
        _lenS = 512 - jax.random.randint(jax.random.fold_in(_rk, 7), (4,), 0, max(1, 512 // 4) + 1, jnp.int32)
        _lenS2 = 512 - jax.random.randint(jax.random.fold_in(_rk, 8), (4,), 0, max(1, 512 // 4) + 1, jnp.int32)
        _ctx_512P = jax.random.normal(jax.random.fold_in(_rk, 11), (4, 16, 128), jnp.float32)
        _ctx_512c = jax.random.dirichlet(jax.random.fold_in(_rk, 511), 0.3 * jnp.ones((16,), jnp.float32), (4, 512))
        _ctx_512t = jnp.einsum('bsk,bkd->bsd', _ctx_512c, _ctx_512P)
        _ctx_512t = _ctx_512t * jax.lax.rsqrt(jnp.mean(jnp.square(_ctx_512t)) + 1e-12) * 0.953939
        ctx_512 = -0.000392918 + 0.999932 * (_ctx_512t + 0.3 * jax.random.normal(jax.random.fold_in(_rk, 611), (4, 512, 128), jnp.float32))
        _g = jax.random.normal(jax.random.fold_in(_rk, 9001), (2, 2), jnp.float32)
        _g = jnp.sign(_g) * jnp.maximum(jnp.abs(_g), 1.0) + (_g == 0) * 1.0
        g_xattn = _g[0]
        g_ffn = _g[1]
        return (x, ctx_512, g_xattn, g_ffn)
    x, ctx_512, g_xattn, g_ffn = _rec_inputs()

    def _L0_xattn_setup():
        import jax, jax.numpy as jnp
        import numpy as np
        B, N, D = (16, 512, 128)
        H = 4
        TOP_K_RATIO = 0.3
        key = jax.random.key(seed)
        k1, k2, k3, k4 = jax.random.split(key, 4)
        h = jax.random.normal(k1, (B, N, D), dtype=jnp.float32)
        adj_raw = jax.random.uniform(k2, (B, N, N), dtype=jnp.float32)
        lim = 1.0 / np.sqrt(D)
        Wq = jax.random.uniform(k3, (D, D), minval=-lim, maxval=lim, dtype=jnp.float32)
        Wk = jax.random.uniform(k4, (D, D), minval=-lim, maxval=lim, dtype=jnp.float32)
        gamma_raw = jnp.float32(-0.85)
        return {'h': h, 'adj_raw': adj_raw, 'Wq': Wq, 'Wk': Wk, 'gamma_raw': gamma_raw}
    _L0_xattn_all = _L0_xattn_setup()
    _L0_xattn_in = {k: v for k, v in _L0_xattn_all.items() if k in ('Wq', 'Wk', 'gamma_raw')}
    del _L0_xattn_all

    def _L0_ffn_setup():
        import jax, jax.numpy as jnp
        import numpy as np
        B, S, H = (2, 512, 512)
        E, I, K = (8, 352, 2)
        SHARED_I = 352 * 2

        def _moe_forward(hidden_states, gate_w, w1, w3, w2, sw1, sw3, sw2):
            x = hidden_states.reshape(-1, H)
            T = x.shape[0]
            logits = x @ gate_w.T
            scores = jax.nn.softmax(logits, axis=-1)
            topk_w, topk_idx = jax.lax.top_k(scores, K)
            topk_w = topk_w / jnp.sum(topk_w, axis=-1, keepdims=True)
            h = jnp.einsum('th,ehi->eti', x, w1)
            g = jnp.einsum('th,ehi->eti', x, w3)
            y_all = jnp.einsum('eti,eih->eth', jax.nn.silu(h) * g, w2)
            tok = jnp.arange(T)[:, None]
            y_sel = y_all[topk_idx, tok]
            y = jnp.sum(y_sel * topk_w[..., None], axis=1)
            shared = jax.nn.silu(x @ sw1) * (x @ sw3) @ sw2
            return (y + shared).reshape(hidden_states.shape)
        key = jax.random.key(seed)
        ks = jax.random.split(key, 8)
        s = 0.02
        return {'hidden_states': jax.random.normal(ks[0], (B, S, H), jnp.float32), 'gate_w': jax.random.normal(ks[1], (E, H), jnp.float32) * s, 'w1': jax.random.normal(ks[2], (E, H, I), jnp.float32) * s, 'w3': jax.random.normal(ks[3], (E, H, I), jnp.float32) * s, 'w2': jax.random.normal(ks[4], (E, I, H), jnp.float32) * s, 'sw1': jax.random.normal(ks[5], (H, SHARED_I), jnp.float32) * s, 'sw3': jax.random.normal(ks[6], (H, SHARED_I), jnp.float32) * s, 'sw2': jax.random.normal(ks[7], (SHARED_I, H), jnp.float32) * s}
    _L0_ffn_all = _L0_ffn_setup()
    _L0_ffn_in = {k: v for k, v in _L0_ffn_all.items() if k in ('gate_w', 'w1', 'w3', 'w2', 'sw1', 'sw3', 'sw2')}
    del _L0_ffn_all

    def _L1_xattn_setup():
        import jax, jax.numpy as jnp
        import numpy as np
        import math
        NUM_Q_HEADS = 32
        NUM_KV_HEADS = 8
        key = jax.random.key(seed)
        k1, k2, k3 = jax.random.split(key, 3)
        B, S, E = (2, 512, 512)
        kv_E = NUM_KV_HEADS * (E // NUM_Q_HEADS)
        q = jax.random.normal(k1, (B, S, E), dtype=jnp.float32)
        k = jax.random.normal(k2, (B, S, kv_E), dtype=jnp.float32)
        v = jax.random.normal(k3, (B, S, kv_E), dtype=jnp.float32)
        return {'q': q, 'k': k, 'v': v}
    _L1_xattn_all = _L1_xattn_setup()
    _L1_xattn_in = {k: v for k, v in _L1_xattn_all.items() if k in ()}
    del _L1_xattn_all

    def _L1_ffn_setup():
        import jax, jax.numpy as jnp
        import numpy as np
        _FP8_MAX = 448.0
        _BLOCK = 32
        _EPS = 1e-30

        def _mx_dequant(t):
            rows, feat = t.shape
            blocks = t.reshape(rows, feat // _BLOCK, _BLOCK)
            max_abs = jnp.max(jnp.abs(blocks), axis=-1)
            scales = jnp.maximum(max_abs / _FP8_MAX, _EPS)
            q = (blocks / scales[..., None]).astype(jnp.float8_e4m3fn).astype(jnp.float32)
            return (q * scales[..., None]).reshape(rows, feat)

        def _mx_linear(x2d, w):
            return _mx_dequant(x2d) @ _mx_dequant(w).T
        key = jax.random.key(seed)
        k1, k2, k3, k4 = jax.random.split(key, 4)
        B, S, H, I = (2, 256, 512, 2048)
        return {'x': jax.random.normal(k1, (B, S, H), dtype=jnp.float32), 'gate_w': jax.random.normal(k2, (I, H), dtype=jnp.float32) * 0.02, 'up_w': jax.random.normal(k3, (I, H), dtype=jnp.float32) * 0.02, 'down_w': jax.random.normal(k4, (H, I), dtype=jnp.float32) * 0.02}
    _L1_ffn_all = _L1_ffn_setup()
    _L1_ffn_in = {k: v for k, v in _L1_ffn_all.items() if k in ('gate_w', 'up_w', 'down_w')}
    del _L1_ffn_all
    return {'x': x, 'ctx_512': ctx_512, 'g_xattn': g_xattn, 'g_ffn': g_ffn, 'L0_xattn_Wq': _L0_xattn_in['Wq'], 'L0_xattn_Wk': _L0_xattn_in['Wk'], 'L0_xattn_gamma_raw': _L0_xattn_in['gamma_raw'], 'L0_ffn_gate_w': _L0_ffn_in['gate_w'], 'L0_ffn_w1': _L0_ffn_in['w1'], 'L0_ffn_w3': _L0_ffn_in['w3'], 'L0_ffn_w2': _L0_ffn_in['w2'], 'L0_ffn_sw1': _L0_ffn_in['sw1'], 'L0_ffn_sw3': _L0_ffn_in['sw3'], 'L0_ffn_sw2': _L0_ffn_in['sw2'], 'L1_ffn_gate_w': _L1_ffn_in['gate_w'], 'L1_ffn_up_w': _L1_ffn_in['up_w'], 'L1_ffn_down_w': _L1_ffn_in['down_w']}

def reference(x, ctx_512, g_xattn, g_ffn, L0_xattn_Wq, L0_xattn_Wk, L0_xattn_gamma_raw, L0_ffn_gate_w, L0_ffn_w1, L0_ffn_w3, L0_ffn_w2, L0_ffn_sw1, L0_ffn_sw3, L0_ffn_sw2, L1_ffn_gate_w, L1_ffn_up_w, L1_ffn_down_w):
    import jax
    import jax.numpy as jnp

    def _L0_xattn_ref(h, adj_raw, Wq, Wk, gamma_raw):
        import jax, jax.numpy as jnp
        import numpy as np
        B, N, D = (16, 512, 128)
        H = 4
        TOP_K_RATIO = 0.3
        b, n, dm = h.shape
        d = dm // H
        Q = (h @ Wq.T).reshape(b, n, H, d).transpose(0, 2, 1, 3)
        K = (h @ Wk.T).reshape(b, n, H, d).transpose(0, 2, 1, 3)
        sim = jnp.einsum('bhnd,bhmd->bnm', Q, K) / (jnp.sqrt(jnp.float32(d)) * H)
        k = max(1, int(n * TOP_K_RATIO))
        topk_vals = jax.lax.top_k(sim, k)[0]
        threshold = topk_vals[:, :, -1:]
        sparse_mask = (sim >= threshold).astype(sim.dtype)
        A_learned = jax.nn.sigmoid(sim) * sparse_mask
        A_learned = (A_learned + jnp.swapaxes(A_learned, -1, -2)) * 0.5
        gamma = jax.nn.sigmoid(gamma_raw)
        return (1.0 - gamma) * adj_raw + gamma * A_learned

    def _L0_ffn_ref(hidden_states, gate_w, w1, w3, w2, sw1, sw3, sw2):
        import jax, jax.numpy as jnp
        import numpy as np
        B, S, H = (2, 512, 512)
        E, I, K = (8, 352, 2)
        SHARED_I = 352 * 2

        def _moe_forward(hidden_states, gate_w, w1, w3, w2, sw1, sw3, sw2):
            x = hidden_states.reshape(-1, H)
            T = x.shape[0]
            logits = x @ gate_w.T
            scores = jax.nn.softmax(logits, axis=-1)
            topk_w, topk_idx = jax.lax.top_k(scores, K)
            topk_w = topk_w / jnp.sum(topk_w, axis=-1, keepdims=True)
            h = jnp.einsum('th,ehi->eti', x, w1)
            g = jnp.einsum('th,ehi->eti', x, w3)
            y_all = jnp.einsum('eti,eih->eth', jax.nn.silu(h) * g, w2)
            tok = jnp.arange(T)[:, None]
            y_sel = y_all[topk_idx, tok]
            y = jnp.sum(y_sel * topk_w[..., None], axis=1)
            shared = jax.nn.silu(x @ sw1) * (x @ sw3) @ sw2
            return (y + shared).reshape(hidden_states.shape)
        return _moe_forward(hidden_states, gate_w, w1, w3, w2, sw1, sw3, sw2)

    def _L1_xattn_ref(q, k, v):
        import jax, jax.numpy as jnp
        import numpy as np
        import math
        NUM_Q_HEADS = 32
        NUM_KV_HEADS = 8
        B, S, E = q.shape
        H, KV = (NUM_Q_HEADS, NUM_KV_HEADS)
        D = E // H
        G = H // KV
        scale = math.sqrt(D)
        qh = q.reshape(B, S, KV, G, D).transpose(0, 2, 3, 1, 4)
        kh = k.reshape(B, S, KV, D).transpose(0, 2, 1, 3)
        vh = v.reshape(B, S, KV, D).transpose(0, 2, 1, 3)
        scores = jnp.einsum('bkgsd,bktd->bkgst', qh, kh) / scale
        weights = jax.nn.softmax(scores, axis=-1)
        out = jnp.einsum('bkgst,bktd->bkgsd', weights, vh)
        return out.transpose(0, 3, 1, 2, 4).reshape(B, S, E)

    def _L1_ffn_ref(x, gate_w, up_w, down_w):
        import jax, jax.numpy as jnp
        import numpy as np
        _FP8_MAX = 448.0
        _BLOCK = 32
        _EPS = 1e-30

        def _mx_dequant(t):
            rows, feat = t.shape
            blocks = t.reshape(rows, feat // _BLOCK, _BLOCK)
            max_abs = jnp.max(jnp.abs(blocks), axis=-1)
            scales = jnp.maximum(max_abs / _FP8_MAX, _EPS)
            q = (blocks / scales[..., None]).astype(jnp.float8_e4m3fn).astype(jnp.float32)
            return (q * scales[..., None]).reshape(rows, feat)

        def _mx_linear(x2d, w):
            return _mx_dequant(x2d) @ _mx_dequant(w).T
        B, S, H = x.shape
        x2d = x.reshape(B * S, H)
        gate = _mx_linear(x2d, gate_w)
        up = _mx_linear(x2d, up_w)
        h = jax.nn.silu(gate) * up
        out = _mx_linear(h, down_w)
        return out.reshape(B, S, H)
    x = x + jnp.tanh(g_xattn[0]) * _L0_xattn_ref(ctx_512, _layernorm(x, axis=-1), L0_xattn_Wq, L0_xattn_Wk, L0_xattn_gamma_raw)
    x = x + jnp.tanh(g_ffn[0]) * _L0_ffn_ref(_layernorm(x, axis=-1), L0_ffn_gate_w, L0_ffn_w1, L0_ffn_w3, L0_ffn_w2, L0_ffn_sw1, L0_ffn_sw3, L0_ffn_sw2)
    x = x + jnp.tanh(g_xattn[1]) * _L1_xattn_ref(_layernorm(x, axis=-1), ctx_512, ctx_512)
    x = x + jnp.tanh(g_ffn[1]) * _L1_ffn_ref(_layernorm(x, axis=-1), L1_ffn_gate_w, L1_ffn_up_w, L1_ffn_down_w)
    return x

_drawn_inputs = setup_inputs


def setup_inputs(seed=0):
    import zlib

    import numpy as np

    out = dict(_drawn_inputs(seed))
    spreads = {'g_ffn': (-1.0, 0.6)}
    factors = {'L0_ffn_gate_w': 3.453, 'L0_ffn_w1': 3.031, 'L0_ffn_w3': 2.969, 'L0_ffn_w2': 2.972}
    for name, (base, spread) in spreads.items():
        noise = np.random.default_rng([zlib.crc32(name.encode()), seed]).standard_normal(out[name].shape)
        drawn = base * np.exp(spread * noise) if base else spread * noise
        out[name] = jnp.asarray(drawn.astype(out[name].dtype))
    for name, factor in factors.items():
        out[name] = (out[name] * factor).astype(out[name].dtype)
    return out
```

```python
from contextlib import ExitStack

import concourse.bass as bass
from concourse import mybir

P = 128
F32 = mybir.dt.float32
F16 = mybir.dt.float16
I32 = mybir.dt.int32
U32 = mybir.dt.uint32
ALU = mybir.AluOpType
ACT = mybir.ActivationFunctionType
AX_X = mybir.AxisListType.X
NEG = -3.0e38
LN_EPS = 1e-5
ROUND = 12582912.0
W_SCALE = 256.0
A_SCALE = 16.0


class Chain:

    def __init__(self, engine, sem):
        self.engine, self.sem, self.n = engine, sem, 0

    def restart(self):
        self.engine.sem_clear(self.sem)
        self.n = 0

    def __call__(self, instruction):
        self.n += 1
        instruction.then_inc(self.sem, 1)
        self.engine.wait_ge(self.sem, self.n)


def build(nc, x, ctx, g_xattn, g_ffn, wq, wk, gamma_raw, gate_w, w1, w3, w2, sw1, sw3, sw2,
          fgate_w, fup_w, fdown_w, out):
    B, S, D = x.shape
    C = ctx.shape[2]
    E, _, I = w1.shape
    T = B * S
    TT = T // P
    R = S // P
    KD = D // P
    TOPK = int(S * 0.3)
    KI = (I + P - 1) // P
    I_LAST = I - (KI - 1) * P
    SLOTS = 2 * TT + E
    E2 = 2

    stack = ExitStack()
    with stack:
        def sb(name, shape, dt=F32):
            return stack.enter_context(nc.sbuf_tensor(name, shape, dt))

        def sem(name):
            return stack.enter_context(nc.semaphore(name))

        PS = stack.enter_context(nc.psum_tensor("PS", [P, 8, 512], F32))
        bank = [PS[:, i, :] for i in range(8)]

        X = sb("X", [P, TT, D])
        BIG = sb("BIG", [P, 34816])
        WORK = sb("WORK", [P, 9728])
        ident = sb("ident", [P, P])
        MV = sb("MV", [P, TT, 2])
        RSTD = sb("RSTD", [P, TT])
        NEWT = sb("NEWT", [P, 2, TT])
        GATES = sb("GATES", [P, 8])
        used = {}

        def carve(region, name, at, shape, dt=F32):
            n = 1
            for s in shape[1:]:
                n *= s
            size = n * (2 if dt == F16 else 4)
            words = (size + 3) // 4
            assert at % 4 == 0 and at // 4 + words <= region.shape[1], (name, at, size)
            v = region[0:shape[0], at // 4:at // 4 + words]
            if dt != F32:
                v = v.bitcast(dt)
            if len(shape) == 3:
                v = v.rearrange("p (a b) -> p a b", b=shape[2])
            elif len(shape) == 4:
                v = v.rearrange("p (a b c) -> p a b c", b=shape[2], c=shape[3])
            elif len(shape) == 5:
                v = v.rearrange("p (a b c d) -> p a b c d", b=shape[2], c=shape[3], d=shape[4])
            return v

        x_in = [sem(f"x_in{b}") for b in range(B)]
        ctx_in = sem("ctx_in")
        wqk_in = sem("wqk_in")
        gates_in = sem("gates_in")
        ident_ok = sem("ident_ok")
        dve_chain = sem("dve_chain")
        act_chain = sem("act_chain")
        pool_chain = sem("pool_chain")
        gates_ok = sem("gates_ok")
        out_done = sem("out_done")
        finished = sem("finished")

        block = stack.enter_context(nc.Block())
        ctx_rows = ctx.rearrange("b (r p) c -> p (b r) c", p=P)
        x_rows = x.rearrange("b (r p) d -> p (b r) d", p=P)
        out_rows = out.rearrange("b (r p) d -> p (b r) d", p=P)

        ctx_tok = carve(WORK, "ctx_tok", 0, [P, TT, C])
        sim = carve(WORK, "sim", 0, [P, R, S])
        ctxT = carve(WORK, "ctxT", 8192, [P, T])
        qT = carve(WORK, "qT", 16384, [P, S])
        kT = carve(WORK, "kT", 18432, [P, S])
        topw = carve(WORK, "topw", 20480, [P, S])
        sig = carve(WORK, "sig", 22528, [P, 2, S])
        wqk = carve(WORK, "wqk", 26624, [P, 2, P])
        wqkT = carve(WORK, "wqkT", 27648, [P, 2, P])
        AL = carve(WORK, "AL", 28672, [P, TT])
        BE = carve(WORK, "BE", 28736, [P, TT])
        top8 = carve(WORK, "top8", 28800, [P, 8])
        th = carve(WORK, "th", 28832, [P, R])
        bnst = carve(WORK, "bnst", 28864, [P, 6])
        srow = [carve(WORK, f"srow{i}", 37632 + i * 4 * R, [P, R]) for i in range(9)]
        th_try, spread_, step, gain, count0, count1, diff, outside, rank = srow
        smv = carve(WORK, "smv", 37632 + 36 * R, [P, R, 2])
        top16 = carve(WORK, "top16", 37632 + 44 * R, [P, R, 2 * 8])
        pick = carve(WORK, "pick", 37632 + 108 * R, [P, R, 2 * 8])
        missed = carve(WORK, "missed", 37632 + 172 * R, [P, R], F16)
        misses = carve(WORK, "misses", 37632 + 174 * R, [P, 1])
        missed_any = carve(WORK, "missed_any", 37632 + 175 * R, [P, 1], I32)
        WINDOW = 2 * 8
        AIM = TOPK - (WINDOW + 1) / 2.0
        TRIES = 3
        SIM_SCALE = 1.0 / (float(C // 4) ** 0.5 * 4)

        ctxT_mm = sem("ctxT_mm")
        ctxT_sb = sem("ctxT_sb")
        coef_ok = sem("coef_ok")
        qk_mm = sem("qk_mm")
        qk_sb = sem("qk_sb")
        sim_mm = sem("sim_mm")
        sim_sb = sem("sim_sb")
        sig_sb = sem("sig_sb")
        xmix = sem("xmix")
        adj_ok = sem("adj_ok")
        adjT_mm = sem("adjT_mm")
        x1_ok = sem("x1_ok")
        missed_ok = sem("missed_ok")
        missed_mm = sem("missed_mm")

        def rsqrt(link, var, y, n):
            a, b = NEWT[:, 0, 0:n], NEWT[:, 1, 0:n]
            v = nc.vector
            link(v.tensor_scalar(a, var, LN_EPS, None, ALU.add))
            link(v.tensor_scalar(y.bitcast(I32), a.bitcast(I32), -0.5, 1597463007.0, ALU.mult, ALU.add))
            for _ in range(4):
                link(v.tensor_tensor(b, y, y, ALU.mult))
                link(v.tensor_tensor(b, b, a, ALU.mult))
                link(v.tensor_scalar(b, b, -0.5, 1.5, ALU.mult, ALU.add))
                link(v.tensor_tensor(y, y, b, ALU.mult))

        def stats(link, tiles, st):
            for t in tiles:
                link(nc.vector.bn_stats(st, X[:, t, :]))
                link(nc.vector.bn_aggr(MV[:, t, :], st))
            a, b = tiles[0], tiles[-1] + 1
            rsqrt(link, MV[:, a:b, 1], RSTD[:, a:b], b - a)

        W13N = 2 * KD * 2 * I
        W2N = 2 * KI * D
        W13 = BIG[:, 0:E * W13N // 2].bitcast(F16)
        W2 = BIG[:, E * W13N // 2:E * (W13N + W2N) // 2].bitcast(F16)
        NBUF = 3
        stage = [carve(WORK, f"stage{i}", 28928 + i * 2816, [P, 704]) for i in range(NBUF)]
        stage_in = [sem(f"stage_in{i}") for i in range(NBUF)]
        split_s = sem("split_s")
        split_h = sem("split_h")
        split_l = sem("split_l")
        pad_ok = sem("pad_ok")
        CHUNKS = [(0, 0, 2), (0, 2, 2), (1, 0, 2), (1, 2, 2), (2, 0, 1), (2, 1, 1), (2, 2, 1)]
        NCH = len(CHUNKS)
        PER_BUF = [len(range(i, NCH, NBUF)) for i in range(NBUF)]

        def rows_of(m, k0, nk):
            return I_LAST if m == 2 and k0 == KI - 1 else P

        def chunk_src(j, src):
            m, k0, nk = CHUNKS[j]
            a = src[m]
            if m < 2:
                return a[k0 * P:(k0 + nk) * P, :].rearrange("(k p) i -> p k i", p=P)
            return a[k0 * P:k0 * P + rows_of(m, k0, nk), :]

        def chunk_stage(j):
            m, k0, nk = CHUNKS[j]
            b = stage[j % NBUF]
            if m < 2:
                return b[:, 0:2 * I].rearrange("p (k i) -> p k i", k=2)
            return b[0:rows_of(m, k0, nk), 0:D]

        def chunk_dst(j, slot, lo):
            m, k0, nk = CHUNKS[j]
            if m < 2:
                v = W13[:, bass.ds(slot * W13N + lo * (W13N // 2) + k0 * 2 * I, 2 * 2 * I)]
                return v.rearrange("p (k m i) -> p k m i", k=2, m=2)[:, :, m, :]
            return W2[0:rows_of(m, k0, nk), bass.ds(slot * W2N + lo * (W2N // 2) + k0 * D, D)]

        def load_slot(sp, n, src):
            for j in range(NCH):
                sp.wait_ge(split_l, n * NCH + (1 + max(j - NBUF + 1, 0)))
                sp.dma_start(chunk_stage(j), chunk_src(j, src)).then_inc(stage_in[j % NBUF], 16)

        def split_hi(act, n, slot):
            for j in range(NCH):
                act.wait_ge(stage_in[j % NBUF], n * (16 * PER_BUF[j % NBUF]) + 16 * (j // NBUF + 1))
                nc.scalar.activation(chunk_stage(j), chunk_stage(j), ACT.Copy, scale=W_SCALE).then_inc(split_s, 1)
                act.wait_ge(split_s, n * NCH + (j + 1))
                nc.scalar.activation(chunk_dst(j, slot, 0), chunk_stage(j), ACT.Copy).then_inc(split_h, 1)

        def split_lo(pool, n, slot):
            for j in range(NCH):
                pool.wait_ge(split_h, n * NCH + (j + 1))
                nc.gpsimd.tensor_tensor(chunk_dst(j, slot, 1), chunk_stage(j), chunk_dst(j, slot, 0),
                                        ALU.subtract).then_inc(split_l, 1)

        def expert_src(e):
            return w1[e, :, :], w3[e, :, :], w2[e, :, :]

        def shared_src(h):
            return sw1[:, h * I:(h + 1) * I], sw3[:, h * I:(h + 1) * I], sw2[h * I:(h + 1) * I, :]

        def a_sync(sp):
            sp.dma_start(wqk[:, 0, :], wq).then_inc(wqk_in, 16)
            sp.dma_start(wqk[:, 1, :], wk).then_inc(wqk_in, 16)
            sp.dma_start(ctx_tok, ctx_rows).then_inc(ctx_in, 16)
            sp.dma_start(GATES[:, 0:2], g_xattn.rearrange("(a n) -> a n", a=1).to_broadcast([P, 2])).then_inc(gates_in, 16)
            sp.dma_start(GATES[:, 2:4], g_ffn.rearrange("(a n) -> a n", a=1).to_broadcast([P, 2])).then_inc(gates_in, 16)
            sp.dma_start(GATES[:, 4:5], gamma_raw.rearrange("(a n) -> a n", a=1).to_broadcast([P, 1])).then_inc(gates_in, 16)
            for p in range(2):
                w_load(sp, 0, p)
            for b in range(B):
                sp.dma_start(X[:, b * R:(b + 1) * R, :], x_rows[:, b * R:(b + 1) * R, :]).then_inc(x_in[b], 16)
            for p in range(2):
                w_store(sp, 0, p)
            with sp.Fori(0, 2) as b:
                for c in (2, 3):
                    w_load(sp, b, c)
                for c in (4, 5):
                    w_load(sp, b, c)
                for c in (2, 3):
                    w_store(sp, b, c)
                for i in range(2):
                    load_slot(sp, b * 2 + i, expert_src(b * 2 + i))
                for c in (4, 5):
                    w_store(sp, b, c)
            for c in (2, 3):
                w_load(sp, 2, c)
            load_slot(sp, 4, expert_src(4))
            for c in (2, 3):
                w_store(sp, 2, c)
            for h in range(2):
                load_slot(sp, 5 + h, shared_src(h))

        def a_gpsimd(pool):
            link = Chain(pool, pool_chain)
            nc.gpsimd.nop().then_inc(split_l, 1)
            link(nc.gpsimd.memset(ident[:, :], 0.0))
            nc.gpsimd.affine_select(out=ident[:, :], in_=ident[:, :], compare_op=ALU.not_equal, fill=1.0,
                                    base=0, pattern=[[-1, P]], channel_multiplier=1).then_inc(ident_ok, 1)
            b_constants(pool, link)
            w_pool(pool, 0, 0)
            with pool.Fori(0, 2) as b:
                w_pool(pool, b, 2)
                w_pool(pool, b, 4)
                for i in range(2):
                    split_lo(pool, b * 2 + i, b * 2 + i)
            w_pool(pool, 2, 2)
            split_lo(pool, 4, 4)
            for p in range(2):
                pool.wait_ge(fw_st[p], 16 * NW // 2)
            pool.wait_ge(split_l, 5 * NCH + 1)
            pads(link, range(5, E))
            nc.gpsimd.nop().then_inc(pad_ok, 1)
            for h in range(2):
                split_lo(pool, 5 + h, E - 2 + h)

        def a_scalar(act):
            link = Chain(act, act_chain)
            act.wait_ge(gates_in, 48)
            link(nc.scalar.activation(GATES[:, 0:4], GATES[:, 0:4], ACT.Tanh))
            nc.scalar.activation(GATES[:, 4:5], GATES[:, 4:5], ACT.Sigmoid).then_inc(gates_ok, 1)
            for c in range(4):
                act.wait_ge(ctxT_mm, c + 1)
                nc.scalar.activation(ctxT[:, c * 512:(c + 1) * 512], bank[c][:, :], ACT.Copy).then_inc(ctxT_sb, 1)
            act.wait_ge(ctxT_mm, 5)
            nc.scalar.activation(wqkT.rearrange("p a b -> p (a b)"), bank[4][:, 0:2 * P], ACT.Copy).then_inc(ctxT_sb, 1)
            def head(b, first):
                for i, (dst, src) in enumerate(((qT, bank[2]), (kT, bank[3]))):
                    act.wait_ge(qk_mm, b * 2 + (i + 1))
                    nc.scalar.activation(dst, src[:, :], ACT.Copy).then_inc(qk_sb, 1)
                for r in range(R):
                    act.wait_ge(sim_mm, b * R + (r + 1))
                    nc.scalar.activation(sim[:, r, :], bank[4 + r][:, :], ACT.Copy).then_inc(sim_sb, 1)
                if first:
                    act.wait_ge(coef_ok, 1)
                for r in range(R):
                    xt = X[:, b * R + r, :]
                    nc.scalar.activation(xt, xt, ACT.Identity, scale=AL[:, bass.ds(b * R + r, 1)],
                                         bias=BE[:, bass.ds(b * R + r, 1)]).then_inc(xmix, 1)

            def sigmoids(b):
                act.wait_ge(sim_sb, b * R + R)
                for r in range(R):
                    if r >= 2:
                        act.wait_ge(adj_ok, b * R + (r - 1))
                    nc.scalar.activation(sig[:, r % 2, :], sim[:, r, :], ACT.Sigmoid, scale=SIM_SCALE).then_inc(sig_sb, 1)

            w_act_up(act, 0, 0)
            head(0, True)
            w_act_hi(act, 0, 0, True)
            with act.Fori(0, 2) as b:
                sigmoids(b)
                head(b + 1, False)
                for c in (2, 4):
                    w_act_up(act, b, c)
                    w_act_hi(act, b, c, False)
                for i in range(2):
                    split_hi(act, b * 2 + i, b * 2 + i)
            sigmoids(2)
            head(3, False)
            w_act_up(act, 2, 2)
            w_act_hi(act, 2, 2, False)
            split_hi(act, 4, 4)
            sigmoids(3)
            for p in range(2):
                act.wait_ge(fw_st[p], 16 * NW // 2)
            for h in range(2):
                split_hi(act, 5 + h, E - 2 + h)

        def a_tensor(pe):
            pe.wait_ge(ident_ok, 1)
            pe.wait_ge(ctx_in, 16)
            for c in range(4):
                for j in range(4):
                    ins = nc.tensor.transpose(bank[c][:, j * P:(j + 1) * P], ctx_tok[:, c * 4 + j, :], ident[:, :])
                ins.then_inc(ctxT_mm, 1)
            pe.wait_ge(wqk_in, 32)
            for j in range(2):
                ins = nc.tensor.transpose(bank[4][:, j * P:(j + 1) * P], wqk[:, j, :], ident[:, :])
            ins.then_inc(ctxT_mm, 1)
            pe.wait_ge(ctxT_sb, 5)
            def head(b):
                for i in range(2):
                    nc.tensor.matmul(bank[2 + i][:, :], wqkT[:, i, :], ctxT[:, bass.ds(b * S, S)],
                                     start=True, stop=True).then_inc(qk_mm, 1)
                pe.wait_ge(qk_sb, b * 2 + 2)
                for r in range(R):
                    nc.tensor.matmul(bank[4 + r][:, :], qT[:, r * P:(r + 1) * P], kT, start=True, stop=True).then_inc(sim_mm, 1)

            def rest(b):
                pe.wait_ge(missed_ok, b + 1)
                nc.tensor.matmul(bank[0][:, 0:R], ONES[:, :], missed, start=True, stop=True).then_inc(missed_mm, 1)
                pe.wait_ge(adj_ok, b * R + R)
                for r in range(R):
                    for c in range(R):
                        ins = nc.tensor.transpose(bank[r][:, c * P:(c + 1) * P], sim[:, c, r * P:(r + 1) * P], ident[:, :])
                    ins.then_inc(adjT_mm, 1)

            head(0)
            w_transpose(pe, 0, 0, True)
            pe.wait_ge(const_ok, 1)
            with pe.Fori(0, 2) as b:
                rest(b)
                pe.wait_ge(x1_ok, b * R + R)
                head(b + 1)
                for c in (2, 4):
                    w_transpose(pe, b, c, False)
            rest(2)
            pe.wait_ge(x1_ok, 3 * R)
            head(3)
            w_transpose(pe, 2, 2, False)
            rest(3)

        def a_vector(dve):
            link = Chain(dve, dve_chain)
            v = nc.vector
            w_scales(dve, link, 0, 0)
            for b in range(B):
                dve.wait_ge(x_in[b], 16)
            stats(link, range(TT), bnst)
            dve.wait_ge(gates_ok, 1)
            link(v.tensor_tensor(GATES[:, 6:7], GATES[:, 0:1], GATES[:, 4:5], ALU.mult))
            link(v.tensor_tensor(GATES[:, 5:6], GATES[:, 0:1], GATES[:, 6:7], ALU.subtract))
            link(v.tensor_scalar(GATES[:, 6:7], GATES[:, 6:7], 0.5, None, ALU.mult))
            link(v.tensor_scalar(AL, RSTD[:, :], GATES[:, 5:6], None, ALU.mult))
            link(v.scalar_tensor_tensor(BE, AL, -1.0, MV[:, :, 0], ALU.mult, ALU.mult))
            v.tensor_scalar(AL, AL, 1.0, None, ALU.add).then_inc(coef_ok, 1)
            w_round(dve, link, 0, 0)
            dve.wait_ge(const_ok, 1)

            def search(b):
                link.restart()
                dve.wait_ge(sim_sb, b * R + R)
                v.nop(nofuse=True)
                for r in range(R):
                    link(v.bn_stats(bnst, sim[:, r, :]))
                    link(v.bn_aggr(smv[:, r, :], bnst))
                link(v.tensor_scalar(spread_.bitcast(I32), smv[:, :, 1].bitcast(I32), 0.5, 532487669.0, ALU.mult, ALU.add))
                link(v.scalar_tensor_tensor(th_try, spread_, 0.52, smv[:, :, 0], ALU.mult, ALU.add))
                link(v.tensor_scalar(gain, spread_, 1.0 / (0.36 * S), None, ALU.mult))
                for n in range(TRIES):
                    count, last = (count0, count1) if n % 2 == 0 else (count1, count0)
                    for r in range(R):
                        link(v.tensor_scalar(topw, sim[:, r, :], th_try[:, r:r + 1], None, ALU.is_ge, ALU.add,
                                             accum_out=count[:, r:r + 1]))
                    if n:
                        link(v.tensor_tensor(diff, count, last, ALU.subtract))
                        link(v.scalar_tensor_tensor(diff, diff, -1.0, diff, ALU.mult, ALU.max))
                        link(v.tensor_scalar(diff, diff, 1.0, None, ALU.max))
                        link(v.reciprocal(diff, diff))
                        link(v.scalar_tensor_tensor(step, step, -1.0, step, ALU.mult, ALU.max))
                        link(v.tensor_tensor(gain, step, diff, ALU.mult))
                    link(v.tensor_scalar(outside, count, -AIM, None, ALU.add))
                    link(v.tensor_tensor(step, outside, gain, ALU.mult))
                    link(v.tensor_tensor(outside, outside, outside, ALU.mult))
                    link(v.tensor_scalar(outside, outside, WINDOW ** 2 / 4.0, None, ALU.is_gt))
                    link(v.tensor_tensor(step, step, outside, ALU.mult))
                    link(v.tensor_tensor(th_try, th_try, step, ALU.add))

            def threshold(b):
                link.restart()
                for r in range(R):
                    link(v.tensor_scalar(topw, sim[:, r, :], th_try[:, r:r + 1], None, ALU.is_ge, ALU.add,
                                         accum_out=rank[:, r:r + 1]))
                    link(v.scalar_tensor_tensor(topw, topw, NEG, sim[:, r, :], ALU.mult, ALU.add))
                    link(v.max(top16[:, r, 0:8], topw))
                    link(v.match_replace(topw, top16[:, r, 0:8], topw, NEG))
                    link(v.max(top16[:, r, 8:16], topw))
                link(v.tensor_scalar(rank, rank, -1.0, TOPK - 1.0, ALU.mult, ALU.add))
                link(v.tensor_scalar(outside, rank, (1.0 - WINDOW) / 2.0, None, ALU.add))
                link(v.tensor_tensor(outside, outside, outside, ALU.mult))
                v.tensor_scalar(missed, outside, WINDOW ** 2 / 4.0, None, ALU.is_gt).then_inc(missed_ok, 1)
                link(v.tensor_tensor(pick, IOTA[:, 0:WINDOW].unsqueeze(1).to_broadcast([P, R, WINDOW]),
                                     rank.unsqueeze(2).to_broadcast([P, R, WINDOW]), ALU.is_equal))
                link(v.tensor_tensor(pick, pick, top16, ALU.mult))
                link(v.tensor_reduce(th, pick, AX_X, ALU.add))
                dve.wait_ge(missed_mm, b + 1)
                v.nop(nofuse=True)
                link(v.tensor_reduce(misses, bank[0][:, 0:R], AX_X, ALU.add))
                link(v.tensor_copy(missed_any, misses))
                some = dve.value_load(missed_any[0:1, 0:1], min_val=0, max_val=P * R)
                with dve.If(some > 0):
                    for r in range(R):
                        link.restart()
                        link(v.tensor_copy(topw, sim[:, r, :]))
                        with dve.Fori(0, (TOPK - 1) // 8):
                            link.restart()
                            link(v.max(top8, topw))
                            link(v.match_replace(topw, top8, topw, NEG))
                        link.restart()
                        link(v.max(top8, topw))
                        k = (TOPK - 1) % 8
                        link(v.tensor_copy(th[:, r:r + 1], top8[:, k:k + 1]))
                link.restart()

            def mix(b):
                for r in range(R):
                    dve.wait_ge(sig_sb, b * R + (r + 1))
                    v.scalar_tensor_tensor(sim[:, r, :], sim[:, r, :], th[:, r:r + 1], sig[:, r % 2, :],
                                           ALU.is_ge, ALU.mult).then_inc(adj_ok, 1)
                dve.wait_ge(adj_ok, b * R + R)
                for r in range(R):
                    xt = X[:, b * R + r, :]
                    dve.wait_ge(xmix, b * R + (r + 1))
                    link(v.scalar_tensor_tensor(xt, sim[:, r, :], GATES[:, 6:7], xt, ALU.mult, ALU.add))
                    dve.wait_ge(adjT_mm, b * R + (r + 1))
                    v.scalar_tensor_tensor(xt, bank[r][:, :], GATES[:, 6:7], xt, ALU.mult, ALU.add).then_inc(x1_ok, 1)

            with dve.Fori(0, 2) as b:
                search(b)
                w_low(dve, b, 0)
                threshold(b)
                mix(b)
                w_scales(dve, link, b, 2)
                w_round(dve, link, b, 2)
                w_scales(dve, link, b, 4)
                w_low(dve, b, 2)
                w_round(dve, link, b, 4)
            search(2)
            w_low(dve, 2, 0)
            threshold(2)
            mix(2)
            w_scales(dve, link, 2, 2)
            w_round(dve, link, 2, 2)
            search(3)
            w_low(dve, 2, 2)
            threshold(3)
            mix(3)


        xn = carve(WORK, "xn", 0, [P, 2, D])
        xT = carve(WORK, "xT", 4096, [P, 2, 2, KD * P], F16)
        sil = carve(WORK, "sil", 8192, [P, 2, I])
        hid = carve(WORK, "hid", 11264, [P, 2, KI * P])
        hT = carve(WORK, "hT", 14336, [P, 2, 2, KI * P], F16)
        yo = carve(WORK, "yo", 17408, [P, 2, D])
        LG = carve(WORK, "LG", 21504, [P, TT, E])
        MX = carve(WORK, "MX", 22016, [P, TT, 8])
        MI = carve(WORK, "MI", 22528, [P, TT, 8], U32)
        MIF = carve(WORK, "MIF", 23040, [P, TT, 8])
        OH = carve(WORK, "OH", 23552, [P, E2, TT, E])
        EQ = carve(WORK, "EQ", 11264, [P, SLOTS, E])
        gatew = carve(WORK, "gatew", 24576, [E, D])
        T1 = carve(WORK, "T1", 24576, [P, TT, E])
        T2 = carve(WORK, "T2", 25088, [P, TT, E])
        slotmap = carve(WORK, "slotmap", 25600, [SLOTS, P])
        OFF = carve(WORK, "OFF", 26112, [P, E + 1])
        CNT = carve(WORK, "CNT", 26148, [P, E])
        CW = carve(WORK, "CW", 26180, [P, TT, 2])
        POSF = carve(WORK, "POSF", 26308, [P, E2, TT])
        POS = carve(WORK, "POS", 26436, [P, E2, TT], U32)
        EIDF = carve(WORK, "EIDF", 26564, [P, SLOTS])
        EID = carve(WORK, "EID", 26724, [P, SLOTS], I32)
        IDX = carve(WORK, "IDX", 26884, [P, SLOTS], U32)
        idx1 = carve(WORK, "idx1", 27044, [P, 2], U32)
        gwT = carve(WORK, "gwT", 27052, [P, 2, KD * E], F16)
        SEL = carve(WORK, "SEL", 27180, [P, TT, E], F16)
        mgath = carve(WORK, "mgath", 28928, [P, 2, 2, D])
        LT = sb("LT", [P, P], F16)
        ONES = sb("ONES", [P, P], F16)
        IOTA = sb("IOTA", [P, SLOTS])
        TOK = sb("TOK", [P, TT])
        IOTAI = carve(WORK, "IOTAI", 37376, [P, SLOTS], I32)
        TOKI = carve(WORK, "TOKI", 37536, [P, TT], I32)
        bnst_b = carve(WORK, "bnst_b", 37600, [P, 6])
        xn_dram = nc.dram_tensor("xn_scratch", [T, D], F32, kind="Internal").ap()
        map_dram = nc.dram_tensor("map_scratch", [SLOTS * P, 1], F32, kind="Internal").ap()
        y_dram = nc.dram_tensor("y_scratch", [SLOTS * P, D], F32, kind="Internal").ap()

        const_ok = sem("const_ok")
        gatew_in = sem("gatew_in")
        gw_mm = sem("gw_mm")
        gw_hi = sem("gw_hi")
        gw_ok = sem("gw_ok")
        xn_st = [sem("xn_st0"), sem("xn_st1")]
        lg_mm = sem("lg_mm")
        lg_sb = sem("lg_sb")
        d12_ok = sem("d12_ok")
        e12_ok = sem("e12_ok")
        sel_ok = sem("sel_ok")
        rank_mm = sem("rank_mm")
        pos_ok = sem("pos_ok")
        eid_ok = sem("eid_ok")
        map_zero = sem("map_zero")
        map_init = sem("map_init")
        map_done = sem("map_done")
        map_in = sem("map_in")
        map_mm = sem("map_mm")
        idx_ok = sem("idx_ok")
        idx1_ok = sem("idx1_ok")
        gath = [sem("gath0"), sem("gath1")]
        yst = [sem("yst0"), sem("yst1")]
        mg_in = [[sem(f"mg_in{p}{k}") for k in range(2)] for p in range(2)]
        mg_used = sem("mg_used")
        x2_ok = sem("x2_ok")

        class Unit:

            def __init__(self, name):
                self.x_ok = sem(f"{name}_x_ok")
                self.tx_mm = sem(f"{name}_tx_mm")
                self.tx_hi = sem(f"{name}_tx_hi")
                self.tx_lo = sem(f"{name}_tx_lo")
                self.hg_mm = sem(f"{name}_hg_mm")
                self.sil_ok = sem(f"{name}_sil_ok")
                self.hid_ok = sem(f"{name}_hid_ok")
                self.th_mm = sem(f"{name}_th_mm")
                self.th_hi = sem(f"{name}_th_hi")
                self.th_lo = sem(f"{name}_th_lo")
                self.y_mm = sem(f"{name}_y_mm")
                self.y_out = sem(f"{name}_y_out")

        SH, MO = Unit("sh"), Unit("mo")

        def pe_tx(q, p, t):
            for k in range(KD):
                ins = nc.tensor.transpose(bank[0][:, k * P:(k + 1) * P], xn[:, p, k * P:(k + 1) * P], ident[:, :])
            ins.then_inc(q.tx_mm, 1)

        def pe_hg(pe, q, p, up, slot):
            half = W13N // 2
            for m in range(2):
                n = 0
                for k in range(KD):
                    for a, w in ((0, 0), (0, 1), (1, 0)):
                        ins = nc.tensor.matmul(bank[1 + 2 * m + up][:, 0:I], xT[:, p, a, k * P:(k + 1) * P],
                                               W13[:, bass.ds(slot * W13N + (w * half + k * 2 * I + m * I), I)],
                                               start=(n == 0), stop=(n == 3 * KD - 1))
                        n += 1
            ins.then_inc(q.hg_mm, 1)

        def pe_th(q, up):
            for k in range(KI):
                ins = nc.tensor.transpose(bank[5][:, k * P:(k + 1) * P], hid[:, up, k * P:(k + 1) * P], ident[:, :])
            ins.then_inc(q.th_mm, 1)

        def pe_y(q, up, slot, dst, first, last):
            n = 0
            for k in range(KI):
                for a, w in ((0, 0), (0, 1), (1, 0)):
                    ins = nc.tensor.matmul(dst[:, :], hT[:, up, a, k * P:(k + 1) * P],
                                           W2[:, bass.ds(slot * W2N + (w * (W2N // 2) + k * D), D)],
                                           start=(first and n == 0), stop=(last and n == 3 * KI - 1))
                    n += 1
            return ins

        def act_hi(act, q, p, t):
            act.wait_ge(q.tx_mm, t + 1)
            nc.scalar.activation(xT[:, p, 0, :], bank[0][:, :], ACT.Copy).then_inc(q.tx_hi, 1)

        def act_sil(act, q, up, u):
            act.wait_ge(q.hg_mm, u + 1)
            nc.scalar.activation(sil[:, up, :], bank[1 + up][:, 0:I], ACT.Silu, scale=1.0 / W_SCALE).then_inc(q.sil_ok, 1)

        def act_thi(act, q, up, u):
            act.wait_ge(q.th_mm, u + 1)
            nc.scalar.activation(hT[:, up, 0, :], bank[5][:, 0:KI * P], ACT.Copy).then_inc(q.th_hi, 1)

        def dve_lo(dve, q, p, t):
            dve.wait_ge(q.tx_hi, t + 1)
            nc.vector.tensor_tensor(xT[:, p, 1, :], bank[0][:, :], xT[:, p, 0, :], ALU.subtract).then_inc(q.tx_lo, 1)

        def dve_hid(dve, q, up, u):
            dve.wait_ge(q.sil_ok, u + 1)
            nc.vector.scalar_tensor_tensor(hid[:, up, 0:I], bank[3 + up][:, 0:I], A_SCALE / W_SCALE, sil[:, up, :],
                                           ALU.mult, ALU.mult).then_inc(q.hid_ok, 1)

        def dve_thl(dve, q, up, u):
            dve.wait_ge(q.th_hi, u + 1)
            nc.vector.tensor_tensor(hT[:, up, 1, :], bank[5][:, 0:KI * P], hT[:, up, 0, :], ALU.subtract).then_inc(q.th_lo, 1)

        def b_constants(pool, link):
            g = nc.gpsimd
            link(g.memset(LT[:, :], 1.0))
            link(g.affine_select(out=LT[:, :], in_=LT[:, :], compare_op=ALU.is_gt, fill=0.0, base=0,
                                 pattern=[[1, P]], channel_multiplier=-1))
            link(g.memset(ONES[:, :], 1.0))
            link(g.iota(IOTAI, pattern=[[1, SLOTS]], base=0, channel_multiplier=0))
            link(g.iota(TOKI, pattern=[[P, TT]], base=0, channel_multiplier=1))
            link(g.tensor_copy(IOTA[:, :], IOTAI))
            link(g.tensor_copy(TOK[:, :], TOKI))
            pads(link, range(5))
            g.nop().then_inc(const_ok, 1)

        def pads(link, slots):
            for s in slots:
                for lo in range(2):
                    at = s * W2N + lo * (W2N // 2) + (KI - 1) * D
                    link(nc.gpsimd.memset(W2[I_LAST:P, at:at + D], 0.0))

        def b_sync(sp):
            sp.wait_ge(x1_ok, TT)
            sp.dma_start(gatew, gate_w).then_inc(gatew_in, 16)
            with sp.Fori(0, TT // 2) as j:
                for p in range(2):
                    sp.wait_ge(SH.x_ok, j * 2 + (p + 1))
                    sp.dma_start(xn_dram[bass.ds(j * (2 * P) + p * P, P), :], xn[:, p, :]).then_inc(xn_st[p], 16)
            for i in range(3):
                if i == 1:
                    sp.wait_ge(SH.y_mm, TT)
                load_slot(sp, 7 + i, expert_src(5 + i))
            sp.wait_ge(map_zero, 1)
            sp.dma_start(map_dram.rearrange("(s p) o -> s (p o)", p=P), slotmap).then_inc(map_init, 16)
            sp.wait_ge(map_done, 16 * 2 * TT)
            sp.dma_start(slotmap, map_dram.rearrange("(s p) o -> s (p o)", p=P)).then_inc(map_in, 16)
            for p in range(2):
                sp.nop().then_inc(yst[p], 16)
            with sp.Fori(0, SLOTS // 2) as j:
                for p in range(2):
                    sp.wait_ge(MO.y_out, j * 2 + (p + 2))
                    sp.dma_start(y_dram[bass.ds(j * (2 * P) + p * P, P), :], yo[:, p, :]).then_inc(yst[p], 16)

        def b_gpsimd(pool):
            for i in range(3):
                split_lo(pool, 7 + i, 5 + i)
            pool.wait_ge(map_init, 16)
            pool.wait_ge(pos_ok, 1)
            for t in range(TT):
                for k in range(2):
                    nc.gpsimd.indirect_dma_start(map_dram, bass.IndirectOffsetOnAxis(ap=POS[:, k, t:t + 1], axis=0),
                                                 TOK[:, t:t + 1], None).then_inc(map_done, 16)
            pool.wait_ge(idx_ok, 1)

            def fetch(j, p, first):
                if not first:
                    pool.wait_ge(MO.tx_mm, j * 2 + (p - 1))
                    pool.wait_ge(gath[p], j * 16)
                nc.gpsimd.tensor_copy(idx1[:, p:p + 1], IDX[:, bass.ds(j * 2 + p, 1)]).then_inc(idx1_ok, 1)
                pool.wait_ge(idx1_ok, j * 2 + (p + 1))
                nc.gpsimd.nop(nofuse=True)
                nc.gpsimd.indirect_dma_start(xn[:, p, :], None, xn_dram,
                                             bass.IndirectOffsetOnAxis(ap=idx1[:, p:p + 1], axis=0)).then_inc(gath[p], 16)

            for p in range(2):
                pool.wait_ge(xn_st[p], 16 * (TT // 2))
            for p in range(2):
                fetch(0, p, True)
            with pool.Fori(1, SLOTS // 2) as j:
                for p in range(2):
                    fetch(j, p, False)
            for p in range(2):
                pool.wait_ge(yst[p], 16 * (SLOTS // 2) + 16)
            for t in range(TT):
                if t >= 2:
                    pool.wait_ge(mg_used, t - 1)
                for k in range(2):
                    nc.gpsimd.indirect_dma_start(mgath[:, t % 2, k, :], None, y_dram,
                                                 bass.IndirectOffsetOnAxis(ap=POS[:, k, t:t + 1], axis=0)
                                                 ).then_inc(mg_in[t % 2][k], 16)

        def b_scalar(act):
            act.wait_ge(gw_mm, 1)
            nc.scalar.activation(gwT[:, 0, :], bank[7][:, 0:KD * E], ACT.Copy, scale=W_SCALE).then_inc(gw_hi, 1)
            act_hi(act, SH, 0, 0)

            def tile(j, p, first):
                for h in range(2):
                    u = j * 4 + (2 * p + h)
                    if not (first and p == 0 and h == 0):
                        act_thi(act, SH, 1 - h, u - 1)
                    act_sil(act, SH, h, u)
                    if h == 0:
                        act_hi(act, SH, 1 - p, j * 2 + (p + 1))

            for p in range(2):
                tile(0, p, True)
            with act.Fori(1, TT // 2 - 1) as j:
                for p in range(2):
                    tile(j, p, False)
            j = TT // 2 - 1
            tile(j, 0, False)
            act_thi(act, SH, 1, 2 * TT - 3)
            act_sil(act, SH, 0, 2 * TT - 2)
            act_thi(act, SH, 0, 2 * TT - 2)
            act_sil(act, SH, 1, 2 * TT - 1)
            act_thi(act, SH, 1, 2 * TT - 1)
            for i in range(3):
                split_hi(act, 7 + i, 5 + i)
            nc.scalar.nop().then_inc(MO.y_out, 1)
            act.wait_ge(d12_ok, 1)
            nc.scalar.activation(CW[:, :, 1], CW[:, :, 0], ACT.Exp).then_inc(e12_ok, 1)
            act_hi(act, MO, 0, 0)

            def slot(j, p, first, last):
                i = j * 2 + p
                if not (first and p == 0):
                    act_thi(act, MO, 1 - p, i - 1)
                act_sil(act, MO, p, i)
                if not (last and p == 1):
                    act_hi(act, MO, 1 - p, i + 1)
                if not (first and p == 0):
                    y_out(i - 1, 1 - p, first)

            def y_out(i, p, first):
                act.wait_ge(MO.y_mm, i + 1)
                if not first:
                    act.wait_ge(yst[p], (i - p) * 8 + 16)
                nc.scalar.activation(yo[:, p, :], bank[6 + p][:, :], ACT.Copy).then_inc(MO.y_out, 1)

            for p in range(2):
                slot(0, p, True, False)
            with act.Fori(1, SLOTS // 2 - 1) as j:
                for p in range(2):
                    slot(j, p, False, False)
            for p in range(2):
                slot(SLOTS // 2 - 1, p, False, True)
            act_thi(act, MO, 1, SLOTS - 1)
            y_out(SLOTS - 1, 1, False)

        def b_tensor(pe):
            pe.wait_ge(x1_ok, TT)
            pe.wait_ge(gatew_in, 16)
            for k in range(KD):
                ins = nc.tensor.transpose(bank[7][:, k * E:(k + 1) * E], gatew[:, k * P:(k + 1) * P], ident[0:E, 0:E])
            ins.then_inc(gw_mm, 1)
            pe.wait_ge(gw_ok, 1)
            pe.wait_ge(const_ok, 1)
            pe.wait_ge(split_l, 7 * NCH + 1)
            pe.wait_ge(pad_ok, 1)
            pe.wait_ge(SH.x_ok, 1)
            pe_tx(SH, 0, 0)

            def finish(j, u, h, t):
                pe.wait_ge(SH.th_lo, u + 1)
                if h == 0:
                    pe.wait_ge(SH.y_out, t)
                ins = pe_y(SH, h, E - 2 + h, bank[6], h == 0, h == 1)
                if h == 1:
                    ins.then_inc(SH.y_mm, 1)

            def tile(j, p, first, last):
                for h in range(2):
                    u = j * 4 + (2 * p + h)
                    t = j * 2 + p
                    before = not (first and p == 0 and h == 0)
                    if before:
                        pe.wait_ge(SH.hid_ok, u)
                        pe_th(SH, 1 - h)
                    pe.wait_ge(SH.tx_lo, t + 1)
                    pe_hg(pe, SH, p, h, E - 2 + h)
                    if h == 0:
                        pe.wait_ge(lg_sb, t)
                        n = 0
                        for k in range(KD):
                            for a in range(2):
                                for w in range(2):
                                    ins = nc.tensor.matmul(bank[7][:, 0:E], xT[:, p, a, k * P:(k + 1) * P],
                                                           gwT[:, w, k * E:(k + 1) * E], start=(n == 0), stop=(n == 4 * KD - 1))
                                    n += 1
                        ins.then_inc(lg_mm, 1)
                        if not (last and p == 1):
                            pe.wait_ge(SH.x_ok, t + 2)
                            pe_tx(SH, 1 - p, t + 1)
                    if before:
                        finish(j, u - 1, 1 - h, t - 1 if h == 0 else t)

            for p in range(2):
                tile(0, p, True, False)
            with pe.Fori(1, TT // 2 - 1) as j:
                for p in range(2):
                    tile(j, p, False, False)
            for p in range(2):
                tile(TT // 2 - 1, p, False, True)
            pe.wait_ge(SH.hid_ok, 2 * TT)
            pe_th(SH, 1)
            finish(0, 2 * TT - 1, 1, TT - 1)

            pe.wait_ge(sel_ok, 1)
            nc.tensor.matmul(bank[0][:, 0:TT * E], LT[:, :], SEL.rearrange("p a b -> p (a b)"), start=True, stop=True)
            for d in range(1, TT):
                nc.tensor.matmul(bank[0][:, d * E:TT * E], ONES[:, :],
                                 SEL[:, 0:TT - d, :].rearrange("p a b -> p (a b)"), start=False, stop=True,
                                 skip_group_check=True)
            for t in range(TT):
                ins = nc.tensor.matmul(bank[1][:, 0:E], ONES[:, :], SEL[:, t, :], start=(t == 0), stop=(t == TT - 1))
            ins.then_inc(rank_mm, 1)
            pe.wait_ge(map_in, 16)
            nc.tensor.transpose(bank[2][:, 0:SLOTS], slotmap, ident[0:SLOTS, 0:SLOTS]).then_inc(map_mm, 1)
            pe.wait_ge(idx_ok, 1)
            pe.wait_ge(eid_ok, 1)
            pe.wait_ge(split_l, (E + 2) * NCH + 1)
            pe.wait_ge(gath[0], 16)
            pe_tx(MO, 0, 0)

            def mfinish(i, p, slot, first):
                pe.wait_ge(MO.th_lo, i + 1)
                if not first:
                    pe.wait_ge(MO.y_out, i)
                pe_y(MO, p, slot, bank[6 + p], True, True).then_inc(MO.y_mm, 1)

            def eid(i):
                return pe.value_load(EID[0:1, bass.ds(i, 1)], min_val=0, max_val=E - 1)

            def slot(j, p, first, last):
                i = j * 2 + p
                if not (first and p == 0):
                    pe.wait_ge(MO.hid_ok, i)
                    pe_th(MO, 1 - p)
                pe.wait_ge(MO.tx_lo, i + 1)
                pe_hg(pe, MO, p, p, eid(i))
                if not (last and p == 1):
                    pe.wait_ge(gath[1 - p], j * 16 + 16 * (1 + p))
                    pe_tx(MO, 1 - p, i + 1)
                if not (first and p == 0):
                    mfinish(i - 1, 1 - p, eid(i - 1), first)

            for p in range(2):
                slot(0, p, True, False)
            with pe.Fori(1, SLOTS // 2 - 1) as j:
                for p in range(2):
                    slot(j, p, False, False)
            for p in range(2):
                slot(SLOTS // 2 - 1, p, False, True)
            pe.wait_ge(MO.hid_ok, SLOTS)
            pe_th(MO, 1)
            mfinish(SLOTS - 1, 1, eid(SLOTS - 1), False)

        def b_vector(dve):
            link = Chain(dve, dve_chain)
            link.restart()
            v = nc.vector
            dve.wait_ge(x1_ok, TT)
            dve.wait_ge(const_ok, 1)
            for p in range(2):
                link(v.memset(hid[:, p, I:KI * P], 0.0))
            link(v.tensor_scalar(GATES[:, 7:8], GATES[:, 2:3], 1.0 / (W_SCALE * A_SCALE), None, ALU.mult))
            stats(link, range(TT), bnst_b)
            dve.wait_ge(gw_hi, 1)
            v.scalar_tensor_tensor(gwT[:, 1, :], bank[7][:, 0:KD * E], W_SCALE, gwT[:, 0, :], ALU.mult,
                                   ALU.subtract).then_inc(gw_ok, 1)

            def norm(t, p, first):
                if not first:
                    dve.wait_ge(xn_st[p], (t - p) * 8)
                v.tensor_scalar(xn[:, p, :], X[:, t, :], MV[:, bass.ds(t, 1), 0], RSTD[:, bass.ds(t, 1)],
                                ALU.subtract, ALU.mult).then_inc(SH.x_ok, 1)

            norm(0, 0, True)
            norm(1, 1, True)
            dve_lo(dve, SH, 0, 0)

            def y_in(t):
                dve.wait_ge(SH.y_mm, t + 1)
                v.scalar_tensor_tensor(X[:, t, :], bank[6][:, :], GATES[:, 7:8], X[:, t, :], ALU.mult,
                                       ALU.add).then_inc(SH.y_out, 1)

            def tile(j, p, first, last):
                t = j * 2 + p
                for h in range(2):
                    u = j * 4 + (2 * p + h)
                    before = not (first and p == 0 and h == 0)
                    if before:
                        dve_thl(dve, SH, 1 - h, u - 1)
                    dve_hid(dve, SH, h, u)
                    if h == 0:
                        dve.wait_ge(lg_mm, t + 1)
                        v.tensor_scalar(LG[:, t, :], bank[7][:, 0:E], 1.0 / W_SCALE, None, ALU.mult).then_inc(lg_sb, 1)
                        if not (last and p == 1):
                            dve_lo(dve, SH, 1 - p, t + 1)
                        if not last:
                            norm(t + 2, p, False)
                        if before:
                            y_in(t - 1)

            for p in range(2):
                tile(0, p, True, False)
            with dve.Fori(1, TT // 2 - 1) as j:
                for p in range(2):
                    tile(j, p, False, False)
            for p in range(2):
                tile(TT // 2 - 1, p, False, True)
            dve_thl(dve, SH, 1, 2 * TT - 1)
            y_in(TT - 1)

            link.restart()
            dve.wait_ge(lg_sb, TT)
            for t in range(TT):
                link(v.max(MX[:, t, :], LG[:, t, :]))
                link(v.max_index(MI[:, t, :], MX[:, t, :], LG[:, t, :]))
            link(v.tensor_copy(MIF, MI))
            for k in range(2):
                link(v.tensor_tensor(OH[:, k, :, :], MIF[:, :, k:k + 1].to_broadcast([P, TT, E]),
                                     IOTA[:, 0:E].unsqueeze(1).to_broadcast([P, TT, E]), ALU.is_equal))
            v.tensor_tensor(SEL, OH[:, 0, :, :], OH[:, 1, :, :], ALU.add).then_inc(sel_ok, 1)
            v.tensor_tensor(CW[:, :, 0], MX[:, :, 1], MX[:, :, 0], ALU.subtract).then_inc(d12_ok, 1)
            dve.wait_ge(e12_ok, 1)
            link(v.tensor_scalar(CW[:, :, 0], CW[:, :, 1], 1.0, None, ALU.add))
            link(v.reciprocal(CW[:, :, 0], CW[:, :, 0]))
            link(v.tensor_tensor(CW[:, :, 1], CW[:, :, 1], CW[:, :, 0], ALU.mult))
            link(v.tensor_scalar(CW, CW, GATES[:, 7:8], None, ALU.mult))
            dve.wait_ge(rank_mm, 1)
            link(v.tensor_scalar(CNT, bank[1][:, 0:E], 1.0 / P, (P - 1.0) / P - 0.5 + 0.5 / P, ALU.mult, ALU.add))
            link(v.tensor_scalar(CNT, CNT, ROUND, ROUND, ALU.add, ALU.subtract))
            link(v.memset(OFF, 0.0))
            for e in range(E):
                link(v.tensor_tensor(OFF[:, e + 1:e + 2], OFF[:, e:e + 1], CNT[:, e:e + 1], ALU.add))
            link(v.scalar_tensor_tensor(T1, OFF[:, 0:E].unsqueeze(1).to_broadcast([P, TT, E]), float(P),
                                        bank[0][:, 0:TT * E].rearrange("p (a b) -> p a b", b=E), ALU.mult, ALU.add))
            for k in range(2):
                link(v.tensor_tensor(T2, T1, OH[:, k, :, :], ALU.mult))
                link(v.tensor_reduce(POSF[:, k, :], T2, AX_X, ALU.add))
            v.tensor_copy(POS, POSF).then_inc(pos_ok, 1)
            link(v.tensor_tensor(EQ, OFF[:, 1:E + 1].unsqueeze(1).to_broadcast([P, SLOTS, E]),
                                 IOTA[:, :].unsqueeze(2).to_broadcast([P, SLOTS, E]), ALU.is_le))
            link(v.tensor_reduce(EIDF, EQ, AX_X, ALU.add))
            link(v.tensor_scalar(EIDF, EIDF, float(E - 1), None, ALU.min))
            v.tensor_copy(EID, EIDF).then_inc(eid_ok, 1)
            dve.wait_ge(eid_ok, 1)
            for p in range(2):
                link(v.memset(hid[:, p, I:KI * P], 0.0))
            dve.wait_ge(pos_ok, 1)
            v.memset(slotmap, 0.0).then_inc(map_zero, 1)
            dve.wait_ge(map_mm, 1)
            v.tensor_copy(IDX, bank[2][:, 0:SLOTS]).then_inc(idx_ok, 1)
            dve_lo(dve, MO, 0, 0)

            def slot(j, p, first, last):
                i = j * 2 + p
                if not (first and p == 0):
                    dve_thl(dve, MO, 1 - p, i - 1)
                dve_hid(dve, MO, p, i)
                if not (last and p == 1):
                    dve_lo(dve, MO, 1 - p, i + 1)

            for p in range(2):
                slot(0, p, True, False)
            with dve.Fori(1, SLOTS // 2 - 1) as j:
                for p in range(2):
                    slot(j, p, False, False)
            for p in range(2):
                slot(SLOTS // 2 - 1, p, False, True)
            dve_thl(dve, MO, 1, SLOTS - 1)
            link.restart()
            for t in range(TT):
                for k in range(2):
                    dve.wait_ge(mg_in[t % 2][k], 16 * (t // 2 + 1))
                    ins = v.scalar_tensor_tensor(X[:, t, :], mgath[:, t % 2, k, :], CW[:, t, k:k + 1], X[:, t, :],
                                                 ALU.mult, ALU.add)
                    if k == 0:
                        link(ins)
                    else:
                        ins.then_inc(mg_used, 1)
            dve.wait_ge(mg_used, TT)
            v.nop().then_inc(x2_ok, 1)


        HD = 16
        H = D // HD
        G = C // HD
        HG = H // G
        NQ = H * S
        QS = BIG[:, 0:NQ // 2].bitcast(F16).rearrange("p (h s) -> p h s", s=S)
        KK = carve(BIG, "KK", 32768, [P, G, 2, S], F16)
        KS, KA = KK[:, :, 0, :], KK[:, :, 1, :]
        PB = carve(BIG, "PB", 49152, [P, 2, 2 * HG, S])
        V = carve(BIG, "V", 81920, [P, R, G, 32])
        qhT = carve(BIG, "qhT", 86016, [P, 2, KD, S], F16)
        khT = carve(BIG, "khT", 94208, [P, 2, S], F16)
        OS = carve(BIG, "OS", 96256, [P, 2, S])
        CT = carve(WORK, "CT", 0, [P, R, C])
        QN = carve(WORK, "QN", 2048, [P, 2, D])
        MXU = carve(WORK, "MXU", 6144, [P, 2, HG * R])
        MT = carve(WORK, "MT", 6400, [HG * R, 2, P], F16)
        RDEN = carve(WORK, "RDEN", 7168, [P, 2, R * HG])
        OO = carve(WORK, "OO", 7424, [P, 2, R * HG, HD])
        bnst_c = carve(WORK, "bnst_c", 9472, [P, 6])
        SOFT_SCALE = 1.0 / float(HD) ** 0.5
        ABANK, TBANK, OBANK = [bank[0], bank[1]], bank[2], bank[3]
        BPAIR = [PS[:, 4:6, :], PS[:, 6:8, :]]
        NPREP = G + R + 1 + G

        ct_in = sem("ct_in")
        cpad_ok = sem("cpad_ok")
        v_ok = sem("v_ok")
        qn_ok = sem("qn_ok")
        t_mm = sem("t_mm")
        t_hi = sem("t_hi")
        t_free = sem("t_free")
        qk_in = [sem(f"qk_in{g}") for g in range(G)]
        a_mm = sem("a_mm")
        max_ok = sem("max_ok")
        mt_ok = sem("mt_ok")
        m_in = [sem(f"m_in{i}") for i in range(2)]
        b_mm = sem("b_mm")
        exp_ok = sem("exp_ok")
        pv_mm = sem("pv_mm")
        o_sb = sem("o_sb")
        o_ok = sem("o_ok")
        x3_ok = sem("x3_ok")
        HALF = 2

        TUSES = []
        for g_ in range(G):
            TUSES.append(("m", g_))
            if g_ > 0:
                TUSES.append(("o", g_ - 1))
            if g_ == 1:
                TUSES.append(("ctx", 0))
            if 1 <= g_ <= R:
                TUSES.append(("q", g_ - 1))
        TUSES.append(("o", G - 1))
        assert len(TUSES) == NPREP
        TLAST = [k for k in TUSES if k[0] == "o" or (k[0] == "m" and k[1] < G - 1)]
        TFIRST = [("ctx", 0)] + [("q", r_) for r_ in range(R)] + [("m", -1)]

        def tuse(b, kind, i):
            if b is None:
                return TFIRST.index((kind, i))
            if isinstance(b, int) and b == B - 1:
                return len(TFIRST) + b * NPREP + TLAST.index((kind, i))
            return len(TFIRST) + b * NPREP + TUSES.index((kind, i))

        def c_sync(sp):
            sp.wait_ge(x2_ok, 1)

            def load_ctx(b):
                sp.dma_start(CT, ctx_rows[:, bass.ds(b * R, R), :]).then_inc(ct_in, 16)

            def stack_group(b, g):
                for n, (a, w) in enumerate(((0, 0), (0, 1), (1, 0))):
                    rows = slice(n * HD, (n + 1) * HD)
                    sp.dma_start(QS[rows, g * HG:(g + 1) * HG, :], qhT[g * HD:(g + 1) * HD, a, :, :]).then_inc(qk_in[g], 16)
                    sp.dma_start(KK[rows, g, :, :], khT[g * HD:(g + 1) * HD, w, :].unsqueeze(1).to_broadcast([HD, 2, S])
                                 ).then_inc(qk_in[g], 16)

            def maxima(u, g, i):
                sp.wait_ge(mt_ok, u + 1)
                sp.dma_start(QS[64:65, g * HG:(g + 1) * HG, :].rearrange("o h (r s) -> o (h r) s", r=R),
                             MT[:, i, :]).then_inc(m_in[i], 16)

            def batch(b, last):
                if not last:
                    sp.wait_ge(v_ok, b * G + G)
                    load_ctx(b + 1)
                for g in range(G):
                    u = b * G + g
                    if not (last and g == G - 1):
                        maxima(u + 1, (g + 1) % G, (g + 1) % 2)
                    if last and g in (2, 4, 6):
                        sp.wait_ge(b_mm, u * 2 * HG)
                    if last and g in (2, 4, 6):
                        load_weights(UW, 1, g // 2 - 1, uw_in)
                    if last or g < 5:
                        continue
                    if g == 5:
                        sp.wait_ge(t_free, tuse(b, "q", R - 1) + 1)
                    for gg in {5: (0, 1, 2, 3), 6: (4, 5), 7: (6,)}[g]:
                        sp.wait_ge(b_mm, (b * G + gg + 1) * 2 * HG)
                        stack_group(b + 1, gg)
                if not last:
                    sp.wait_ge(b_mm, (b * G + G) * 2 * HG)
                    stack_group(b + 1, G - 1)

            def load_weights(dst, m, j, loaded):
                sp.dma_start(dst[:, j, :, :, :], wdq_dram[m * FCH + j, :, :].rearrange(
                    "p (l k f) -> p l k f", l=2, k=KD)).then_inc(loaded, 16)

            load_ctx(0)
            sp.wait_ge(cpad_ok, 1)
            sp.wait_ge(t_free, tuse(None, "q", R - 1) + 1)
            for g in range(G):
                stack_group(0, g)
            maxima(0, 0, 0)
            for j in range(FCH):
                load_weights(GW, 0, j, gw_in)
            with sp.Fori(0, B - 1) as b:
                batch(b, False)
            batch(B - 1, True)
            sp.wait_ge(b_mm, B * G * 2 * HG)
            load_weights(UW, 1, FCH - 1, uw_in)
            sp.wait_ge(pv_mm, B * G * 2)
            for j in range(FCH):
                load_weights(DW, 2, j, dw_in)

        def c_gpsimd(pool):
            pool.wait_ge(x2_ok, 1)
            nc.gpsimd.memset(V.rearrange("p a b c -> p (a b c)"), 1.0).then_inc(v_ones, 1)
            pool.wait_ge(v_ones, 1)

            def values(b, g):
                nc.gpsimd.nop(nofuse=True)
                nc.gpsimd.tensor_copy(V[:, :, g, 0:HD], CT[:, :, g * HD:(g + 1) * HD]).then_inc(v_ok, 1)

            pool.wait_ge(ct_in, 16)
            for g in range(G):
                values(0, g)
            with pool.Fori(0, B - 1) as b:
                pool.wait_ge(ct_in, b * 16 + 32)
                for g in range(G):
                    pool.wait_ge(pv_mm, (b * G + g + 1) * 2)
                    values(b + 1, g)

        def c_scalar(act):
            def hi(b, kind, i, dst, src):
                act.wait_ge(t_mm, tuse(b, kind, i) + 1)
                nc.scalar.activation(dst, src, ACT.Copy).then_inc(t_hi, 1)

            def hi_q(b, r):
                hi(b, "q", r, qhT[:, 0, :, r * P:(r + 1) * P], TBANK.rearrange("p (k s) -> p k s", k=KD))

            def hi_ctx(b):
                hi(b, "ctx", 0, khT[:, 0, :], TBANK)

            def maxima(b, g, i):
                act.wait_ge(t_mm, tuse(b, "m", g) + 1)
                nc.scalar.activation(MT[:, i, :], TBANK[0:HG * R, 0:P], ACT.Copy).then_inc(t_free, 1)
                act.wait_ge(t_free, tuse(b, "m", g) + 1)
                nc.scalar.nop().then_inc(mt_ok, 1)

            def out_copy(b, g):
                u = b * G + g
                act.wait_ge(pv_mm, u * 2 + 2)
                nc.scalar.activation(OS[:, g % 2, :], OBANK, ACT.Copy).then_inc(o_sb, 1)

            def batch(b, last):
                for g in range(G):
                    for tp in range(2):
                        n = (b * G + g) * 2 + tp
                        for h in range(HG):
                            act.wait_ge(b_mm, n * HG + (h + 1))
                            nc.scalar.activation(PB[:, tp, 2 * h:2 * h + 2, :], BPAIR[h % 2], ACT.Exp,
                                                 scale=SOFT_SCALE).then_inc(exp_ok, 1)
                            if tp == 0 and h == 3 and not (last and g == G - 1):
                                maxima(b, g, (g + 1) % 2)
                            if tp == 1 and h == 0 and g > 0:
                                out_copy(b, g - 1)
                            if tp == 1 and h == 3 and not last:
                                if g == 1:
                                    hi_ctx(b)
                                if 1 <= g <= R:
                                    hi_q(b, g - 1)
                out_copy(b, G - 1)

            nc.scalar.nop().then_inc(exp_ok, 2)
            nc.scalar.nop().then_inc(o_sb, 1)
            hi_ctx(None)
            for r in range(R):
                hi_q(None, r)
            maxima(None, -1, 0)
            with act.Fori(0, B - 1) as b:
                batch(b, False)
            batch(B - 1, True)

        def c_tensor(pe):
            def t_wait(b, kind, i):
                pe.wait_ge(t_free, tuse(b, kind, i))

            def t_ctx(b, nb):
                pe.wait_ge(ct_in, nb * 16 + 16)
                t_wait(b, "ctx", 0)
                for r in range(R):
                    ins = nc.tensor.transpose(TBANK[:, r * P:(r + 1) * P], CT[:, r, :], ident[:, :])
                ins.then_inc(t_mm, 1)

            def t_q(b, nb, r):
                pe.wait_ge(qn_ok, nb * R + (r + 1))
                t_wait(b, "q", r)
                for k in range(HG):
                    ins = nc.tensor.transpose(TBANK[:, k * P:(k + 1) * P], QN[:, r % 2, k * P:(k + 1) * P], ident[:, :])
                ins.then_inc(t_mm, 1)

            def t_max(b, g, u, i):
                pe.wait_ge(max_ok, (u + 1) * HG * R)
                t_wait(b, "m", g)
                nc.tensor.transpose(TBANK[0:HG * R, 0:P], MXU[:, i, :], ident[:, :]).then_inc(t_mm, 1)

            def t_out(b, g):
                u = b * G + g
                pe.wait_ge(o_sb, u + 2)
                t_wait(b, "o", g)
                for r in range(R):
                    ins = nc.tensor.transpose(TBANK[:, r * P:(r + 1) * P], OS[:, g % 2, r * P:(r + 1) * P], ident[:, :])
                ins.then_inc(t_mm, 1)

            def a_slot(u, g, tp, h, first, reuse):
                if tp == 0 and h == 0:
                    first()
                for i in range(2):
                    n = u * HG * R + (tp * 2 * HG + 2 * h + i)
                    if reuse or tp or h:
                        pe.wait_ge(max_ok, n - 1)
                    r = 2 * tp + i
                    nc.tensor.matmul(ABANK[i], QS[:, g * HG + h, r * P:(r + 1) * P], KA[:, g, :],
                                     start=True, stop=True).then_inc(a_mm, 1)

            def b_slot(n, g, tp, h, first):
                if not first:
                    pe.wait_ge(exp_ok, n * HG + (h + 1))
                for j in range(HALF):
                    t = HALF * tp + j
                    ins = nc.tensor.matmul(BPAIR[h % 2][:, j, :], KS[:, g, t * P:(t + 1) * P],
                                           QS[:, g * HG + h, :], start=True, stop=True)
                ins.then_inc(b_mm, 1)

            def pv(n, u, g, tp, j):
                pe.wait_ge(exp_ok, (n + 1) * HG + 2)
                t = HALF * tp + j
                if t == 0:
                    pe.wait_ge(o_sb, u + 1)
                    pe.wait_ge(v_ok, u + 1)
                for h in range(HG):
                    ins = nc.tensor.matmul(OBANK[32 * h:32 * h + 32, :], V[:, t, g, :], PB[:, tp, 2 * h + j, :],
                                           start=(t == 0), stop=(t == R - 1))
                if j == HALF - 1:
                    ins.then_inc(pv_mm, 1)

            def batch(b, last, first=False):
                for g in range(G):
                    u = b * G + g
                    for tp in range(2):
                        n = u * 2 + tp
                        if tp == 0:
                            pe.wait_ge(m_in[g % 2], (u - g % 2) * 8 + 16)
                        ahead = not (last and g >= G - 2)
                        for h in range(HG):
                            if ahead:
                                a_slot(u + 2, (g + 2) % G, tp, h,
                                       lambda: pe.wait_ge(qk_in[(g + 2) % G], (b if g < G - 2 else b + 1) * (16 * 6) + 16 * 6), True)
                            b_slot(n, g, tp, h, False)
                            if h % 2:
                                j = h // 2
                                if tp == 1:
                                    pv(n - 1, u, g, 0, j)
                                elif g > 0:
                                    pv(n - 1, u - 1, g - 1, 1, j)
                            if tp == 0 and h == 3 and not (last and g == G - 1):
                                t_max(b, g, u + 1, (g + 1) % 2)
                            if tp == 1 and h == 2 and g > 0:
                                t_out(b, g - 1)
                            if tp == 1 and h == 3 and not last:
                                if g == 1:
                                    t_ctx(b, b + 1)
                                if 1 <= g <= R:
                                    t_q(b, b + 1, g - 1)
                for j in range(HALF):
                    pv(b * (G * 2) + (2 * G - 1), b * G + (G - 1), G - 1, 1, j)
                t_out(b, G - 1)

            pe.wait_ge(x2_ok, 1)
            t_ctx(None, 0)
            for r in range(R):
                t_q(None, 0, r)
            for u in range(2):
                for tp in range(2):
                    for h in range(HG):
                        a_slot(u, u, tp, h, lambda: pe.wait_ge(qk_in[u], 16 * 6), u > 0)
                if u == 0:
                    t_max(None, -1, 0, 0)
            with pe.Fori(0, B - 1) as b:
                batch(b, False)
            batch(B - 1, True)

        def c_vector(dve):
            link = Chain(dve, dve_chain)
            link.restart()
            v = nc.vector
            for a in (QS.rearrange("p a b -> p (a b)"), KK.rearrange("p a b c -> p (a b c)")):
                link(v.memset(a[32:64, :].bitcast(F32), 0.0))
                link(v.memset(a[64:128, :].bitcast(F32), 0.0))
            link(v.memset(KS[64:65, :, :], 1.0))
            v.nop().then_inc(cpad_ok, 1)
            stats(link, range(TT), bnst_c)

            def norm(b, r):
                t = b * R + r
                v.tensor_scalar(QN[:, r % 2, :].rearrange("p (k g d) -> p k g d", k=HG, d=HD),
                                X[:, t, :].rearrange("p (g k d) -> p k g d", k=HG, d=HD),
                                MV[:, bass.ds(t, 1), 0], RSTD[:, bass.ds(t, 1)],
                                ALU.subtract, ALU.mult).then_inc(qn_ok, 1)

            def lo(b, kind, i, dst, src, hi):
                dve.wait_ge(t_hi, lo_n(b, kind, i))
                v.tensor_tensor(dst, src, hi, ALU.subtract).then_inc(t_free, 1)

            def lo_n(b, kind, i):
                seq = [k for k in TUSES if k[0] in ("ctx", "q")]
                if b is None:
                    return [k for k in TFIRST if k[0] in ("ctx", "q")].index((kind, i)) + 1
                return b * len(seq) + (len(seq) + seq.index((kind, i)) + 1)

            def lo_q(b, r):
                lo(b, "q", r, qhT[:, 1, :, r * P:(r + 1) * P], TBANK.rearrange("p (k s) -> p k s", k=KD),
                   qhT[:, 0, :, r * P:(r + 1) * P])

            def lo_ctx(b):
                lo(b, "ctx", 0, khT[:, 1, :], TBANK, khT[:, 0, :])

            def max_slot(u, g, tp, h):
                for i in range(2):
                    n = u * HG * R + (tp * 2 * HG + 2 * h + i)
                    dve.wait_ge(a_mm, n + 1)
                    c = h * R + 2 * tp + i
                    v.tensor_reduce(MXU[:, g % 2, c:c + 1], ABANK[i], AX_X, ALU.max, negate=True).then_inc(max_ok, 1)

            def out_add(b, g):
                i = g % 2
                dve.wait_ge(t_mm, tuse(b, "o", g) + 1)
                o = TBANK.rearrange("p (n c) -> p n c", c=32)
                v.reciprocal(RDEN[:, i, :], o[:, :, HD]).then_inc(oo_ok, 1)
                dve.wait_ge(oo_ok, (b * G + g) * 2 + 1)
                v.tensor_tensor(OO[:, i, :, :], o[:, :, 0:HD], RDEN[:, i, :].unsqueeze(2).to_broadcast([P, R * HG, HD]),
                                ALU.mult).then_inc(oo_ok, 1)
                dve.wait_ge(oo_ok, (b * G + g) * 2 + 2)
                v.nop().then_inc(t_free, 1)
                xs = X[:, bass.ds(b * R, R), g * HG * HD:(g + 1) * HG * HD]
                v.scalar_tensor_tensor(xs, OO[:, i, :, :].rearrange("p (r h) d -> p r (h d)", r=R), GATES[:, 1:2], xs,
                                       ALU.mult, ALU.add).then_inc(o_ok, 1)

            def batch(b, last):
                for g in range(G):
                    u = b * G + g
                    for tp in range(2):
                        ahead = not (last and g >= G - 2)
                        for h in range(HG):
                            if ahead:
                                max_slot(u + 2, g, tp, h)
                            if tp == 0 and h == 1 and not last and 1 <= g <= R:
                                norm(b + 1, g - 1)
                            if tp == 1 and h == 2 and g > 0:
                                out_add(b, g - 1)
                            if tp == 1 and h == 3 and not last:
                                if g == 1:
                                    lo_ctx(b)
                                if 1 <= g <= R:
                                    lo_q(b, g - 1)
                out_add(b, G - 1)

            for r in range(2):
                norm(0, r)
            lo_ctx(None)
            for r in range(R):
                lo_q(None, r)
                if r < 2:
                    norm(0, r + 2)
            for u in range(2):
                for tp in range(2):
                    for h in range(HG):
                        max_slot(u, u, tp, h)
            with dve.Fori(0, B - 1) as b:
                batch(b, False)
            batch(B - 1, True)
            dve.wait_ge(o_ok, B * G)
            v.nop().then_inc(x3_ok, 1)

        v_ones = sem("v_ones")
        oo_ok = sem("oo_ok")

        F = fgate_w.shape[0]
        QB = 32
        NB = D // QB
        FT = F // P
        FCH = F // D
        TINY = 1e-30
        LEAST = 1.5 * 2.0 ** 14
        FSCALE = 1.0 / (W_SCALE * A_SCALE)
        NGRP = 4
        GW = carve(BIG, "GW", 106496, [P, FCH, 2, KD * D], F16)
        UW = carve(BIG, "UW", 0, [P, FCH, 2, KD * D], F16)
        DW = carve(BIG, "DW", 32768, [P, FCH, 2, KD * D], F16)
        GW, UW, DW = (a.rearrange("p c l (k f) -> p c l k f", k=KD) for a in (GW, UW, DW))
        hq = carve(BIG, "hq", 65536, [P, 2, F])
        he = carve(BIG, "he", 81920, [P, F])
        fhT = carve(BIG, "fhT", 90112, [P, 2, FT, P], F16)
        fxT = carve(BIG, "fxT", 98304, [P, 2, 2, D], F16)
        fx = carve(WORK, "fx", 0, [P, 2, D])
        fe = carve(WORK, "fe", 4096, [P, D])
        sg = carve(WORK, "sg", 6144, [P, 2, D])
        hsc = carve(WORK, "hsc", 10240, [P, 3, F // QB])
        xsc = carve(WORK, "xsc", 11008, [P, 3, NB])
        bnst_d = carve(WORK, "bnst_d", 11200, [P, 6])
        wst = carve(BIG, "wst", 56320, [P, 2, NGRP, D])
        we = carve(BIG, "we", 72704, [P, 2, NGRP * D])
        wo = carve(BIG, "wo", 120832, [P, 2, 2, NGRP * D], F16)
        wsc = carve(BIG, "wsc", 137216, [P, 2, 3, NGRP * NB])
        NW = 3 * FCH
        wdq_dram = nc.dram_tensor("wdq_scratch", [NW, P, 2 * NGRP * D], F16, kind="Internal").ap()

        fw_in = [sem("fw_in0"), sem("fw_in1")]
        fw_st = [sem("fw_st0"), sem("fw_st1")]
        gw_in = sem("gw_in")
        uw_in = sem("uw_in")
        dw_in = sem("dw_in")

        class Quant:

            def __init__(self, name):
                self.inv_ok = sem(f"{name}_inv_ok")
                self.q_ok = sem(f"{name}_q_ok")
                self.up_ok = sem(f"{name}_up_ok")
                self.n_ok = sem(f"{name}_n_ok")
                self.dq_ok = sem(f"{name}_dq_ok")
                self.t_mm = sem(f"{name}_t_mm")
                self.t_hi = sem(f"{name}_t_hi")
                self.t_lo = sem(f"{name}_t_lo")

        QW, QX, QH = Quant("qw"), Quant("qx"), Quant("qh")
        gu_mm = sem("gu_mm")
        sg_ok = sem("sg_ok")
        h_ok = sem("h_ok")
        d_mm = sem("d_mm")
        x4_ok = sem("x4_ok")
        fxn_ok = sem("fxn_ok")

        def blocks(a):
            return a.rearrange("p (n k) -> p n k", k=QB)

        def spread(a, n):
            return a.unsqueeze(2).to_broadcast([P, n, QB])

        def scales(link, src, sc, n, back):
            v = nc.vector
            link(v.tensor_reduce(sc[:, 0, :], blocks(src), AX_X, ALU.max, apply_absolute_value=True))
            link(v.tensor_scalar(sc[:, 0, :], sc[:, 0, :], 1.0 / 448.0, TINY, ALU.mult, ALU.max))
            link(v.tensor_scalar(sc[:, 2, :], sc[:, 0, :], -back, None, ALU.mult))
            return v.reciprocal(sc[:, 1, :], sc[:, 0, :])

        def round_e4m3(link, q, e):
            v = nc.vector
            link(v.tensor_scalar(e.bitcast(I32), e.bitcast(I32), 0x7F800000, 0x00400000, ALU.bitwise_and, ALU.bitwise_or))
            link(v.scalar_tensor_tensor(q, e, LEAST, q, ALU.max, ALU.add))
            return v.scalar_tensor_tensor(q, e, LEAST, q, ALU.max, ALU.subtract)

        def pool_q(pool, s, n, x, sc, nb):
            pool.wait_ge(s.inv_ok, n)
            nc.gpsimd.tensor_tensor(blocks(x), blocks(x), spread(sc[:, 1, :], nb), ALU.mult).then_inc(s.q_ok, 1)

        def pool_dq(pool, s, n, x, sc, nb):
            pool.wait_ge(s.n_ok, n)
            nc.gpsimd.tensor_tensor(blocks(x), blocks(x), spread(sc[:, 2, :], nb), ALU.mult).then_inc(s.dq_ok, 1)

        def act_up(act, s, n, x, e):
            act.wait_ge(s.q_ok, n)
            nc.scalar.activation(e, x, ACT.Copy, scale=2.0 ** 20).then_inc(s.up_ok, 1)

        def w_which(b, c):
            if c < 2:
                assert isinstance(b, int) and b == 0
                return c, 0
            return (c - 2, b + 1) if c < 4 else (2, b * 2 + (c - 4))

        def w_load(sp, b, c):
            m, j = w_which(b, c)
            if c >= 2:
                sp.wait_ge(QW.t_mm, b * 4 + (c - 1))
            if m < 2:
                src = (fgate_w, fup_w)[m].rearrange("(j i p) k -> p j i k", i=NGRP, p=P)
            else:
                src = fdown_w.rearrange("(i p) (j k) -> p j i k", p=P, k=D)
            sp.dma_start(wst[:, c % 2, :, :].unsqueeze(1), src[:, bass.ds(j, 1), :, :]).then_inc(fw_in[c % 2], 16)

        def w_store(sp, b, c):
            m, j = w_which(b, c)
            sp.wait_ge(QW.t_lo, b * 4 + (c + 1))
            sp.dma_start(wdq_dram[bass.ds(j + m * FCH, 1), :, :].rearrange("o p f -> (o p) f"),
                         wo[:, c % 2, :, :].rearrange("p l f -> p (l f)")).then_inc(fw_st[c % 2], 16)

        def w_flat(p):
            return wst[:, p, :, :].rearrange("p i k -> p (i k)")

        def w_pool(pool, b, c):
            for p in range(2):
                pool_q(pool, QW, b * 4 + (c + p + 1), w_flat(p), wsc[:, p], NGRP * NB)
            for p in range(2):
                pool_dq(pool, QW, b * 4 + (c + p + 1), w_flat(p), wsc[:, p], NGRP * NB)

        def w_act_up(act, b, c):
            for p in range(2):
                act_up(act, QW, b * 4 + (c + p + 1), w_flat(p), we[:, p, :])

        def w_banks(p):
            return PS[:, 4 * p:4 * p + 4, :].rearrange("p k f -> p (k f)")

        def w_act_hi(act, b, c, first):
            for p in range(2):
                act.wait_ge(QW.t_mm, b * 4 + (c + p + 1))
                if not first:
                    act.wait_ge(fw_st[p], b * 32 + c // 2 * 16)
                nc.scalar.activation(wo[:, p, 0, :], w_banks(p), ACT.Copy).then_inc(QW.t_hi, 1)

        def w_transpose(pe, b, c, first):
            for p in range(2):
                if p == 1 and c < 4:
                    pe.wait_ge(sim_sb, b * R + (R if first else 2 * R))
                if c >= 4:
                    pe.wait_ge(QW.t_lo, b * 4 + (c + p - 1))
                pe.wait_ge(QW.dq_ok, b * 4 + (c + p + 1))
                for i in range(NGRP):
                    for k in range(KD):
                        ins = nc.tensor.transpose(bank[4 * p + k][:, i * P:(i + 1) * P],
                                                  wst[:, p, i, k * P:(k + 1) * P], ident[:, :])
                ins.then_inc(QW.t_mm, 1)

        def w_scales(dve, link, b, c):
            for p in range(2):
                dve.wait_ge(fw_in[p], b * 32 + (c // 2 + 1) * 16)
                scales(link, w_flat(p), wsc[:, p], NGRP * NB, W_SCALE).then_inc(QW.inv_ok, 1)

        def w_round(dve, link, b, c):
            for p in range(2):
                dve.wait_ge(QW.up_ok, b * 4 + (c + p + 1))
                round_e4m3(link, w_flat(p), we[:, p, :]).then_inc(QW.n_ok, 1)

        def w_low(dve, b, c):
            for p in range(2):
                dve.wait_ge(QW.t_hi, b * 4 + (c + p + 1))
                nc.vector.tensor_tensor(wo[:, p, 1, :], w_banks(p), wo[:, p, 0, :], ALU.subtract).then_inc(QW.t_lo, 1)

        def d_gpsimd(pool):
            pool.wait_ge(x3_ok, 1)

            def quant_x(n, p):
                pool_q(pool, QX, n + 1, fx[:, p, :], xsc, NB)
                pool_dq(pool, QX, n + 1, fx[:, p, :], xsc, NB)

            def quant_h(n, p):
                pool_q(pool, QH, n + 1, hq[:, p, :], hsc, F // QB)
                pool_dq(pool, QH, n + 1, hq[:, p, :], hsc, F // QB)

            quant_x(0, 0)
            with pool.Fori(0, TT // 2 - 1) as j:
                for p in range(2):
                    quant_x(j * 2 + (p + 1), 1 - p)
                    quant_h(j * 2 + p, p)
            quant_x(TT - 1, 1)
            quant_h(TT - 2, 0)
            quant_h(TT - 1, 1)

        def d_scalar(act):
            def quant_x(n, p):
                act_up(act, QX, n + 1, fx[:, p, :], fe)
                act.wait_ge(QX.t_mm, n + 1)
                nc.scalar.activation(fxT[:, p, 0, :], bank[7], ACT.Copy).then_inc(QX.t_hi, 1)

            def gates(n):
                for c in range(FCH):
                    act.wait_ge(gu_mm, n * FCH + (c + 1))
                    nc.scalar.activation(sg[:, c % 2, :], bank[2 * (c % 2)], ACT.Silu, scale=FSCALE).then_inc(sg_ok, 1)

            def quant_h(n, p):
                for c in range(FCH):
                    act.wait_ge(QH.t_mm, n * FCH + (c + 1))
                    nc.scalar.activation(fhT[:, 0, 4 * c:4 * c + 4, :], bank[4 + c % 2].rearrange("p (k f) -> p k f", k=4),
                                         ACT.Copy).then_inc(QH.t_hi, 1)

            quant_x(0, 0)

            def tile(n, p, last):
                gates(n)
                if not last:
                    quant_x(n + 1, 1 - p)
                act_up(act, QH, n + 1, hq[:, p, :], he)

            gates(0)
            quant_x(1, 1)
            act_up(act, QH, 1, hq[:, 0, :], he)
            with act.Fori(0, TT // 2 - 1) as j:
                for p in range(2):
                    n = j * 2 + (p + 1)
                    gates(n)
                    quant_x(n + 1, p)
                    quant_h(n - 1, p)
                    act_up(act, QH, n + 1, hq[:, 1 - p, :], he)
            gates(TT - 1)
            quant_h(TT - 2, 0)
            act_up(act, QH, TT, hq[:, 1, :], he)
            quant_h(TT - 1, 1)

        def d_tensor(pe):
            def t_x(n, p):
                pe.wait_ge(QX.dq_ok, n + 1)
                for k in range(KD):
                    ins = nc.tensor.transpose(bank[7][:, k * P:(k + 1) * P], fx[:, p, k * P:(k + 1) * P], ident[:, :])
                ins.then_inc(QX.t_mm, 1)

            def gates(n, p, first):
                pe.wait_ge(QX.t_lo, n + 1)
                for c in range(FCH):
                    if not (first and c < 2):
                        pe.wait_ge(h_ok, n * FCH + (c - 1))
                    for w, b in ((GW, 2 * (c % 2)), (UW, 2 * (c % 2) + 1)):
                        i = 0
                        for k in range(KD):
                            for a, l in ((0, 0), (0, 1), (1, 0)):
                                ins = nc.tensor.matmul(bank[b], fxT[:, p, a, k * P:(k + 1) * P],
                                                       w[:, c, l, k, :], start=(i == 0), stop=(i == 3 * KD - 1))
                                i += 1
                    ins.then_inc(gu_mm, 1)

            def down(n, p):
                pe.wait_ge(QH.dq_ok, n + 1)
                for c in range(FCH):
                    if c >= 2:
                        pe.wait_ge(QH.t_lo, n * FCH + (c - 1))
                    for k in range(4):
                        ins = nc.tensor.transpose(bank[4 + c % 2][:, k * P:(k + 1) * P],
                                                  hq[:, p, (4 * c + k) * P:(4 * c + k + 1) * P], ident[:, :])
                    ins.then_inc(QH.t_mm, 1)
                pe.wait_ge(x4_ok, n + 1)
                i = 0
                for k in range(FT):
                    if k % 4 == 0:
                        pe.wait_ge(QH.t_lo, n * FCH + (k // 4 + 1))
                    for a, l in ((0, 0), (0, 1), (1, 0)):
                        ins = nc.tensor.matmul(bank[6], fhT[:, a, k, :], DW[:, k // KD, l, k % KD, :], start=(i == 0), stop=(i == 3 * FT - 1))
                        i += 1
                ins.then_inc(d_mm, 1)

            t_x(0, 0)
            pe.wait_ge(gw_in, 16 * FCH)
            pe.wait_ge(uw_in, 16 * FCH)
            gates(0, 0, True)
            t_x(1, 1)
            pe.wait_ge(dw_in, 16 * FCH)
            with pe.Fori(0, TT // 2 - 1) as j:
                for p in range(2):
                    n = j * 2 + (p + 1)
                    gates(n, 1 - p, False)
                    t_x(n + 1, p)
                    down(n - 1, p)
            gates(TT - 1, 1, False)
            down(TT - 2, 0)
            down(TT - 1, 1)

        def d_vector(dve):
            link = Chain(dve, dve_chain)
            link.restart()
            v = nc.vector
            v.nop().then_inc(x4_ok, 1)
            stats(link, range(TT), bnst_d)
            link(v.tensor_scalar(GATES[:, 7:8], GATES[:, 3:4], FSCALE, None, ALU.mult))

            def x_first(n, p):
                v.tensor_scalar(fx[:, p, :], X[:, n, :], MV[:, bass.ds(n, 1), 0], RSTD[:, bass.ds(n, 1)],
                                ALU.subtract, ALU.mult).then_inc(fxn_ok, 1)
                dve.wait_ge(fxn_ok, n + 1)
                scales(link, fx[:, p, :], xsc, NB, A_SCALE).then_inc(QX.inv_ok, 1)

            def x_second(n, p):
                dve.wait_ge(QX.up_ok, n + 1)
                round_e4m3(link, fx[:, p, :], fe).then_inc(QX.n_ok, 1)

            def x_third(n, p):
                dve.wait_ge(QX.t_hi, n + 1)
                v.tensor_tensor(fxT[:, p, 1, :], bank[7], fxT[:, p, 0, :], ALU.subtract).then_inc(QX.t_lo, 1)

            def hidden(n, p, c):
                dve.wait_ge(sg_ok, n * FCH + (c + 1))
                v.scalar_tensor_tensor(hq[:, p, c * D:(c + 1) * D], bank[2 * (c % 2) + 1], FSCALE, sg[:, c % 2, :],
                                       ALU.mult, ALU.mult).then_inc(h_ok, 1)

            def h_first(n, p):
                dve.wait_ge(h_ok, n * FCH + FCH)
                scales(link, hq[:, p, :], hsc, F // QB, A_SCALE).then_inc(QH.inv_ok, 1)

            def h_second(n, p):
                dve.wait_ge(QH.up_ok, n + 1)
                round_e4m3(link, hq[:, p, :], he).then_inc(QH.n_ok, 1)

            def h_third(n, p):
                for c in range(FCH):
                    dve.wait_ge(QH.t_hi, n * FCH + (c + 1))
                    v.tensor_tensor(fhT[:, 1, 4 * c:4 * c + 4, :], bank[4 + c % 2].rearrange("p (k f) -> p k f", k=4),
                                    fhT[:, 0, 4 * c:4 * c + 4, :], ALU.subtract).then_inc(QH.t_lo, 1)

            def add(n):
                dve.wait_ge(d_mm, n + 1)
                v.scalar_tensor_tensor(X[:, n, :], bank[6], GATES[:, 7:8], X[:, n, :], ALU.mult, ALU.add).then_inc(x4_ok, 1)

            link.restart()
            x_first(0, 0)
            x_second(0, 0)
            x_third(0, 0)
            x_first(1, 1)
            for c in range(FCH):
                hidden(0, 0, c)
            x_second(1, 1)
            x_third(1, 1)
            h_first(0, 0)
            h_second(0, 0)
            with dve.Fori(0, TT // 2 - 1) as j:
                link.restart()
                for p in range(2):
                    n = j * 2 + (p + 1)
                    x_first(n + 1, p)
                    hidden(n, 1 - p, 0)
                    hidden(n, 1 - p, 1)
                    x_second(n + 1, p)
                    hidden(n, 1 - p, 2)
                    hidden(n, 1 - p, 3)
                    x_third(n + 1, p)
                    h_third(n - 1, p)
                    h_first(n, 1 - p)
                    h_second(n, 1 - p)
                    add(n - 1)
            link.restart()
            for c in range(FCH):
                hidden(TT - 1, 1, c)
            h_third(TT - 2, 0)
            h_first(TT - 1, 1)
            h_second(TT - 1, 1)
            add(TT - 2)
            h_third(TT - 1, 1)
            add(TT - 1)


        def end_sync(sp):
            for b in range(B):
                sp.wait_ge(x4_ok, (b + 1) * R + 1)
                sp.dma_start(out_rows[:, b * R:(b + 1) * R, :], X[:, b * R:(b + 1) * R, :]).then_inc(out_done, 16)
            sp.wait_ge(out_done, 16 * B)

        @block.sync
        def _(sp):
            a_sync(sp)
            b_sync(sp)
            c_sync(sp)
            end_sync(sp)

        @block.gpsimd
        def _(pool):
            a_gpsimd(pool)
            b_gpsimd(pool)
            c_gpsimd(pool)
            d_gpsimd(pool)

        @block.scalar
        def _(act):
            a_scalar(act)
            b_scalar(act)
            c_scalar(act)
            d_scalar(act)

        @block.tensor
        def _(pe):
            a_tensor(pe)
            b_tensor(pe)
            c_tensor(pe)
            d_tensor(pe)

        @block.vector
        def _(dve):
            a_vector(dve)
            b_vector(dve)
            c_vector(dve)
            d_vector(dve)


_INS = ["x", "ctx_512", "g_xattn", "g_ffn", "L0_xattn_Wq", "L0_xattn_Wk", "L0_xattn_gamma_raw", "L0_ffn_gate_w",
        "L0_ffn_w1", "L0_ffn_w3", "L0_ffn_w2", "L0_ffn_sw1", "L0_ffn_sw3", "L0_ffn_sw2", "L1_ffn_gate_w",
        "L1_ffn_up_w", "L1_ffn_down_w"]
_OUTS = [((4, 512, 512), "float32")]


def kernel(**inputs):
    import numpy as _np
    import concourse.bacc as _bacc
    from concourse import mybir as _mybir
    from concourse.bass_utils import run_bass_kernel_spmd as _run

    nc = _bacc.Bacc("TRN2", target_bir_lowering=False, num_devices=1)
    arrays, args = {}, []
    for name in _INS:
        a = _np.ascontiguousarray(inputs[name])
        if a.ndim == 0:
            a = a.reshape(1)
        arrays[f"in_{name}_dram"] = a
        args.append(nc.dram_tensor(f"in_{name}_dram", a.shape, _mybir.dt.from_np(a.dtype), kind="ExternalInput").ap())
    for i, (shape, dtype) in enumerate(_OUTS):
        dt = _mybir.dt.from_np(_np.dtype(dtype))
        args.append(nc.dram_tensor(f"out_{i}_dram", shape, dt, kind="ExternalOutput").ap())
    build(nc, *args)
    r = _run(nc, [arrays], core_ids=[0])
    got = tuple(r.results[0][f"out_{i}_dram"] for i in range(len(_OUTS)))
    return got[0]
```

```python
from contextlib import ExitStack

import concourse.bass as bass
from concourse import mybir

P = 128
F32 = mybir.dt.float32
F16 = mybir.dt.float16
I32 = mybir.dt.int32
U32 = mybir.dt.uint32
ALU = mybir.AluOpType
ACT = mybir.ActivationFunctionType
AX_X = mybir.AxisListType.X
NEG = -3.0e38
LN_EPS = 1e-5
ROUND = 12582912.0
W_SCALE = 256.0
A_SCALE = 16.0


class Chain:

    def __init__(self, engine, sem):
        self.engine, self.sem, self.n = engine, sem, 0

    def restart(self):
        self.engine.sem_clear(self.sem)
        self.n = 0

    def __call__(self, instruction):
        self.n += 1
        instruction.then_inc(self.sem, 1)
        self.engine.wait_ge(self.sem, self.n)


def build(nc, x, ctx, g_xattn, g_ffn, wq, wk, gamma_raw, gate_w, w1, w3, w2, sw1, sw3, sw2,
          fgate_w, fup_w, fdown_w, out):
    B, S, D = x.shape
    C = ctx.shape[2]
    E, _, I = w1.shape
    T = B * S
    TT = T // P
    R = S // P
    KD = D // P
    TOPK = int(S * 0.3)
    KI = (I + P - 1) // P
    I_LAST = I - (KI - 1) * P
    SLOTS = 2 * TT + E
    E2 = 2

    stack = ExitStack()
    with stack:
        def sb(name, shape, dt=F32):
            return stack.enter_context(nc.sbuf_tensor(name, shape, dt))

        def sem(name):
            return stack.enter_context(nc.semaphore(name))

        PS = stack.enter_context(nc.psum_tensor("PS", [P, 8, 512], F32))
        bank = [PS[:, i, :] for i in range(8)]

        X = sb("X", [P, TT, D])
        BIG = sb("BIG", [P, 34816])
        WORK = sb("WORK", [P, 9632])
        ident = sb("ident", [P, P])
        MV = sb("MV", [P, TT, 2])
        RSTD = sb("RSTD", [P, TT])
        NEWT = sb("NEWT", [P, 2, TT])
        GATES = sb("GATES", [P, 8])

        def carve(region, name, at, shape, dt=F32):
            n = 1
            for s in shape[1:]:
                n *= s
            size = n * (2 if dt == F16 else 4)
            words = (size + 3) // 4
            assert at % 4 == 0 and at // 4 + words <= region.shape[1], (name, at, size)
            v = region[0:shape[0], at // 4:at // 4 + words]
            if dt != F32:
                v = v.bitcast(dt)
            if len(shape) == 3:
                v = v.rearrange("p (a b) -> p a b", b=shape[2])
            elif len(shape) == 4:
                v = v.rearrange("p (a b c) -> p a b c", b=shape[2], c=shape[3])
            elif len(shape) == 5:
                v = v.rearrange("p (a b c d) -> p a b c d", b=shape[2], c=shape[3], d=shape[4])
            return v

        x_in = [sem(f"x_in{b}") for b in range(B)]
        ctx_in = sem("ctx_in")
        wqk_in = sem("wqk_in")
        gates_in = sem("gates_in")
        ident_ok = sem("ident_ok")
        dve_chain = sem("dve_chain")
        act_chain = sem("act_chain")
        pool_chain = sem("pool_chain")
        gates_ok = sem("gates_ok")
        out_done = sem("out_done")

        block = stack.enter_context(nc.Block())
        ctx_rows = ctx.rearrange("b (r p) c -> p (b r) c", p=P)
        x_rows = x.rearrange("b (r p) d -> p (b r) d", p=P)
        out_rows = out.rearrange("b (r p) d -> p (b r) d", p=P)

        ctx_tok = carve(WORK, "ctx_tok", 0, [P, TT, C])
        sim = carve(WORK, "sim", 0, [P, R, S])
        ctxT = carve(WORK, "ctxT", 8192, [P, T])
        qT = carve(WORK, "qT", 16384, [P, S])
        kT = carve(WORK, "kT", 18432, [P, S])
        topw = carve(WORK, "topw", 20480, [P, S])
        sig = carve(WORK, "sig", 22528, [P, 2, S])
        wqk = carve(WORK, "wqk", 26624, [P, 2, P])
        wqkT = carve(WORK, "wqkT", 27648, [P, 2, P])
        AL = carve(WORK, "AL", 28672, [P, TT])
        BE = carve(WORK, "BE", 28736, [P, TT])
        top8 = carve(WORK, "top8", 28800, [P, 8])
        th = carve(WORK, "th", 28832, [P, R])
        bnst = carve(WORK, "bnst", 37632 + 176 * R, [P, 4, 6])
        srow = [carve(WORK, f"srow{i}", 37632 + i * 4 * R, [P, R]) for i in range(9)]
        th_try, row_dev, step, gain, count0, count1, diff, outside, rank = srow
        smv = carve(WORK, "smv", 37632 + 36 * R, [P, R, 2])
        top16 = carve(WORK, "top16", 37632 + 44 * R, [P, R, 2 * 8])
        pick = carve(WORK, "pick", 37632 + 108 * R, [P, R, 2 * 8])
        missed = carve(WORK, "missed", 37632 + 172 * R, [P, R], F16)
        misses = carve(WORK, "misses", 37632 + 174 * R, [P, 1])
        missed_any = carve(WORK, "missed_any", 37632 + 175 * R, [P, 1], I32)
        WINDOW = 2 * 8
        AIM = TOPK - (WINDOW + 1) / 2.0
        TRIES = 3
        SIM_SCALE = 1.0 / (float(C // 4) ** 0.5 * 4)

        ctxT_mm = sem("ctxT_mm")
        ctxT_sb = sem("ctxT_sb")
        coef_ok = sem("coef_ok")
        qk_mm = sem("qk_mm")
        qk_sb = sem("qk_sb")
        sim_mm = sem("sim_mm")
        sim_sb = sem("sim_sb")
        sig_sb = sem("sig_sb")
        xmix = sem("xmix")
        adj_ok = sem("adj_ok")
        adjT_mm = sem("adjT_mm")
        x1_ok = sem("x1_ok")
        missed_ok = sem("missed_ok")
        missed_mm = sem("missed_mm")

        def rsqrt(link, var, y, n):
            a, b = NEWT[:, 0, 0:n], NEWT[:, 1, 0:n]
            v = nc.vector
            link(v.tensor_scalar(a, var, LN_EPS, None, ALU.add))
            link(v.tensor_scalar(y.bitcast(I32), a.bitcast(I32), -0.5, 1597463007.0, ALU.mult, ALU.add))
            for _ in range(4):
                link(v.tensor_tensor(b, y, y, ALU.mult))
                link(v.tensor_tensor(b, b, a, ALU.mult))
                link(v.tensor_scalar(b, b, -0.5, 1.5, ALU.mult, ALU.add))
                link(v.tensor_tensor(y, y, b, ALU.mult))

        def row_moments(link, b, st):
            for r in range(R):
                nc.vector.bn_stats(st[:, r, :], X[:, b * R + r, :]).then_inc(link.sem, 1)
            link.n += R
            link.engine.wait_ge(link.sem, link.n)
            for r in range(R):
                nc.vector.bn_aggr(MV[:, b * R + r, :], st[:, r, :]).then_inc(link.sem, 1)
            link.n += R
            link.engine.wait_ge(link.sem, link.n)

        W13N = 2 * KD * 2 * I
        W2N = 2 * KI * D
        W13 = BIG[:, 0:E * W13N // 2].bitcast(F16)
        W2 = BIG[:, E * W13N // 2:E * (W13N + W2N) // 2].bitcast(F16)
        NBUF = 3
        stage = [carve(WORK, f"stage{i}", 28928 + i * 2816, [P, 704]) for i in range(NBUF)]
        stage_in = [sem(f"stage_in{i}") for i in range(NBUF)]
        split_s = sem("split_s")
        split_h = sem("split_h")
        split_l = sem("split_l")
        pad_ok = sem("pad_ok")
        CHUNKS = [(0, 0, 2), (0, 2, 2), (1, 0, 2), (1, 2, 2), (2, 0, 1), (2, 1, 1), (2, 2, 1)]
        NCH = len(CHUNKS)
        PER_BUF = [len(range(i, NCH, NBUF)) for i in range(NBUF)]

        def rows_of(m, k0, nk):
            return I_LAST if m == 2 and k0 == KI - 1 else P

        def chunk_src(j, src):
            m, k0, nk = CHUNKS[j]
            a = src[m]
            if m < 2:
                return a[k0 * P:(k0 + nk) * P, :].rearrange("(k p) i -> p k i", p=P)
            return a[k0 * P:k0 * P + rows_of(m, k0, nk), :]

        def chunk_stage(j):
            m, k0, nk = CHUNKS[j]
            b = stage[j % NBUF]
            if m < 2:
                return b[:, 0:2 * I].rearrange("p (k i) -> p k i", k=2)
            return b[0:rows_of(m, k0, nk), 0:D]

        def chunk_dst(j, slot, lo):
            m, k0, nk = CHUNKS[j]
            if m < 2:
                v = W13[:, bass.ds(slot * W13N + lo * (W13N // 2) + k0 * 2 * I, 2 * 2 * I)]
                return v.rearrange("p (k m i) -> p k m i", k=2, m=2)[:, :, m, :]
            return W2[0:rows_of(m, k0, nk), bass.ds(slot * W2N + lo * (W2N // 2) + k0 * D, D)]

        def load_slot(sp, n, src):
            for j in range(NCH):
                sp.wait_ge(split_l, n * NCH + (1 + max(j - NBUF + 1, 0)))
                sp.dma_start(chunk_stage(j), chunk_src(j, src)).then_inc(stage_in[j % NBUF], 16)

        def split_hi(act, n, slot):
            for j in range(NCH):
                act.wait_ge(stage_in[j % NBUF], n * (16 * PER_BUF[j % NBUF]) + 16 * (j // NBUF + 1))
                nc.scalar.activation(chunk_stage(j), chunk_stage(j), ACT.Copy, scale=W_SCALE).then_inc(split_s, 1)
                act.wait_ge(split_s, n * NCH + (j + 1))
                nc.scalar.activation(chunk_dst(j, slot, 0), chunk_stage(j), ACT.Copy).then_inc(split_h, 1)

        def fast_hi(act, n, slot, chunks):
            for j in chunks:
                act.wait_ge(stage_in[j % NBUF], n * (16 * PER_BUF[j % NBUF]) + 16 * (j // NBUF + 1))
                nc.scalar.activation(chunk_dst(j, slot, 0), chunk_stage(j), ACT.Copy, scale=W_SCALE).then_inc(split_h, 1)

        def fast_lo(dve, n, slot, chunks):
            for j in chunks:
                dve.wait_ge(split_h, n * NCH + (j + 1))
                nc.vector.scalar_tensor_tensor(chunk_dst(j, slot, 1), chunk_stage(j), W_SCALE, chunk_dst(j, slot, 0),
                                               ALU.mult, ALU.subtract).then_inc(split_l, 1)

        def split_lo(pool, n, slot):
            for j in range(NCH):
                pool.wait_ge(split_h, n * NCH + (j + 1))
                nc.gpsimd.tensor_tensor(chunk_dst(j, slot, 1), chunk_stage(j), chunk_dst(j, slot, 0),
                                        ALU.subtract).then_inc(split_l, 1)

        def expert_src(e):
            return w1[e, :, :], w3[e, :, :], w2[e, :, :]

        def shared_src(h):
            return sw1[:, h * I:(h + 1) * I], sw3[:, h * I:(h + 1) * I], sw2[h * I:(h + 1) * I, :]

        def a_sync(sp):
            sp.dma_start(wqk[:, 0, :], wq).then_inc(wqk_in, 16)
            sp.dma_start(wqk[:, 1, :], wk).then_inc(wqk_in, 16)
            sp.dma_start(ctx_tok, ctx_rows).then_inc(ctx_in, 16)
            sp.dma_start(GATES[:, 0:2], g_xattn.rearrange("(a n) -> a n", a=1).to_broadcast([P, 2])).then_inc(gates_in, 16)
            sp.dma_start(GATES[:, 2:4], g_ffn.rearrange("(a n) -> a n", a=1).to_broadcast([P, 2])).then_inc(gates_in, 16)
            sp.dma_start(GATES[:, 4:5], gamma_raw.rearrange("(a n) -> a n", a=1).to_broadcast([P, 1])).then_inc(gates_in, 16)
            for c in (0, 1):
                w_load(sp, 0, c)
            for b in range(B):
                sp.dma_start(X[:, b * R:(b + 1) * R, :], x_rows[:, b * R:(b + 1) * R, :]).then_inc(x_in[b], 16)
            for c in (2, 3):
                w_load(sp, 0, c)
            for c in (0, 1):
                w_store(sp, 0, c)
            with sp.Fori(0, 2) as b:
                for c in (4, 5, 6, 7):
                    w_load(sp, b, c)
                for c in (2, 3):
                    w_store(sp, b, c)
                for i in range(2):
                    load_slot(sp, b * 2 + i, expert_src(b * 2 + i))
                for c in (4, 5):
                    w_store(sp, b, c)
            load_slot(sp, 4, expert_src(4))
            for c in (2, 3):
                w_store(sp, 2, c)
            for h in range(2):
                load_slot(sp, 5 + h, shared_src(h))

        def a_gpsimd(pool):
            link = Chain(pool, pool_chain)
            nc.gpsimd.nop().then_inc(split_l, 1)
            link(nc.gpsimd.memset(ident[:, :], 0.0))
            nc.gpsimd.affine_select(out=ident[:, :], in_=ident[:, :], compare_op=ALU.not_equal, fill=1.0,
                                    base=0, pattern=[[-1, P]], channel_multiplier=1).then_inc(ident_ok, 1)
            b_constants(pool, link)
            w_pool(pool, 0, 0)
            with pool.Fori(0, 2) as b:
                w_pool(pool, b, 2)
                w_pool(pool, b, 4)
                for i in range(2):
                    split_lo(pool, b * 2 + i, b * 2 + i)
            w_pool(pool, 2, 2)
            split_lo(pool, 4, 4)
            for p in range(2):
                pool.wait_ge(fw_st[p], 16 * NW // 2)
            pool.wait_ge(split_l, 5 * NCH + 1)
            pads(link, range(4, E))
            nc.gpsimd.nop().then_inc(pad_ok, 1)
            for h in range(2):
                split_lo(pool, 5 + h, E - 2 + h)

        def a_scalar(act):
            link = Chain(act, act_chain)
            act.wait_ge(gates_in, 48)
            link(nc.scalar.activation(GATES[:, 0:4], GATES[:, 0:4], ACT.Tanh))
            nc.scalar.activation(GATES[:, 4:5], GATES[:, 4:5], ACT.Sigmoid).then_inc(gates_ok, 1)
            for c in range(4):
                act.wait_ge(ctxT_mm, c + 1)
                nc.scalar.activation(ctxT[:, c * 512:(c + 1) * 512], bank[c][:, :], ACT.Copy).then_inc(ctxT_sb, 1)
            act.wait_ge(ctxT_mm, 5)
            nc.scalar.activation(wqkT.rearrange("p a b -> p (a b)"), bank[4][:, 0:2 * P], ACT.Copy).then_inc(ctxT_sb, 1)
            def head(b, first, between):
                for i, (dst, src) in enumerate(((qT, bank[2]), (kT, bank[3]))):
                    act.wait_ge(qk_mm, b * 2 + (i + 1))
                    nc.scalar.activation(dst, src[:, :], ACT.Copy).then_inc(qk_sb, 1)
                between()
                for r in range(R):
                    act.wait_ge(sim_mm, b * R + (r + 1))
                    nc.scalar.activation(sim[:, r, :], bank[4 + r][:, :], ACT.Copy).then_inc(sim_sb, 1)
                if first:
                    act.wait_ge(coef_ok, 1)
                for r in range(R):
                    xt = X[:, b * R + r, :]
                    nc.scalar.activation(xt, xt, ACT.Identity, scale=AL[:, bass.ds(b * R + r, 1)],
                                         bias=BE[:, bass.ds(b * R + r, 1)]).then_inc(xmix, 1)

            def sigmoids(b, rows=range(R)):
                act.wait_ge(sim_sb, b * R + R)
                for r in rows:
                    if r >= 2:
                        act.wait_ge(adj_ok, b * R + (r - 1))
                    nc.scalar.activation(sig[:, r % 2, :], sim[:, r, :], ACT.Sigmoid, scale=SIM_SCALE).then_inc(sig_sb, 1)

            head(0, True, lambda: w_act_up(act, 0, 0))
            w_act_hi(act, 0, 0, True)
            with act.Fori(0, 2) as b:
                sigmoids(b)
                head(b + 1, False, lambda: w_act_up(act, b, 2))
                w_act_hi(act, b, 2, False)
                w_act_up(act, b, 4)
                w_act_hi(act, b, 4, False)
                for i in range(2):
                    split_hi(act, b * 2 + i, b * 2 + i)
            sigmoids(2)
            head(3, False, lambda: w_act_up(act, 2, 2))
            w_act_hi(act, 2, 2, False)
            split_hi(act, 4, 4)
            sigmoids(3, (0, 1))
            for p in range(2):
                act.wait_ge(fw_st[p], 16 * NW // 2)
            split_hi(act, 5, E - 2)
            sigmoids(3, (2, 3))
            split_hi(act, 6, E - 1)

        def a_tensor(pe):
            pe.wait_ge(ident_ok, 1)
            pe.wait_ge(ctx_in, 16)
            for c in range(4):
                for j in range(4):
                    ins = nc.tensor.transpose(bank[c][:, j * P:(j + 1) * P], ctx_tok[:, c * 4 + j, :], ident[:, :])
                ins.then_inc(ctxT_mm, 1)
            pe.wait_ge(wqk_in, 32)
            for j in range(2):
                ins = nc.tensor.transpose(bank[4][:, j * P:(j + 1) * P], wqk[:, j, :], ident[:, :])
            ins.then_inc(ctxT_mm, 1)
            pe.wait_ge(ctxT_sb, 5)
            def head(b):
                for i in range(2):
                    nc.tensor.matmul(bank[2 + i][:, :], wqkT[:, i, :], ctxT[:, bass.ds(b * S, S)],
                                     start=True, stop=True).then_inc(qk_mm, 1)
                pe.wait_ge(qk_sb, b * 2 + 2)
                for r in range(R):
                    nc.tensor.matmul(bank[4 + r][:, :], qT[:, r * P:(r + 1) * P], kT, start=True, stop=True).then_inc(sim_mm, 1)

            def rest(b):
                pe.wait_ge(missed_ok, b + 1)
                nc.tensor.matmul(bank[0][:, 0:R], ONES[:, :], missed, start=True, stop=True).then_inc(missed_mm, 1)
                pe.wait_ge(adj_ok, b * R + R)
                for r in range(R):
                    for c in range(R):
                        ins = nc.tensor.transpose(bank[r][:, c * P:(c + 1) * P], sim[:, c, r * P:(r + 1) * P], ident[:, :])
                    ins.then_inc(adjT_mm, 1)

            head(0)
            w_transpose(pe, 0, 0, True)
            pe.wait_ge(const_ok, 1)
            with pe.Fori(0, 2) as b:
                rest(b)
                pe.wait_ge(x1_ok, b * R + R)
                head(b + 1)
                for c in (2, 4):
                    w_transpose(pe, b, c, False)
            rest(2)
            pe.wait_ge(x1_ok, 3 * R)
            head(3)
            w_transpose(pe, 2, 2, False)
            rest(3)

        def a_vector(dve):
            link = Chain(dve, dve_chain)
            v = nc.vector
            w_scales(dve, link, 0, 0)
            for b in range(B):
                dve.wait_ge(x_in[b], 16)
                row_moments(link, b, bnst)
            rsqrt(link, MV[:, :, 1], RSTD[:, :], TT)
            dve.wait_ge(gates_ok, 1)
            link(v.tensor_tensor(GATES[:, 6:7], GATES[:, 0:1], GATES[:, 4:5], ALU.mult))
            link(v.tensor_tensor(GATES[:, 5:6], GATES[:, 0:1], GATES[:, 6:7], ALU.subtract))
            link(v.tensor_scalar(GATES[:, 6:7], GATES[:, 6:7], 0.5, None, ALU.mult))
            link(v.tensor_scalar(AL, RSTD[:, :], GATES[:, 5:6], None, ALU.mult))
            link(v.scalar_tensor_tensor(BE, AL, -1.0, MV[:, :, 0], ALU.mult, ALU.mult))
            v.tensor_scalar(AL, AL, 1.0, None, ALU.add).then_inc(coef_ok, 1)
            w_round(dve, link, 0, 0)
            dve.wait_ge(const_ok, 1)

            def search(b):
                link.restart()
                dve.wait_ge(sim_sb, b * R + R)
                v.nop(nofuse=True)
                for r in range(R):
                    v.bn_stats(bnst[:, r, :], sim[:, r, :]).then_inc(dve_chain, 1)
                dve.wait_ge(dve_chain, R)
                for r in range(R):
                    v.bn_aggr(smv[:, r, :], bnst[:, r, :]).then_inc(dve_chain, 1)
                dve.wait_ge(dve_chain, 2 * R)
                link.n = 2 * R
                link(v.tensor_scalar(row_dev.bitcast(I32), smv[:, :, 1].bitcast(I32), 0.5, 532487669.0, ALU.mult, ALU.add))
                link(v.scalar_tensor_tensor(th_try, row_dev, 0.52, smv[:, :, 0], ALU.mult, ALU.add))
                link(v.tensor_scalar(gain, row_dev, 1.0 / (0.36 * S), None, ALU.mult))
                for n in range(TRIES):
                    count, last = (count0, count1) if n % 2 == 0 else (count1, count0)
                    for r in range(R):
                        link(v.tensor_scalar(topw, sim[:, r, :], th_try[:, r:r + 1], None, ALU.is_ge, ALU.add,
                                             accum_out=count[:, r:r + 1]))
                    if n:
                        link(v.tensor_tensor(diff, count, last, ALU.subtract))
                        link(v.scalar_tensor_tensor(diff, diff, -1.0, diff, ALU.mult, ALU.max))
                        link(v.tensor_scalar(diff, diff, 1.0, None, ALU.max))
                        link(v.reciprocal(diff, diff))
                        link(v.scalar_tensor_tensor(step, step, -1.0, step, ALU.mult, ALU.max))
                        link(v.tensor_tensor(gain, step, diff, ALU.mult))
                    link(v.tensor_scalar(outside, count, -AIM, None, ALU.add))
                    link(v.tensor_tensor(step, outside, gain, ALU.mult))
                    link(v.tensor_tensor(outside, outside, outside, ALU.mult))
                    link(v.tensor_scalar(outside, outside, WINDOW ** 2 / 4.0, None, ALU.is_gt))
                    link(v.tensor_tensor(step, step, outside, ALU.mult))
                    link(v.tensor_tensor(th_try, th_try, step, ALU.add))

            def threshold(b):
                link.restart()
                for r in range(R):
                    link(v.tensor_scalar(topw, sim[:, r, :], th_try[:, r:r + 1], None, ALU.is_ge, ALU.add,
                                         accum_out=rank[:, r:r + 1]))
                    link(v.scalar_tensor_tensor(topw, topw, NEG, sim[:, r, :], ALU.mult, ALU.add))
                    link(v.max(top16[:, r, 0:8], topw))
                    link(v.match_replace(topw, top16[:, r, 0:8], topw, NEG))
                    link(v.max(top16[:, r, 8:16], topw))
                link(v.tensor_scalar(rank, rank, -1.0, TOPK - 1.0, ALU.mult, ALU.add))
                link(v.tensor_scalar(outside, rank, (1.0 - WINDOW) / 2.0, None, ALU.add))
                link(v.tensor_tensor(outside, outside, outside, ALU.mult))
                v.tensor_scalar(missed, outside, WINDOW ** 2 / 4.0, None, ALU.is_gt).then_inc(missed_ok, 1)
                link(v.tensor_tensor(pick, IOTA[:, 0:WINDOW].unsqueeze(1).to_broadcast([P, R, WINDOW]),
                                     rank.unsqueeze(2).to_broadcast([P, R, WINDOW]), ALU.is_equal))
                link(v.tensor_tensor(pick, pick, top16, ALU.mult))
                link(v.tensor_reduce(th, pick, AX_X, ALU.add))
                dve.wait_ge(missed_mm, b + 1)
                v.nop(nofuse=True)
                link(v.tensor_reduce(misses, bank[0][:, 0:R], AX_X, ALU.add))
                link(v.tensor_copy(missed_any, misses))
                some = dve.value_load(missed_any[0:1, 0:1], min_val=0, max_val=P * R)
                with dve.If(some > 0):
                    for r in range(R):
                        link.restart()
                        link(v.tensor_copy(topw, sim[:, r, :]))
                        with dve.Fori(0, (TOPK - 1) // 8):
                            link.restart()
                            link(v.max(top8, topw))
                            link(v.match_replace(topw, top8, topw, NEG))
                        link.restart()
                        link(v.max(top8, topw))
                        k = (TOPK - 1) % 8
                        link(v.tensor_copy(th[:, r:r + 1], top8[:, k:k + 1]))
                link.restart()

            def mix(b):
                for r in range(R):
                    dve.wait_ge(sig_sb, b * R + (r + 1))
                    v.scalar_tensor_tensor(sim[:, r, :], sim[:, r, :], th[:, r:r + 1], sig[:, r % 2, :],
                                           ALU.is_ge, ALU.mult).then_inc(adj_ok, 1)
                dve.wait_ge(adj_ok, b * R + R)
                for r in range(R):
                    xt = X[:, b * R + r, :]
                    dve.wait_ge(xmix, b * R + (r + 1))
                    link(v.scalar_tensor_tensor(xt, sim[:, r, :], GATES[:, 6:7], xt, ALU.mult, ALU.add))
                    dve.wait_ge(adjT_mm, b * R + (r + 1))
                    v.scalar_tensor_tensor(xt, bank[r][:, :], GATES[:, 6:7], xt, ALU.mult, ALU.add).then_inc(x1_ok, 1)

            with dve.Fori(0, 2) as b:
                search(b)
                w_low(dve, b, 0)
                threshold(b)
                mix(b)
                w_scales(dve, link, b, 2)
                w_round(dve, link, b, 2)
                w_scales(dve, link, b, 4)
                w_low(dve, b, 2)
                w_round(dve, link, b, 4)
            search(2)
            w_low(dve, 2, 0)
            threshold(2)
            mix(2)
            w_scales(dve, link, 2, 2)
            w_round(dve, link, 2, 2)
            search(3)
            w_low(dve, 2, 2)
            threshold(3)
            mix(3)


        xn = carve(WORK, "xn", 0, [P, 2, D])
        xT = carve(WORK, "xT", 4096, [P, 2, 2, KD * P], F16)
        sil = carve(WORK, "sil", 8192, [P, 2, I])
        hid = carve(WORK, "hid", 11264, [P, 2, KI * P])
        hT = carve(WORK, "hT", 14336, [P, 2, 2, KI * P], F16)
        yo = carve(WORK, "yo", 17408, [P, 2, D])
        LG = carve(WORK, "LG", 21504, [P, TT, E])
        MX = carve(WORK, "MX", 22016, [P, TT, 8])
        MI = carve(WORK, "MI", 22528, [P, TT, 8], U32)
        MIF = carve(WORK, "MIF", 23040, [P, TT, 8])
        OH = carve(WORK, "OH", 23552, [P, E2, TT, E])
        EQ = carve(WORK, "EQ", 17408, [P, SLOTS, E])
        row_hot = carve(WORK, "row_hot", 4096, [P, E2 * TT, P], F16)
        tile_hot = carve(WORK, "tile_hot", 12288, [P, E2 * TT, SLOTS], F16)
        TILE = carve(WORK, "TILE", 18688, [P, E2, TT])
        ROW = carve(WORK, "ROW", 18816, [P, E2, TT])
        gatew = carve(WORK, "gatew", 24576, [E, D])
        T1 = carve(WORK, "T1", 24576, [P, TT, E])
        T2 = carve(WORK, "T2", 25088, [P, TT, E])
        OFF = carve(WORK, "OFF", 26112, [P, E + 1])
        CNT = carve(WORK, "CNT", 26148, [P, E])
        CW = carve(WORK, "CW", 26180, [P, TT, 2])
        POSF = carve(WORK, "POSF", 26308, [P, E2, TT])
        POS = carve(WORK, "POS", 26436, [P, E2, TT], U32)
        EIDF = carve(WORK, "EIDF", 26564, [P, SLOTS])
        EID = carve(WORK, "EID", 26724, [P, SLOTS], I32)
        IDX = carve(WORK, "IDX", 26884, [P, SLOTS], U32)
        idx1 = carve(WORK, "idx1", 27044, [P, 2], U32)
        gwT = carve(WORK, "gwT", 27052, [P, 2, KD * E], F16)
        SEL = carve(WORK, "SEL", 27180, [P, TT, E], F16)
        mgath = [carve(WORK, f"mgath{i}", at, [P, 2, D]) for i, at in enumerate((28928, 33024, 10240, 14336))]
        LT = sb("LT", [P, P], F16)
        ONES = sb("ONES", [P, P], F16)
        IOTA = sb("IOTA", [P, P])
        TOK = sb("TOK", [P, TT])
        IOTAI = carve(WORK, "IOTAI", 20480, [P, P], I32)
        TOKI = carve(WORK, "TOKI", 20992, [P, TT], I32)
        xn_dram = nc.dram_tensor("xn_scratch", [T, D], F32, kind="Internal").ap()
        y_dram = nc.dram_tensor("y_scratch", [SLOTS * P, D], F32, kind="Internal").ap()

        const_ok = sem("const_ok")
        gatew_in = sem("gatew_in")
        gw_mm = sem("gw_mm")
        gw_hi = sem("gw_hi")
        gw_ok = sem("gw_ok")
        xn_st = [sem("xn_st0"), sem("xn_st1")]
        lg_mm = sem("lg_mm")
        lg_sb = sem("lg_sb")
        d12_ok = sem("d12_ok")
        e12_ok = sem("e12_ok")
        sel_ok = sem("sel_ok")
        rank_mm = sem("rank_mm")
        pos_ok = sem("pos_ok")
        eid_ok = sem("eid_ok")
        hot_ok = sem("hot_ok")
        map_mm = sem("map_mm")
        idx_ok = sem("idx_ok")
        idx1_ok = sem("idx1_ok")
        gath = [sem("gath0"), sem("gath1")]
        yst = [sem("yst0"), sem("yst1")]
        mg_in = [sem(f"mg_in{p}") for p in range(len(mgath))]
        mg_used = sem("mg_used")

        class Unit:

            def __init__(self, name):
                self.x_ok = sem(f"{name}_x_ok")
                self.tx_mm = sem(f"{name}_tx_mm")
                self.tx_hi = sem(f"{name}_tx_hi")
                self.tx_lo = sem(f"{name}_tx_lo")
                self.hg_mm = sem(f"{name}_hg_mm")
                self.sil_ok = sem(f"{name}_sil_ok")
                self.hid_ok = sem(f"{name}_hid_ok")
                self.th_mm = sem(f"{name}_th_mm")
                self.th_hi = sem(f"{name}_th_hi")
                self.th_lo = sem(f"{name}_th_lo")
                self.y_mm = sem(f"{name}_y_mm")
                self.y_out = sem(f"{name}_y_out")

        SH, MO = Unit("sh"), Unit("mo")

        def pe_tx(q, p, t):
            for k in range(KD):
                ins = nc.tensor.transpose(bank[0][:, k * P:(k + 1) * P], xn[:, p, k * P:(k + 1) * P], ident[:, :])
            ins.then_inc(q.tx_mm, 1)

        def pe_hg(pe, q, p, up, slot):
            half = W13N // 2
            for m in range(2):
                n = 0
                for k in range(KD):
                    for a, w in ((0, 0), (0, 1), (1, 0)):
                        ins = nc.tensor.matmul(bank[1 + 2 * m + up][:, 0:I], xT[:, p, a, k * P:(k + 1) * P],
                                               W13[:, bass.ds(slot * W13N + (w * half + k * 2 * I + m * I), I)],
                                               start=(n == 0), stop=(n == 3 * KD - 1))
                        n += 1
            ins.then_inc(q.hg_mm, 1)

        def pe_th(q, up):
            for k in range(KI):
                ins = nc.tensor.transpose(bank[5][:, k * P:(k + 1) * P], hid[:, up, k * P:(k + 1) * P], ident[:, :])
            ins.then_inc(q.th_mm, 1)

        def pe_y(q, up, slot, dst, first, last):
            n = 0
            for k in range(KI):
                for a, w in ((0, 0), (0, 1), (1, 0)):
                    ins = nc.tensor.matmul(dst[:, :], hT[:, up, a, k * P:(k + 1) * P],
                                           W2[:, bass.ds(slot * W2N + (w * (W2N // 2) + k * D), D)],
                                           start=(first and n == 0), stop=(last and n == 3 * KI - 1))
                    n += 1
            return ins

        def act_hi(act, q, p, t):
            act.wait_ge(q.tx_mm, t + 1)
            nc.scalar.activation(xT[:, p, 0, :], bank[0][:, :], ACT.Copy).then_inc(q.tx_hi, 1)

        def act_sil(act, q, up, u):
            act.wait_ge(q.hg_mm, u + 1)
            nc.scalar.activation(sil[:, up, :], bank[1 + up][:, 0:I], ACT.Silu, scale=1.0 / W_SCALE).then_inc(q.sil_ok, 1)

        def act_thi(act, q, up, u):
            act.wait_ge(q.th_mm, u + 1)
            nc.scalar.activation(hT[:, up, 0, :], bank[5][:, 0:KI * P], ACT.Copy).then_inc(q.th_hi, 1)

        def dve_lo(dve, q, p, t):
            dve.wait_ge(q.tx_hi, t + 1)
            nc.vector.tensor_tensor(xT[:, p, 1, :], bank[0][:, :], xT[:, p, 0, :], ALU.subtract).then_inc(q.tx_lo, 1)

        def dve_hid(dve, q, up, u):
            dve.wait_ge(q.sil_ok, u + 1)
            nc.vector.scalar_tensor_tensor(hid[:, up, 0:I], bank[3 + up][:, 0:I], A_SCALE / W_SCALE, sil[:, up, :],
                                           ALU.mult, ALU.mult).then_inc(q.hid_ok, 1)

        def dve_thl(dve, q, up, u):
            dve.wait_ge(q.th_hi, u + 1)
            nc.vector.tensor_tensor(hT[:, up, 1, :], bank[5][:, 0:KI * P], hT[:, up, 0, :], ALU.subtract).then_inc(q.th_lo, 1)

        def b_constants(pool, link):
            g = nc.gpsimd
            link(g.memset(LT[:, :], 1.0))
            link(g.affine_select(out=LT[:, :], in_=LT[:, :], compare_op=ALU.is_gt, fill=0.0, base=0,
                                 pattern=[[1, P]], channel_multiplier=-1))
            link(g.memset(ONES[:, :], 1.0))
            link(g.iota(IOTAI, pattern=[[1, P]], base=0, channel_multiplier=0))
            link(g.iota(TOKI, pattern=[[P, TT]], base=0, channel_multiplier=1))
            link(g.tensor_copy(IOTA[:, :], IOTAI))
            link(g.tensor_copy(TOK[:, :], TOKI))
            pads(link, range(4))
            g.nop().then_inc(const_ok, 1)

        def pads(link, slots):
            for s in slots:
                for lo in range(2):
                    at = s * W2N + lo * (W2N // 2) + (KI - 1) * D
                    link(nc.gpsimd.memset(W2[I_LAST:P, at:at + D], 0.0))

        def b_sync(sp):
            sp.wait_ge(x1_ok, TT)
            sp.dma_start(gatew, gate_w).then_inc(gatew_in, 16)
            with sp.Fori(0, TT // 2) as j:
                for p in range(2):
                    sp.wait_ge(SH.x_ok, j * 2 + (p + 1))
                    sp.dma_start(xn_dram[bass.ds(j * (2 * P) + p * P, P), :], xn[:, p, :]).then_inc(xn_st[p], 16)
            for i in range(3):
                load_slot(sp, 7 + i, expert_src(5 + i))
            for p in range(2):
                sp.nop().then_inc(yst[p], 16)
            with sp.Fori(0, SLOTS // 2) as j:
                for p in range(2):
                    sp.wait_ge(MO.y_out, j * 2 + (p + 2))
                    sp.dma_start(y_dram[bass.ds(j * (2 * P) + p * P, P), :], yo[:, p, :]).then_inc(yst[p], 16)

        def b_gpsimd(pool):
            pool.wait_ge(idx_ok, 1)

            def fetch(j, p, first):
                if not first:
                    pool.wait_ge(MO.tx_mm, j * 2 + (p - 1))
                    pool.wait_ge(gath[p], j * 16)
                nc.gpsimd.tensor_copy(idx1[:, p:p + 1], IDX[:, bass.ds(j * 2 + p, 1)]).then_inc(idx1_ok, 1)
                pool.wait_ge(idx1_ok, j * 2 + (p + 1))
                nc.gpsimd.nop(nofuse=True)
                nc.gpsimd.indirect_dma_start(xn[:, p, :], None, xn_dram,
                                             bass.IndirectOffsetOnAxis(ap=idx1[:, p:p + 1], axis=0)).then_inc(gath[p], 16)

            for p in range(2):
                pool.wait_ge(xn_st[p], 16 * (TT // 2))
            for p in range(2):
                fetch(0, p, True)
            with pool.Fori(1, SLOTS // 2) as j:
                for p in range(2):
                    fetch(j, p, False)
            pool.wait_ge(MO.y_mm, SLOTS)
            nc.gpsimd.memset(KK.rearrange("p a b c -> p (a b c)")[32:64, :].bitcast(F32), 0.0).then_inc(zeros_ok, 1)
            for p in range(2):
                pool.wait_ge(yst[p], 16 * (SLOTS // 2) + 16)
            for t in range(TT):
                if t >= len(mgath):
                    pool.wait_ge(mg_used, t - len(mgath) + 1)
                for k in range(2):
                    nc.gpsimd.indirect_dma_start(mgath[t % len(mgath)][:, k, :], None, y_dram,
                                                 bass.IndirectOffsetOnAxis(ap=POS[:, k, t:t + 1], axis=0)
                                                 ).then_inc(mg_in[t % len(mgath)], 16)

        def b_scalar(act):
            act.wait_ge(gw_mm, 1)
            nc.scalar.activation(gwT[:, 0, :], bank[7][:, 0:KD * E], ACT.Copy, scale=W_SCALE).then_inc(gw_hi, 1)
            act_hi(act, SH, 0, 0)

            def tile(j, p, first, last=False):
                for h in range(2):
                    u = j * 4 + (2 * p + h)
                    if not (first and p == 0 and h == 0):
                        act_thi(act, SH, 1 - h, u - 1)
                    act_sil(act, SH, h, u)
                    if h == 0:
                        act_hi(act, SH, 1 - p, j * 2 + (p + 1))
                    if last:
                        fast_hi(act, 7, 5, (2 * h, 2 * h + 1))

            for p in range(2):
                tile(0, p, True)
            with act.Fori(1, TT // 2 - 1) as j:
                for p in range(2):
                    tile(j, p, False)
            j = TT // 2 - 1
            tile(j, 0, False, True)
            act_thi(act, SH, 1, 2 * TT - 3)
            act_sil(act, SH, 0, 2 * TT - 2)
            fast_hi(act, 7, 5, (4, 5))
            act_thi(act, SH, 0, 2 * TT - 2)
            act_sil(act, SH, 1, 2 * TT - 1)
            fast_hi(act, 7, 5, (6,))
            act_thi(act, SH, 1, 2 * TT - 1)
            act.wait_ge(SH.y_mm, TT)
            fast_hi(act, 8, E - 2, range(NBUF))
            nc.scalar.nop().then_inc(MO.y_out, 1)
            act.wait_ge(d12_ok, 1)
            nc.scalar.activation(CW[:, :, 1], CW[:, :, 0], ACT.Exp).then_inc(e12_ok, 1)
            fast_hi(act, 8, E - 2, range(NBUF, NCH))
            fast_hi(act, 9, E - 1, range(NCH))
            act_hi(act, MO, 0, 0)

            def slot(j, p, first, last):
                i = j * 2 + p
                if not (first and p == 0):
                    act_thi(act, MO, 1 - p, i - 1)
                act_sil(act, MO, p, i)
                if not (last and p == 1):
                    act_hi(act, MO, 1 - p, i + 1)
                if not (first and p == 0):
                    y_out(i - 1, 1 - p, first)

            def y_out(i, p, first):
                act.wait_ge(MO.y_mm, i + 1)
                if not first:
                    act.wait_ge(yst[p], (i - p) * 8 + 16)
                nc.scalar.activation(yo[:, p, :], bank[6 + p][:, :], ACT.Copy).then_inc(MO.y_out, 1)

            for p in range(2):
                slot(0, p, True, False)
            with act.Fori(1, SLOTS // 2 - 1) as j:
                for p in range(2):
                    slot(j, p, False, False)
            for p in range(2):
                slot(SLOTS // 2 - 1, p, False, True)
            act_thi(act, MO, 1, SLOTS - 1)
            y_out(SLOTS - 1, 1, False)

        def b_tensor(pe):
            pe.wait_ge(x1_ok, TT)
            pe.wait_ge(gatew_in, 16)
            for k in range(KD):
                ins = nc.tensor.transpose(bank[7][:, k * E:(k + 1) * E], gatew[:, k * P:(k + 1) * P], ident[0:E, 0:E])
            ins.then_inc(gw_mm, 1)
            pe.wait_ge(gw_ok, 1)
            pe.wait_ge(const_ok, 1)
            pe.wait_ge(split_l, 7 * NCH + 1)
            pe.wait_ge(pad_ok, 1)
            pe.wait_ge(SH.x_ok, 1)
            pe_tx(SH, 0, 0)

            def finish(j, u, h, t):
                pe.wait_ge(SH.th_lo, u + 1)
                if h == 0:
                    pe.wait_ge(SH.y_out, t)
                ins = pe_y(SH, h, E - 2 + h, bank[6], h == 0, h == 1)
                if h == 1:
                    ins.then_inc(SH.y_mm, 1)

            def tile(j, p, first, last):
                for h in range(2):
                    u = j * 4 + (2 * p + h)
                    t = j * 2 + p
                    before = not (first and p == 0 and h == 0)
                    if before:
                        pe.wait_ge(SH.hid_ok, u)
                        pe_th(SH, 1 - h)
                    pe.wait_ge(SH.tx_lo, t + 1)
                    pe_hg(pe, SH, p, h, E - 2 + h)
                    if h == 0:
                        pe.wait_ge(lg_sb, t)
                        n = 0
                        for k in range(KD):
                            for a in range(2):
                                for w in range(2):
                                    ins = nc.tensor.matmul(bank[7][:, 0:E], xT[:, p, a, k * P:(k + 1) * P],
                                                           gwT[:, w, k * E:(k + 1) * E], start=(n == 0), stop=(n == 4 * KD - 1))
                                    n += 1
                        ins.then_inc(lg_mm, 1)
                        if not (last and p == 1):
                            pe.wait_ge(SH.x_ok, t + 2)
                            pe_tx(SH, 1 - p, t + 1)
                    if before:
                        finish(j, u - 1, 1 - h, t - 1 if h == 0 else t)

            for p in range(2):
                tile(0, p, True, False)
            with pe.Fori(1, TT // 2 - 1) as j:
                for p in range(2):
                    tile(j, p, False, False)
            for p in range(2):
                tile(TT // 2 - 1, p, False, True)
            pe.wait_ge(SH.hid_ok, 2 * TT)
            pe_th(SH, 1)
            finish(0, 2 * TT - 1, 1, TT - 1)

            pe.wait_ge(sel_ok, 1)
            nc.tensor.matmul(bank[0][:, 0:TT * E], LT[:, :], SEL.rearrange("p a b -> p (a b)"), start=True, stop=True)
            for d in range(1, TT):
                nc.tensor.matmul(bank[0][:, d * E:TT * E], ONES[:, :],
                                 SEL[:, 0:TT - d, :].rearrange("p a b -> p (a b)"), start=False, stop=True,
                                 skip_group_check=True)
            for t in range(TT):
                ins = nc.tensor.matmul(bank[1][:, 0:E], ONES[:, :], SEL[:, t, :], start=(t == 0), stop=(t == TT - 1))
            ins.then_inc(rank_mm, 1)
            pe.wait_ge(hot_ok, 1)
            for i in range(E2 * TT):
                ins = nc.tensor.matmul(bank[2][:, 0:SLOTS], row_hot[:, i, :], tile_hot[:, i, :],
                                       start=(i == 0), stop=(i == E2 * TT - 1))
            ins.then_inc(map_mm, 1)
            pe.wait_ge(idx_ok, 1)
            pe.wait_ge(eid_ok, 1)
            pe.wait_ge(split_l, (E + 2) * NCH + 1)
            pe.wait_ge(gath[0], 16)
            pe_tx(MO, 0, 0)

            def mfinish(i, p, slot, first):
                pe.wait_ge(MO.th_lo, i + 1)
                if not first:
                    pe.wait_ge(MO.y_out, i)
                pe_y(MO, p, slot, bank[6 + p], True, True).then_inc(MO.y_mm, 1)

            def eid(i):
                return pe.value_load(EID[0:1, bass.ds(i, 1)], min_val=0, max_val=E - 1)

            def slot(j, p, first, last):
                i = j * 2 + p
                if not (first and p == 0):
                    pe.wait_ge(MO.hid_ok, i)
                    pe_th(MO, 1 - p)
                pe.wait_ge(MO.tx_lo, i + 1)
                pe_hg(pe, MO, p, p, eid(i))
                if not (last and p == 1):
                    pe.wait_ge(gath[1 - p], j * 16 + 16 * (1 + p))
                    pe_tx(MO, 1 - p, i + 1)
                if not (first and p == 0):
                    mfinish(i - 1, 1 - p, eid(i - 1), first)

            for p in range(2):
                slot(0, p, True, False)
            with pe.Fori(1, SLOTS // 2 - 1) as j:
                for p in range(2):
                    slot(j, p, False, False)
            for p in range(2):
                slot(SLOTS // 2 - 1, p, False, True)
            pe.wait_ge(MO.hid_ok, SLOTS)
            pe_th(MO, 1)
            mfinish(SLOTS - 1, 1, eid(SLOTS - 1), False)

        def b_vector(dve):
            link = Chain(dve, dve_chain)
            link.restart()
            v = nc.vector
            dve.wait_ge(x1_ok, TT)
            dve.wait_ge(const_ok, 1)
            for p in range(2):
                link(v.memset(hid[:, p, I:KI * P], 0.0))
            link(v.tensor_scalar(GATES[:, 7:8], GATES[:, 2:3], 1.0 / (W_SCALE * A_SCALE), None, ALU.mult))
            row_moments(link, 0, bnst)
            rsqrt(link, MV[:, 0:R, 1], RSTD[:, 0:R], R)
            dve.wait_ge(gw_hi, 1)
            v.scalar_tensor_tensor(gwT[:, 1, :], bank[7][:, 0:KD * E], W_SCALE, gwT[:, 0, :], ALU.mult,
                                   ALU.subtract).then_inc(gw_ok, 1)

            def norm(t, p, first):
                if not first:
                    dve.wait_ge(xn_st[p], (t - p) * 8)
                v.tensor_scalar(xn[:, p, :], X[:, t, :], MV[:, bass.ds(t, 1), 0], RSTD[:, bass.ds(t, 1)],
                                ALU.subtract, ALU.mult).then_inc(SH.x_ok, 1)

            norm(0, 0, True)
            norm(1, 1, True)
            dve_lo(dve, SH, 0, 0)

            def y_in(t):
                dve.wait_ge(SH.y_mm, t + 1)
                v.scalar_tensor_tensor(X[:, t, :], bank[6][:, :], GATES[:, 7:8], X[:, t, :], ALU.mult,
                                       ALU.add).then_inc(SH.y_out, 1)

            def tile(j, p, first, last):
                t = j * 2 + p
                for h in range(2):
                    u = j * 4 + (2 * p + h)
                    before = not (first and p == 0 and h == 0)
                    if before:
                        dve_thl(dve, SH, 1 - h, u - 1)
                    dve_hid(dve, SH, h, u)
                    if h == 0:
                        dve.wait_ge(lg_mm, t + 1)
                        v.tensor_scalar(LG[:, t, :], bank[7][:, 0:E], 1.0 / W_SCALE, None, ALU.mult).then_inc(lg_sb, 1)
                        if not (last and p == 1):
                            dve_lo(dve, SH, 1 - p, t + 1)
                        if not last:
                            norm(t + 2, p, False)
                        if before:
                            y_in(t - 1)
                    if first and 2 * p + h < B - 1:
                        row_moments(link, 2 * p + h + 1, bnst)
                    elif first:
                        rsqrt(link, MV[:, R:TT, 1], RSTD[:, R:TT], TT - R)
                    if last:
                        n = 2 * (2 * p + h)
                        fast_lo(dve, 7, 5, range(n, min(n + 2, NCH)))

            for p in range(2):
                tile(0, p, True, False)
            with dve.Fori(1, TT // 2 - 1) as j:
                for p in range(2):
                    tile(j, p, False, False)
            for p in range(2):
                tile(TT // 2 - 1, p, False, True)
            dve_thl(dve, SH, 1, 2 * TT - 1)
            y_in(TT - 1)

            link.restart()
            dve.wait_ge(lg_sb, TT)
            for t in range(TT):
                v.max(MX[:, t, :], LG[:, t, :]).then_inc(dve_chain, 1)
            dve.wait_ge(dve_chain, TT)
            for t in range(TT):
                v.max_index(MI[:, t, :], MX[:, t, :], LG[:, t, :]).then_inc(dve_chain, 1)
            dve.wait_ge(dve_chain, 2 * TT)
            link.n = 2 * TT
            link(v.tensor_copy(MIF, MI))
            for k in range(2):
                link(v.tensor_tensor(OH[:, k, :, :], MIF[:, :, k:k + 1].to_broadcast([P, TT, E]),
                                     IOTA[:, 0:E].unsqueeze(1).to_broadcast([P, TT, E]), ALU.is_equal))
            v.tensor_tensor(SEL, OH[:, 0, :, :], OH[:, 1, :, :], ALU.add).then_inc(sel_ok, 1)
            v.tensor_tensor(CW[:, :, 0], MX[:, :, 1], MX[:, :, 0], ALU.subtract).then_inc(d12_ok, 1)
            fast_lo(dve, 8, E - 2, range(NBUF))
            dve.wait_ge(rank_mm, 1)
            link(v.tensor_scalar(CNT, bank[1][:, 0:E], 1.0 / P, (P - 1.0) / P - 0.5 + 0.5 / P, ALU.mult, ALU.add))
            link(v.tensor_scalar(CNT, CNT, ROUND, ROUND, ALU.add, ALU.subtract))
            link(v.memset(OFF, 0.0))
            for e in range(E):
                link(v.tensor_tensor(OFF[:, e + 1:e + 2], OFF[:, e:e + 1], CNT[:, e:e + 1], ALU.add))
            link(v.scalar_tensor_tensor(T1, OFF[:, 0:E].unsqueeze(1).to_broadcast([P, TT, E]), float(P),
                                        bank[0][:, 0:TT * E].rearrange("p (a b) -> p a b", b=E), ALU.mult, ALU.add))
            for k in range(2):
                link(v.tensor_tensor(T2, T1, OH[:, k, :, :], ALU.mult))
                link(v.tensor_reduce(POSF[:, k, :], T2, AX_X, ALU.add))
            link(v.tensor_scalar(TILE, POSF, -(P - 1) / 2.0, 1.0 / P, ALU.add, ALU.mult))
            link(v.tensor_scalar(TILE, TILE, ROUND, ROUND, ALU.add, ALU.subtract))
            link(v.scalar_tensor_tensor(ROW, TILE, -float(P), POSF, ALU.mult, ALU.add))
            link(v.tensor_tensor(row_hot, IOTA[:, :].unsqueeze(1).to_broadcast([P, E2 * TT, P]),
                                 ROW.rearrange("p a b -> p (a b)").unsqueeze(2).to_broadcast([P, E2 * TT, P]),
                                 ALU.is_equal))
            fast_lo(dve, 8, E - 2, range(NBUF, 2 * NBUF))
            link(v.tensor_tensor(tile_hot, IOTA[:, 0:SLOTS].unsqueeze(1).to_broadcast([P, E2 * TT, SLOTS]),
                                 TILE.rearrange("p a b -> p (a b)").unsqueeze(2).to_broadcast([P, E2 * TT, SLOTS]),
                                 ALU.is_equal))
            for k in range(2):
                half = tile_hot[:, k * TT:(k + 1) * TT, :]
                link(v.tensor_tensor(half, half, TOK[:, :].unsqueeze(2).to_broadcast([P, TT, SLOTS]), ALU.mult))
            v.nop().then_inc(hot_ok, 1)
            v.tensor_copy(POS, POSF).then_inc(pos_ok, 1)
            fast_lo(dve, 8, E - 2, range(2 * NBUF, NCH))
            link(v.tensor_tensor(EQ, OFF[:, 1:E + 1].unsqueeze(1).to_broadcast([P, SLOTS, E]),
                                 IOTA[:, 0:SLOTS].unsqueeze(2).to_broadcast([P, SLOTS, E]), ALU.is_le))
            link(v.tensor_reduce(EIDF, EQ, AX_X, ALU.add))
            link(v.tensor_scalar(EIDF, EIDF, float(E - 1), None, ALU.min))
            v.tensor_copy(EID, EIDF).then_inc(eid_ok, 1)
            dve.wait_ge(eid_ok, 1)
            dve.wait_ge(map_mm, 1)
            v.tensor_copy(IDX, bank[2][:, 0:SLOTS]).then_inc(idx_ok, 1)
            fast_lo(dve, 9, E - 1, range(2))
            for p in range(2):
                link(v.memset(hid[:, p, I:KI * P], 0.0))
            dve.wait_ge(e12_ok, 1)
            link(v.tensor_scalar(CW[:, :, 0], CW[:, :, 1], 1.0, None, ALU.add))
            link(v.reciprocal(CW[:, :, 0], CW[:, :, 0]))
            link(v.tensor_tensor(CW[:, :, 1], CW[:, :, 1], CW[:, :, 0], ALU.mult))
            link(v.tensor_scalar(CW, CW, GATES[:, 7:8], None, ALU.mult))
            fast_lo(dve, 9, E - 1, range(2, NCH))
            dve_lo(dve, MO, 0, 0)

            def slot(j, p, first, last):
                i = j * 2 + p
                if not (first and p == 0):
                    dve_thl(dve, MO, 1 - p, i - 1)
                dve_hid(dve, MO, p, i)
                if not (last and p == 1):
                    dve_lo(dve, MO, 1 - p, i + 1)

            for p in range(2):
                slot(0, p, True, False)
            with dve.Fori(1, SLOTS // 2 - 1) as j:
                for p in range(2):
                    slot(j, p, False, False)
            for p in range(2):
                slot(SLOTS // 2 - 1, p, False, True)
            dve_thl(dve, MO, 1, SLOTS - 1)

        HD = 16
        H = D // HD
        G = C // HD
        HG = H // G
        NQ = H * S
        QS = BIG[:, 0:NQ // 2].bitcast(F16).rearrange("p (h s) -> p h s", s=S)
        KK = carve(BIG, "KK", 32768, [P, G, 2, S], F16)
        KS, KA = KK[:, :, 0, :], KK[:, :, 1, :]
        PB = carve(BIG, "PB", 49152, [P, 2, 2 * HG, S])
        V = carve(BIG, "V", 81920, [P, R, G, 32])
        qhT = carve(BIG, "qhT", 86016, [P, 2, KD, S], F16)
        khT = carve(BIG, "khT", 94208, [P, 2, S], F16)
        OS = carve(BIG, "OS", 96256, [P, 2, S])
        CT = carve(WORK, "CT", 0, [P, R, C])
        QN = carve(WORK, "QN", 2048, [P, 2, D])
        MXU = carve(WORK, "MXU", 6144, [P, 2, HG * R])
        MT = carve(WORK, "MT", 6400, [HG * R, 2, P], F16)
        RDEN = carve(WORK, "RDEN", 7168, [P, 2, R * HG])
        OO = carve(WORK, "OO", 7424, [P, 2, R * HG, HD])
        bnst_c = carve(WORK, "bnst_c", 9472, [P, TT, 6])
        mvs = carve(WORK, "mvs", 9856, [P, R, 2])
        SOFT_SCALE = 1.0 / float(HD) ** 0.5
        ABANK, TBANK, OBANK = [bank[0], bank[1]], bank[2], bank[3]
        BPAIR = [PS[:, 4:6, :], PS[:, 6:8, :]]
        NPREP = G + R + 1 + G

        ct_in = sem("ct_in")
        cpad_ok = sem("cpad_ok")
        zeros_ok = sem("zeros_ok")
        row_st = sem("row_st")
        row_mv = sem("row_mv")
        mvs_ok = sem("mvs_ok")
        v_ok = sem("v_ok")
        qn_ok = sem("qn_ok")
        t_mm = sem("t_mm")
        t_hi = sem("t_hi")
        t_free = sem("t_free")
        qk_in = [sem(f"qk_in{g}") for g in range(G)]
        a_mm = sem("a_mm")
        max_ok = sem("max_ok")
        mt_ok = sem("mt_ok")
        m_in = [sem(f"m_in{i}") for i in range(2)]
        b_mm = sem("b_mm")
        exp_ok = sem("exp_ok")
        pv_mm = sem("pv_mm")
        o_sb = sem("o_sb")
        o_ok = sem("o_ok")
        x3_ok = sem("x3_ok")
        HALF = 2

        TUSES = []
        for g_ in range(G):
            TUSES.append(("m", g_))
            TUSES.append(("o", g_ - 1))
            if g_ == 1:
                TUSES.append(("ctx", 0))
            if 1 <= g_ <= R:
                TUSES.append(("q", g_ - 1))
        assert len(TUSES) == NPREP
        TLAST = [k for k in TUSES if k[0] == "o" or (k[0] == "m" and k[1] < G - 1)] + [("o", G - 1)]
        TFIRST = [("ctx", 0)] + [("q", r_) for r_ in range(R)] + [("m", -1)]

        def tuse(b, kind, i):
            if b is None:
                return TFIRST.index((kind, i))
            if isinstance(b, int) and b == B - 1:
                return len(TFIRST) + b * NPREP + (TLAST.index((kind, i)) - 1)
            if isinstance(b, int) and b == 0 and (kind, i) == ("m", 0):
                return len(TFIRST)
            return len(TFIRST) + b * NPREP + (TUSES.index((kind, i)) - 1)

        def c_sync(sp):
            sp.wait_ge(MO.y_mm, SLOTS)

            def load_ctx(b):
                sp.dma_start(CT, ctx_rows[:, bass.ds(b * R, R), :]).then_inc(ct_in, 16)

            def stack_group(b, g):
                for n, (a, w) in enumerate(((0, 0), (0, 1), (1, 0))):
                    rows = slice(n * HD, (n + 1) * HD)
                    sp.dma_start(QS[rows, g * HG:(g + 1) * HG, :], qhT[g * HD:(g + 1) * HD, a, :, :]).then_inc(qk_in[g], 16)
                    sp.dma_start(KK[rows, g, :, :], khT[g * HD:(g + 1) * HD, w, :].unsqueeze(1).to_broadcast([HD, 2, S])
                                 ).then_inc(qk_in[g], 16)

            def maxima(u, g, i):
                sp.wait_ge(mt_ok, u + 1)
                sp.dma_start(QS[64:65, g * HG:(g + 1) * HG, :].rearrange("o h (r s) -> o (h r) s", r=R),
                             MT[:, i, :]).then_inc(m_in[i], 16)

            def batch(b, last):
                if not last:
                    sp.wait_ge(v_ok, b * G + G)
                    load_ctx(b + 1)
                for g in range(G):
                    u = b * G + g
                    if not (last and g == G - 1):
                        maxima(u + 1, (g + 1) % G, (g + 1) % 2)
                    if last and g in (2, 4, 6):
                        sp.wait_ge(b_mm, u * 2 * HG)
                    if last and g in (2, 4, 6):
                        load_weights(UW, 1, g // 2 - 1, uw_in)
                    if last or g < 5:
                        continue
                    if g == 5:
                        sp.wait_ge(t_free, tuse(b, "q", R - 1) + 1)
                    for gg in {5: (0, 1, 2, 3), 6: (4, 5), 7: (6,)}[g]:
                        sp.wait_ge(b_mm, (b * G + gg + 1) * 2 * HG)
                        stack_group(b + 1, gg)
                if not last:
                    sp.wait_ge(b_mm, (b * G + G) * 2 * HG)
                    stack_group(b + 1, G - 1)

            def load_weights(dst, m, j, loaded):
                sp.dma_start(dst[:, j, :, :, :], wdq_dram[m * FCH + j, :, :].rearrange(
                    "p (l k f) -> p l k f", l=2, k=KD)).then_inc(loaded, 16)

            load_ctx(0)
            sp.wait_ge(cpad_ok, 1)
            sp.wait_ge(t_free, tuse(None, "q", R - 1) + 1)
            for g in range(G):
                stack_group(0, g)
            maxima(0, 0, 0)
            for j in range(FCH):
                load_weights(GW, 0, j, gw_in)
            batch(0, False)
            with sp.Fori(1, B - 1) as b:
                batch(b, False)
            batch(B - 1, True)
            sp.wait_ge(b_mm, B * G * 2 * HG)
            load_weights(UW, 1, FCH - 1, uw_in)
            sp.wait_ge(pv_mm, B * G * 2)
            for j in range(FCH):
                load_weights(DW, 2, j, dw_in)

        def c_gpsimd(pool):
            pool.wait_ge(MO.y_mm, SLOTS)
            nc.gpsimd.memset(V.rearrange("p a b c -> p (a b c)"), 1.0).then_inc(v_ones, 1)
            pool.wait_ge(v_ones, 1)

            def values(b, g):
                nc.gpsimd.nop(nofuse=True)
                nc.gpsimd.tensor_copy(V[:, :, g, 0:HD], CT[:, :, g * HD:(g + 1) * HD]).then_inc(v_ok, 1)

            pool.wait_ge(ct_in, 16)
            for g in range(G):
                values(0, g)
            with pool.Fori(0, B - 1) as b:
                pool.wait_ge(ct_in, b * 16 + 32)
                for g in range(G):
                    pool.wait_ge(pv_mm, (b * G + g + 1) * 2)
                    values(b + 1, g)

        def c_scalar(act):
            def hi(b, kind, i, dst, src):
                act.wait_ge(t_mm, tuse(b, kind, i) + 1)
                nc.scalar.activation(dst, src, ACT.Copy).then_inc(t_hi, 1)

            def hi_q(b, r):
                hi(b, "q", r, qhT[:, 0, :, r * P:(r + 1) * P], TBANK.rearrange("p (k s) -> p k s", k=KD))

            def hi_ctx(b):
                hi(b, "ctx", 0, khT[:, 0, :], TBANK)

            def maxima(b, g, i):
                act.wait_ge(t_mm, tuse(b, "m", g) + 1)
                nc.scalar.activation(MT[:, i, :], TBANK[0:HG * R, 0:P], ACT.Copy).then_inc(t_free, 1)
                act.wait_ge(t_free, tuse(b, "m", g) + 1)
                nc.scalar.nop().then_inc(mt_ok, 1)

            def out_copy(b, g):
                act.wait_ge(pv_mm, b * (2 * G) + (2 * g + 2))
                nc.scalar.activation(OS[:, g % 2, :], OBANK, ACT.Copy).then_inc(o_sb, 1)

            def batch(b, first, last):
                for g in range(G):
                    for tp in range(2):
                        n = (b * G + g) * 2 + tp
                        for h in range(HG):
                            act.wait_ge(b_mm, n * HG + (h + 1))
                            nc.scalar.activation(PB[:, tp, 2 * h:2 * h + 2, :], BPAIR[h % 2], ACT.Exp,
                                                 scale=SOFT_SCALE).then_inc(exp_ok, 1)
                            if tp == 0 and h == 3 and not (last and g == G - 1):
                                maxima(b, g, (g + 1) % 2)
                            if tp == 1 and h == 0 and not (first and g == 0):
                                out_copy(b, g - 1)
                            if last and g == G - 1 and (tp, h) == (1, 1):
                                x_up(act, 0, 0)
                            if tp == 1 and h == 3 and not last:
                                if g == 1:
                                    hi_ctx(b)
                                if 1 <= g <= R:
                                    hi_q(b, g - 1)
                if last:
                    out_copy(b, G - 1)

            act.wait_ge(MO.y_mm, SLOTS)
            for a in (QS.rearrange("p a b -> p (a b)"), KK.rearrange("p a b c -> p (a b c)")):
                z = a[64:128, :].bitcast(F32)
                n = z.shape[1]
                nc.scalar.activation(z, ident[64:128, 0:1].to_broadcast([64, n]), ACT.Copy, scale=0.0).then_inc(zeros_ok, 1)
            nc.scalar.nop().then_inc(exp_ok, 2)
            nc.scalar.nop().then_inc(o_sb, 1)
            hi_ctx(None)
            for r in range(R):
                hi_q(None, r)
            maxima(None, -1, 0)
            batch(0, True, False)
            with act.Fori(1, B - 1) as b:
                batch(b, False, False)
            batch(B - 1, False, True)

        def c_tensor(pe):
            def t_wait(b, kind, i):
                pe.wait_ge(t_free, tuse(b, kind, i))

            def t_ctx(b, nb):
                pe.wait_ge(ct_in, nb * 16 + 16)
                t_wait(b, "ctx", 0)
                for r in range(R):
                    ins = nc.tensor.transpose(TBANK[:, r * P:(r + 1) * P], CT[:, r, :], ident[:, :])
                ins.then_inc(t_mm, 1)

            def t_q(b, nb, r):
                pe.wait_ge(qn_ok, nb * R + (r + 1))
                t_wait(b, "q", r)
                for k in range(HG):
                    ins = nc.tensor.transpose(TBANK[:, k * P:(k + 1) * P], QN[:, r % 2, k * P:(k + 1) * P], ident[:, :])
                ins.then_inc(t_mm, 1)

            def t_max(b, g, u, i):
                pe.wait_ge(max_ok, (u + 1) * HG * R)
                t_wait(b, "m", g)
                nc.tensor.transpose(TBANK[0:HG * R, 0:P], MXU[:, i, :], ident[:, :]).then_inc(t_mm, 1)

            def t_out(b, g):
                pe.wait_ge(o_sb, b * G + (g + 2))
                t_wait(b, "o", g)
                for r in range(R):
                    ins = nc.tensor.transpose(TBANK[:, r * P:(r + 1) * P], OS[:, g % 2, r * P:(r + 1) * P], ident[:, :])
                ins.then_inc(t_mm, 1)

            def a_slot(u, g, tp, h, first, reuse, which=(0, 1)):
                if tp == 0 and h == 0 and 0 in which:
                    first()
                for i in which:
                    n = u * HG * R + (tp * 2 * HG + 2 * h + i)
                    if reuse or tp or h:
                        pe.wait_ge(max_ok, n - 1)
                    r = 2 * tp + i
                    nc.tensor.matmul(ABANK[i], QS[:, g * HG + h, r * P:(r + 1) * P], KA[:, g, :],
                                     start=True, stop=True).then_inc(a_mm, 1)

            def b_slot(n, g, tp, h, first):
                if not first:
                    pe.wait_ge(exp_ok, n * HG + (h + 1))
                for j in range(HALF):
                    t = HALF * tp + j
                    ins = nc.tensor.matmul(BPAIR[h % 2][:, j, :], KS[:, g, t * P:(t + 1) * P],
                                           QS[:, g * HG + h, :], start=True, stop=True)
                ins.then_inc(b_mm, 1)

            def pv(n, u, g, tp, j):
                pe.wait_ge(exp_ok, (n + 1) * HG + 2)
                t = HALF * tp + j
                if t == 0:
                    pe.wait_ge(o_sb, u + 1)
                    pe.wait_ge(v_ok, u + 1)
                for h in range(HG):
                    ins = nc.tensor.matmul(OBANK[32 * h:32 * h + 32, :], V[:, t, g, :], PB[:, tp, 2 * h + j, :],
                                           start=(t == 0), stop=(t == R - 1))
                if j == HALF - 1:
                    ins.then_inc(pv_mm, 1)

            def batch(b, first, last):
                for g in range(G):
                    u = b * G + g
                    for tp in range(2):
                        n = u * 2 + tp
                        if tp == 0:
                            pe.wait_ge(m_in[g % 2], (u - g % 2) * 8 + 16)
                        ahead = not (last and g >= G - 2)
                        for h in range(HG):
                            if ahead:
                                a_slot(u + 2, (g + 2) % G, tp, h,
                                       lambda: pe.wait_ge(qk_in[(g + 2) % G], (b if g < G - 2 else b + 1) * (16 * 6) + 16 * 6), True, (0,))
                            b_slot(n, g, tp, h, False)
                            if ahead:
                                a_slot(u + 2, (g + 2) % G, tp, h,
                                       lambda: pe.wait_ge(qk_in[(g + 2) % G], (b if g < G - 2 else b + 1) * (16 * 6) + 16 * 6), True, (1,))
                            if h % 2:
                                j = h // 2
                                if tp == 1:
                                    pv(n - 1, u, g, 0, j)
                                elif not (first and g == 0):
                                    pv(n - 1, u - 1, (g - 1) % G, 1, j)
                            if tp == 0 and h == 3 and not (last and g == G - 1):
                                t_max(b, g, u + 1, (g + 1) % 2)
                            if tp == 1 and h == 2 and not (first and g == 0):
                                t_out(b, g - 1)
                            if tp == 1 and h == 3 and not last:
                                if g == 1:
                                    t_ctx(b, b + 1)
                                if 1 <= g <= R:
                                    t_q(b, b + 1, g - 1)
                if last:
                    for j in range(HALF):
                        pv(b * (G * 2) + (2 * G - 1), b * G + (G - 1), G - 1, 1, j)
                    t_out(b, G - 1)

            pe.wait_ge(MO.y_out, SLOTS + 1)
            t_ctx(None, 0)
            for r in range(R):
                t_q(None, 0, r)
            for u in range(2):
                for tp in range(2):
                    for h in range(HG):
                        a_slot(u, u, tp, h, lambda: pe.wait_ge(qk_in[u], 16 * 6), u > 0)
                if u == 0:
                    t_max(None, -1, 0, 0)
            pe.wait_ge(cpad_ok, 2)
            batch(0, True, False)
            with pe.Fori(1, B - 1) as b:
                batch(b, False, False)
            batch(B - 1, False, True)

        def c_vector(dve):
            link = Chain(dve, dve_chain)
            link.restart()
            v = nc.vector
            dve.wait_ge(MO.y_mm, SLOTS)
            link(v.memset(QS.rearrange("p a b -> p (a b)")[32:64, :].bitcast(F32), 0.0))

            def combine(t):
                dve.wait_ge(mg_in[t % len(mgath)], 32 * (t // len(mgath) + 1))
                for k in range(2):
                    ins = v.scalar_tensor_tensor(X[:, t, :], mgath[t % len(mgath)][:, k, :], CW[:, t, k:k + 1], X[:, t, :],
                                                 ALU.mult, ALU.add)
                    if k == 0:
                        link(ins)
                    else:
                        ins.then_inc(mg_used, 1)
                dve.wait_ge(mg_used, t + 1)
                v.bn_stats(bnst_c[:, t, :], X[:, t, :]).then_inc(row_st, 1)

            def moments(a, b):
                dve.wait_ge(row_st, b)
                for t in range(a, b):
                    ins = v.bn_aggr(MV[:, t, :], bnst_c[:, t, :])
                    if t == b - 1:
                        link(ins)
                    else:
                        ins.then_inc(dve_chain, 1)
                        link.n += 1
                rsqrt(link, MV[:, a:b, 1], RSTD[:, a:b], b - a)

            for t in range(R):
                combine(t)
            dve.wait_ge(zeros_ok, 3)
            v.nop().then_inc(cpad_ok, 1)
            moments(0, R)

            def norm(b, r):
                t = b * R + r
                v.tensor_scalar(QN[:, r % 2, :].rearrange("p (k g d) -> p k g d", k=HG, d=HD),
                                X[:, t, :].rearrange("p (g k d) -> p k g d", k=HG, d=HD),
                                MV[:, bass.ds(t, 1), 0], RSTD[:, bass.ds(t, 1)],
                                ALU.subtract, ALU.mult).then_inc(qn_ok, 1)

            def lo(b, kind, i, dst, src, hi):
                dve.wait_ge(t_hi, lo_n(b, kind, i))
                v.tensor_tensor(dst, src, hi, ALU.subtract).then_inc(t_free, 1)

            def lo_n(b, kind, i):
                seq = [k for k in TUSES if k[0] in ("ctx", "q")]
                if b is None:
                    return [k for k in TFIRST if k[0] in ("ctx", "q")].index((kind, i)) + 1
                return b * len(seq) + (len(seq) + seq.index((kind, i)) + 1)

            def lo_q(b, r):
                lo(b, "q", r, qhT[:, 1, :, r * P:(r + 1) * P], TBANK.rearrange("p (k s) -> p k s", k=KD),
                   qhT[:, 0, :, r * P:(r + 1) * P])

            def lo_ctx(b):
                lo(b, "ctx", 0, khT[:, 1, :], TBANK, khT[:, 0, :])

            def max_slot(u, g, tp, h):
                for i in range(2):
                    n = u * HG * R + (tp * 2 * HG + 2 * h + i)
                    dve.wait_ge(a_mm, n + 1)
                    c = h * R + 2 * tp + i
                    v.tensor_reduce(MXU[:, g % 2, c:c + 1], ABANK[i], AX_X, ALU.max, negate=True).then_inc(max_ok, 1)

            def out_add(b, g):
                i = g % 2
                dve.wait_ge(t_mm, tuse(b, "o", g) + 1)
                o = TBANK.rearrange("p (n c) -> p n c", c=32)
                v.reciprocal(RDEN[:, i, :], o[:, :, HD]).then_inc(oo_ok, 1)
                dve.wait_ge(oo_ok, b * (2 * G) + (2 * g + 1))
                v.tensor_tensor(OO[:, i, :, :], o[:, :, 0:HD], RDEN[:, i, :].unsqueeze(2).to_broadcast([P, R * HG, HD]),
                                ALU.mult).then_inc(oo_ok, 1)
                dve.wait_ge(oo_ok, b * (2 * G) + (2 * g + 2))
                v.nop().then_inc(t_free, 1)
                xb, xg = (b, g) if g >= 0 else (b - 1, G - 1)
                xs = X[:, bass.ds(xb * R, R), xg * HG * HD:(xg + 1) * HG * HD]
                v.scalar_tensor_tensor(xs, OO[:, i, :, :].rearrange("p (r h) d -> p r (h d)", r=R), GATES[:, 1:2], xs,
                                       ALU.mult, ALU.add).then_inc(o_ok, 1)

            def rows_complete(b):
                dve.wait_ge(o_ok, b * G + G)
                v.nop(nofuse=True)
                for r in range(R):
                    v.bn_stats(bnst_c[:, r, :], X[:, bass.ds(b * R + r, 1), :]).then_inc(row_st, 1)
                for r in range(R):
                    dve.wait_ge(row_st, b * R + (TT + r + 1))
                    v.nop(nofuse=True)
                    v.bn_aggr(mvs[:, r, :], bnst_c[:, r, :]).then_inc(mvs_ok, 1)
                dve.wait_ge(mvs_ok, b * R + R)
                v.nop(nofuse=True)
                v.tensor_scalar(MV[:, bass.ds(b * R, R), :], mvs, 0.0, None, ALU.add).then_inc(row_mv, 1)

            def batch(b, first, last):
                for g in range(G):
                    u = b * G + g
                    for tp in range(2):
                        ahead = not (last and g >= G - 2)
                        for h in range(HG):
                            if ahead:
                                max_slot(u + 2, g, tp, h)
                            if tp == 0 and h == 1 and not last and 1 <= g <= R:
                                norm(b + 1, g - 1)
                            if tp == 1 and h == 2 and not (first and g == 0):
                                out_add(b, g - 1)
                            if tp == 1 and h == 3 and g == 0 and not first:
                                rows_complete(b - 1)
                            if last and g == G - 1 and (tp, h) == (0, 0):
                                dve.wait_ge(row_mv, B - 1)
                                rsqrt(link, MV[:, 0:TT - R, 1], RSTD[:, 0:TT - R], TT - R)
                                dve.wait_ge(v_ok, B * G)
                                x_scales(link, 0, 0)
                            if last and g == G - 1 and (tp, h) == (1, 2):
                                x_round(dve, link, 0, 0)
                            if tp == 1 and h == 3 and not last:
                                if g == 1:
                                    lo_ctx(b)
                                if 1 <= g <= R:
                                    lo_q(b, g - 1)
                if last:
                    out_add(b, G - 1)
                    rows_complete(b)

            for r in range(2):
                norm(0, r)
            combine(R)
            lo_ctx(None)
            for r in range(R):
                lo_q(None, r)
                if r < 2:
                    norm(0, r + 2)
                if r < 3:
                    combine(R + 1 + r)
            v.memset(KS[64:65, :, :], 1.0).then_inc(cpad_ok, 1)
            t = 2 * R
            combine(t)
            t += 1
            for u in range(2):
                for tp in range(2):
                    for h in range(HG):
                        max_slot(u, u, tp, h)
                        if h % 2 == 0 and t < TT:
                            combine(t)
                            t += 1
            moments(R, TT)
            batch(0, True, False)
            with dve.Fori(1, B - 1) as b:
                batch(b, False, False)
            batch(B - 1, False, True)
            dve.wait_ge(o_ok, B * G)
            v.nop().then_inc(x3_ok, 1)

        v_ones = sem("v_ones")
        oo_ok = sem("oo_ok")

        F = fgate_w.shape[0]
        QB = 32
        NB = D // QB
        FT = F // P
        FCH = F // D
        TINY = 1e-30
        LEAST = 1.5 * 2.0 ** 14
        FSCALE = 1.0 / (W_SCALE * A_SCALE)
        NGRP = 4
        GW = carve(BIG, "GW", 106496, [P, FCH, 2, KD * D], F16)
        UW = carve(BIG, "UW", 0, [P, FCH, 2, KD * D], F16)
        DW = carve(BIG, "DW", 32768, [P, FCH, 2, KD * D], F16)
        GW, UW, DW = (a.rearrange("p c l (k f) -> p c l k f", k=KD) for a in (GW, UW, DW))
        hq = carve(BIG, "hq", 65536, [P, 2, F])
        he = carve(BIG, "he", 81920, [P, F])
        fhT = carve(BIG, "fhT", 90112, [P, 2, FT, P], F16)
        fxT = carve(BIG, "fxT", 98304, [P, 2, 2, D], F16)
        fx = carve(WORK, "fx", 0, [P, 2, D])
        fe = carve(WORK, "fe", 4096, [P, D])
        sg = carve(WORK, "sg", 6144, [P, 2, D])
        hsc = carve(WORK, "hsc", 10240, [P, 3, F // QB])
        xsc = carve(WORK, "xsc", 11008, [P, 3, NB])
        hsc_end = carve(WORK, "hsc_end", 11264, [P, FCH, 3, NB])
        wst = carve(BIG, "wst", 45056, [P, 4, NGRP, D])
        we = [carve(BIG, f"we{i}", at, [P, NGRP * D]) for i, at in enumerate((77824, 114688))]
        wsc = carve(BIG, "wsc", 86016, [P, 4, 3, NGRP * NB])
        wo = carve(BIG, "wo", 122880, [P, 2, 2, NGRP * D], F16)
        NW = 3 * FCH
        wdq_dram = nc.dram_tensor("wdq_scratch", [NW, P, 2 * NGRP * D], F16, kind="Internal").ap()

        fw_in = [sem(f"fw_in{i}") for i in range(4)]
        fw_st = [sem("fw_st0"), sem("fw_st1")]
        gw_in = sem("gw_in")
        uw_in = sem("uw_in")
        dw_in = sem("dw_in")

        class Quant:

            def __init__(self, name):
                self.inv_ok = sem(f"{name}_inv_ok")
                self.q_ok = sem(f"{name}_q_ok")
                self.up_ok = sem(f"{name}_up_ok")
                self.n_ok = sem(f"{name}_n_ok")
                self.dq_ok = sem(f"{name}_dq_ok")
                self.t_mm = sem(f"{name}_t_mm")
                self.t_hi = sem(f"{name}_t_hi")
                self.t_lo = sem(f"{name}_t_lo")

        QW, QX, QH = Quant("qw"), Quant("qx"), Quant("qh")
        gu_mm = sem("gu_mm")
        sg_ok = sem("sg_ok")
        h_ok = sem("h_ok")
        d_mm = sem("d_mm")
        x4_ok = sem("x4_ok")

        def blocks(a):
            return a.rearrange("p (n k) -> p n k", k=QB)

        def spread(a, n):
            return a.unsqueeze(2).to_broadcast([P, n, QB])

        def scales(link, src, sc, n, back):
            v = nc.vector
            link(v.tensor_reduce(sc[:, 0, :], blocks(src), AX_X, ALU.max, apply_absolute_value=True))
            link(v.tensor_scalar(sc[:, 0, :], sc[:, 0, :], 1.0 / 448.0, TINY, ALU.mult, ALU.max))
            link(v.tensor_scalar(sc[:, 2, :], sc[:, 0, :], -back, None, ALU.mult))
            return v.reciprocal(sc[:, 1, :], sc[:, 0, :])

        def round_e4m3(link, q, e):
            v = nc.vector
            link(v.tensor_scalar(e.bitcast(I32), e.bitcast(I32), 0x7F800000, 0x00400000, ALU.bitwise_and, ALU.bitwise_or))
            link(v.scalar_tensor_tensor(q, e, LEAST, q, ALU.max, ALU.add))
            return v.scalar_tensor_tensor(q, e, LEAST, q, ALU.max, ALU.subtract)

        def pool_q(pool, s, n, x, sc, nb):
            pool.wait_ge(s.inv_ok, n)
            nc.gpsimd.tensor_tensor(blocks(x), blocks(x), spread(sc[:, 1, :], nb), ALU.mult).then_inc(s.q_ok, 1)

        def pool_dq(pool, s, n, x, sc, nb):
            pool.wait_ge(s.n_ok, n)
            nc.gpsimd.tensor_tensor(blocks(x), blocks(x), spread(sc[:, 2, :], nb), ALU.mult).then_inc(s.dq_ok, 1)

        def act_up(act, s, n, x, e):
            act.wait_ge(s.q_ok, n)
            nc.scalar.activation(e, x, ACT.Copy, scale=2.0 ** 20).then_inc(s.up_ok, 1)

        def w_which(b, c):
            if c < 2:
                assert isinstance(b, int) and b == 0
                return c, 0
            if c >= 6:
                b, c = b + 1, c - 4
            return (c - 2, b + 1) if c < 4 else (2, b * 2 + (c - 4))

        def w_load(sp, b, c):
            m, j = w_which(b, c)
            if c >= 4:
                sp.wait_ge(QW.t_mm, b * 4 + (c - 3))
            if m < 2:
                src = (fgate_w, fup_w)[m].rearrange("(j i p) k -> p j i k", i=NGRP, p=P)
            else:
                src = fdown_w.rearrange("(i p) (j k) -> p j i k", p=P, k=D)
            sp.dma_start(wst[:, c % 4, :, :].unsqueeze(1), src[:, bass.ds(j, 1), :, :]).then_inc(fw_in[c % 4], 16)

        def w_store(sp, b, c):
            m, j = w_which(b, c)
            sp.wait_ge(QW.t_lo, b * 4 + (c + 1))
            sp.dma_start(wdq_dram[bass.ds(j + m * FCH, 1), :, :].rearrange("o p f -> (o p) f"),
                         wo[:, c % 2, :, :].rearrange("p l f -> p (l f)")).then_inc(fw_st[c % 2], 16)

        def w_flat(i):
            return wst[:, i % 4, :, :].rearrange("p i k -> p (i k)")

        def w_pool(pool, b, c):
            for p in range(2):
                pool_q(pool, QW, b * 4 + (c + p + 1), w_flat(c + p), wsc[:, (c + p) % 4], NGRP * NB)
            for p in range(2):
                pool_dq(pool, QW, b * 4 + (c + p + 1), w_flat(c + p), wsc[:, (c + p) % 4], NGRP * NB)

        def w_act_up(act, b, c):
            for p in range(2):
                act_up(act, QW, b * 4 + (c + p + 1), w_flat(c + p), we[p])

        def w_banks(p):
            return PS[:, 4 * p:4 * p + 4, :].rearrange("p k f -> p (k f)")

        def w_act_hi(act, b, c, first):
            for p in range(2):
                act.wait_ge(QW.t_mm, b * 4 + (c + p + 1))
                if not first:
                    act.wait_ge(fw_st[p], b * 32 + c // 2 * 16)
                nc.scalar.activation(wo[:, p, 0, :], w_banks(p), ACT.Copy).then_inc(QW.t_hi, 1)

        def w_transpose(pe, b, c, first):
            for p in range(2):
                if p == 1 and c < 4:
                    pe.wait_ge(sim_sb, b * R + (R if first else 2 * R))
                if c >= 4:
                    pe.wait_ge(QW.t_lo, b * 4 + (c + p - 1))
                pe.wait_ge(QW.dq_ok, b * 4 + (c + p + 1))
                for i in range(NGRP):
                    for k in range(KD):
                        ins = nc.tensor.transpose(bank[4 * p + k][:, i * P:(i + 1) * P],
                                                  wst[:, (c + p) % 4, i, k * P:(k + 1) * P], ident[:, :])
                ins.then_inc(QW.t_mm, 1)

        def w_scales(dve, link, b, c):
            for p in range(2):
                dve.wait_ge(fw_in[(c + p) % 4], b * 16 + ((c + p) // 4 + 1) * 16)
                scales(link, w_flat(c + p), wsc[:, (c + p) % 4], NGRP * NB, W_SCALE).then_inc(QW.inv_ok, 1)

        def w_round(dve, link, b, c):
            for p in range(2):
                dve.wait_ge(QW.up_ok, b * 4 + (c + p + 1))
                round_e4m3(link, w_flat(c + p), we[p]).then_inc(QW.n_ok, 1)

        def w_low(dve, b, c):
            for p in range(2):
                dve.wait_ge(QW.t_hi, b * 4 + (c + p + 1))
                nc.vector.tensor_tensor(wo[:, p, 1, :], w_banks(p), wo[:, p, 0, :], ALU.subtract).then_inc(QW.t_lo, 1)

        def x_scales(link, n, p):
            link(nc.vector.tensor_scalar(fx[:, p, :], X[:, n, :], MV[:, bass.ds(n, 1), 0], RSTD[:, bass.ds(n, 1)],
                                         ALU.subtract, ALU.mult))
            scales(link, fx[:, p, :], xsc, NB, A_SCALE).then_inc(QX.inv_ok, 1)

        def x_round(dve, link, n, p):
            dve.wait_ge(QX.up_ok, n + 1)
            round_e4m3(link, fx[:, p, :], fe).then_inc(QX.n_ok, 1)

        def x_up(act, n, p):
            act_up(act, QX, n + 1, fx[:, p, :], fe)

        def d_gpsimd(pool):
            def q_x(n, p):
                pool_q(pool, QX, n + 1, fx[:, p, :], xsc, NB)

            def dq_x(n, p):
                pool_dq(pool, QX, n + 1, fx[:, p, :], xsc, NB)

            def q_h(n, p):
                pool_q(pool, QH, n + 1, hq[:, p, :], hsc, F // QB)

            def dq_h(n, p):
                pool_dq(pool, QH, n + 1, hq[:, p, :], hsc, F // QB)

            q_x(0, 0)
            dq_x(0, 0)
            pool.wait_ge(x3_ok, 1)
            q_x(1, 1)
            dq_x(1, 1)
            q_h(0, 0)
            with pool.Fori(0, TT // 2 - 1) as j:
                for p in range(2):
                    n = j * 2 + (p + 1)
                    q_x(n + 1, p)
                    dq_h(n - 1, p)
                    dq_x(n + 1, p)
                    q_h(n, 1 - p)
            dq_h(TT - 2, 0)
            end = [hq[:, 1, c * D:(c + 1) * D] for c in range(FCH)]
            for c in range(FCH):
                pool_q(pool, QH, TT + c, end[c], hsc_end[:, c], NB)
                if c >= 1:
                    pool_dq(pool, QH, TT + c - 1, end[c - 1], hsc_end[:, c - 1], NB)
            pool_dq(pool, QH, TT + FCH - 1, end[-1], hsc_end[:, FCH - 1], NB)

        def d_scalar(act):
            def up_x(n, p):
                x_up(act, n, p)

            def hi_x(n, p):
                act.wait_ge(QX.t_mm, n + 1)
                nc.scalar.activation(fxT[:, p, 0, :], bank[7], ACT.Copy).then_inc(QX.t_hi, 1)

            def gate(n, c):
                act.wait_ge(gu_mm, n * FCH + (c + 1))
                nc.scalar.activation(sg[:, c % 2, :], bank[2 * (c % 2)], ACT.Silu, scale=FSCALE).then_inc(sg_ok, 1)

            def hi_h(n, c):
                act.wait_ge(QH.t_mm, n * FCH + (c + 1))
                nc.scalar.activation(fhT[:, 0, 4 * c:4 * c + 4, :], bank[4 + c % 2].rearrange("p (k f) -> p k f", k=4),
                                     ACT.Copy).then_inc(QH.t_hi, 1)

            def tile(n, p, first=False):
                gate(n, 0)
                gate(n, 1)
                up_x(n + 1, 1 - p)
                gate(n, 2)
                gate(n, 3)
                if not first:
                    hi_h(n - 1, 0)
                    hi_h(n - 1, 1)
                hi_x(n + 1, 1 - p)
                if not first:
                    hi_h(n - 1, 2)
                    hi_h(n - 1, 3)
                act_up(act, QH, n + 1, hq[:, p, :], he)

            hi_x(0, 0)
            tile(0, 0, first=True)
            with act.Fori(0, TT // 2 - 1) as j:
                for p in range(2):
                    tile(j * 2 + (p + 1), 1 - p)
            def up_end(c):
                act_up(act, QH, TT + c, hq[:, 1, c * D:(c + 1) * D], he[:, c * D:(c + 1) * D])

            gate(TT - 1, 0)
            gate(TT - 1, 1)
            up_end(0)
            gate(TT - 1, 2)
            up_end(1)
            gate(TT - 1, 3)
            hi_h(TT - 2, 0)
            hi_h(TT - 2, 1)
            up_end(2)
            hi_h(TT - 2, 2)
            up_end(3)
            hi_h(TT - 2, 3)
            for c in range(FCH):
                hi_h(TT - 1, c)

        def d_tensor(pe):
            def t_x(n, p):
                pe.wait_ge(QX.dq_ok, n + 1)
                for k in range(KD):
                    ins = nc.tensor.transpose(bank[7][:, k * P:(k + 1) * P], fx[:, p, k * P:(k + 1) * P], ident[:, :])
                ins.then_inc(QX.t_mm, 1)

            def gates(n, p, first):
                pe.wait_ge(QX.t_lo, n + 1)
                for c in range(FCH):
                    if not (first and c < 2):
                        pe.wait_ge(h_ok, n * FCH + (c - 1))
                    for w, b in ((GW, 2 * (c % 2)), (UW, 2 * (c % 2) + 1)):
                        i = 0
                        for k in range(KD):
                            for a, l in ((0, 0), (0, 1), (1, 0)):
                                ins = nc.tensor.matmul(bank[b], fxT[:, p, a, k * P:(k + 1) * P],
                                                       w[:, c, l, k, :], start=(i == 0), stop=(i == 3 * KD - 1))
                                i += 1
                    ins.then_inc(gu_mm, 1)

            def t_h(n, p, c, end=False):
                if end:
                    pe.wait_ge(QH.dq_ok, TT + c)
                elif c == 0:
                    pe.wait_ge(QH.dq_ok, n + 1)
                if c >= 2:
                    pe.wait_ge(QH.t_lo, n * FCH + (c - 1))
                for k in range(4):
                    ins = nc.tensor.transpose(bank[4 + c % 2][:, k * P:(k + 1) * P],
                                              hq[:, p, (4 * c + k) * P:(4 * c + k + 1) * P], ident[:, :])
                ins.then_inc(QH.t_mm, 1)

            def down(n, c):
                if c == 0:
                    pe.wait_ge(x4_ok, n + 1)
                pe.wait_ge(QH.t_lo, n * FCH + (c + 1))
                for k in range(4 * c, 4 * c + 4):
                    for i, (a, l) in enumerate(((0, 0), (0, 1), (1, 0))):
                        ins = nc.tensor.matmul(bank[6], fhT[:, a, k, :], DW[:, k // KD, l, k % KD, :],
                                               start=(k == 0 and i == 0), stop=(k == FT - 1 and i == 2))
                if c == FCH - 1:
                    ins.then_inc(d_mm, 1)

            def second(n, p, between, end=False):
                t_h(n, p, 0, end)
                t_h(n, p, 1, end)
                between()
                down(n, 0)
                t_h(n, p, 2, end)
                down(n, 1)
                t_h(n, p, 3, end)
                down(n, 2)
                down(n, 3)

            t_x(0, 0)
            pe.wait_ge(x3_ok, 1)
            pe.wait_ge(gw_in, 16 * FCH)
            pe.wait_ge(uw_in, 16 * FCH)
            gates(0, 0, True)
            t_x(1, 1)
            pe.wait_ge(dw_in, 16 * FCH)
            with pe.Fori(0, TT // 2 - 1) as j:
                for p in range(2):
                    n = j * 2 + (p + 1)
                    gates(n, 1 - p, False)
                    second(n - 1, p, lambda: t_x(n + 1, p))
            gates(TT - 1, 1, False)
            second(TT - 2, 0, lambda: None)
            second(TT - 1, 1, lambda: None, True)

        def d_vector(dve):
            link = Chain(dve, dve_chain)
            link.restart()
            v = nc.vector
            v.nop().then_inc(x4_ok, 1)
            link(v.tensor_scalar(GATES[:, 7:8], GATES[:, 3:4], FSCALE, None, ALU.mult))

            def x_first(n, p):
                x_scales(link, n, p)

            def x_second(n, p):
                x_round(dve, link, n, p)

            def x_third(n, p):
                dve.wait_ge(QX.t_hi, n + 1)
                v.tensor_tensor(fxT[:, p, 1, :], bank[7], fxT[:, p, 0, :], ALU.subtract).then_inc(QX.t_lo, 1)

            def hidden(n, p, c):
                dve.wait_ge(sg_ok, n * FCH + (c + 1))
                v.scalar_tensor_tensor(hq[:, p, c * D:(c + 1) * D], bank[2 * (c % 2) + 1], FSCALE, sg[:, c % 2, :],
                                       ALU.mult, ALU.mult).then_inc(h_ok, 1)

            def h_first(n, p):
                dve.wait_ge(h_ok, n * FCH + FCH)
                scales(link, hq[:, p, :], hsc, F // QB, A_SCALE).then_inc(QH.inv_ok, 1)

            def h_second(n, p, half):
                if half == 0:
                    dve.wait_ge(QH.up_ok, n + 1)
                part = slice(half * (F // 2), (half + 1) * (F // 2))
                ins = round_e4m3(link, hq[:, p, part], he[:, part])
                if half == 0:
                    link(ins)
                else:
                    ins.then_inc(QH.n_ok, 1)

            def h_third(n, chunks):
                for c in chunks:
                    dve.wait_ge(QH.t_hi, n * FCH + (c + 1))
                    v.tensor_tensor(fhT[:, 1, 4 * c:4 * c + 4, :], bank[4 + c % 2].rearrange("p (k f) -> p k f", k=4),
                                    fhT[:, 0, 4 * c:4 * c + 4, :], ALU.subtract).then_inc(QH.t_lo, 1)

            def add(n):
                dve.wait_ge(d_mm, n + 1)
                v.scalar_tensor_tensor(X[:, n, :], bank[6], GATES[:, 7:8], X[:, n, :], ALU.mult, ALU.add).then_inc(x4_ok, 1)

            x_third(0, 0)
            x_first(1, 1)
            dve.wait_ge(row_mv, B)
            rsqrt(link, MV[:, TT - R:TT, 1], RSTD[:, TT - R:TT], R)
            for c in range(FCH):
                hidden(0, 0, c)
            x_second(1, 1)
            x_third(1, 1)
            h_first(0, 0)
            with dve.Fori(0, TT // 2 - 1) as j:
                link.restart()
                for p in range(2):
                    n = j * 2 + (p + 1)
                    x_first(n + 1, p)
                    h_second(n - 1, p, 0)
                    hidden(n, 1 - p, 0)
                    h_second(n - 1, p, 1)
                    hidden(n, 1 - p, 1)
                    x_second(n + 1, p)
                    hidden(n, 1 - p, 2)
                    hidden(n, 1 - p, 3)
                    h_third(n - 1, (0, 1))
                    x_third(n + 1, p)
                    h_third(n - 1, (2, 3))
                    h_first(n, 1 - p)
                    add(n - 1)
            link.restart()
            def end_first(c):
                dve.wait_ge(h_ok, (TT - 1) * FCH + (c + 1))
                scales(link, hq[:, 1, c * D:(c + 1) * D], hsc_end[:, c], NB, A_SCALE).then_inc(QH.inv_ok, 1)

            def end_second(c):
                dve.wait_ge(QH.up_ok, TT + c)
                round_e4m3(link, hq[:, 1, c * D:(c + 1) * D], he[:, c * D:(c + 1) * D]).then_inc(QH.n_ok, 1)

            h_second(TT - 2, 0, 0)
            hidden(TT - 1, 1, 0)
            h_second(TT - 2, 0, 1)
            end_first(0)
            hidden(TT - 1, 1, 1)
            end_first(1)
            end_second(0)
            hidden(TT - 1, 1, 2)
            end_first(2)
            end_second(1)
            hidden(TT - 1, 1, 3)
            end_first(3)
            h_third(TT - 2, (0, 1))
            end_second(2)
            h_third(TT - 2, (2,))
            end_second(3)
            h_third(TT - 2, (3,))
            add(TT - 2)
            h_third(TT - 1, range(FCH))
            add(TT - 1)

        def end_sync(sp):
            for b in range(B):
                sp.wait_ge(x4_ok, (b + 1) * R + 1)
                sp.dma_start(out_rows[:, b * R:(b + 1) * R, :], X[:, b * R:(b + 1) * R, :]).then_inc(out_done, 16)
            sp.wait_ge(out_done, 16 * B)

        @block.sync
        def _(sp):
            a_sync(sp)
            b_sync(sp)
            c_sync(sp)
            end_sync(sp)

        @block.gpsimd
        def _(pool):
            a_gpsimd(pool)
            b_gpsimd(pool)
            c_gpsimd(pool)
            d_gpsimd(pool)

        @block.scalar
        def _(act):
            a_scalar(act)
            b_scalar(act)
            c_scalar(act)
            d_scalar(act)

        @block.tensor
        def _(pe):
            a_tensor(pe)
            b_tensor(pe)
            c_tensor(pe)
            d_tensor(pe)

        @block.vector
        def _(dve):
            a_vector(dve)
            b_vector(dve)
            c_vector(dve)
            d_vector(dve)


_INS = ["x", "ctx_512", "g_xattn", "g_ffn", "L0_xattn_Wq", "L0_xattn_Wk", "L0_xattn_gamma_raw", "L0_ffn_gate_w",
        "L0_ffn_w1", "L0_ffn_w3", "L0_ffn_w2", "L0_ffn_sw1", "L0_ffn_sw3", "L0_ffn_sw2", "L1_ffn_gate_w",
        "L1_ffn_up_w", "L1_ffn_down_w"]
_OUTS = [((4, 512, 512), "float32")]


def kernel(**inputs):
    import numpy as _np
    import concourse.bacc as _bacc
    from concourse import mybir as _mybir
    from concourse.bass_utils import run_bass_kernel_spmd as _run

    nc = _bacc.Bacc("TRN2", target_bir_lowering=False, num_devices=1)
    arrays, args = {}, []
    for name in _INS:
        a = _np.ascontiguousarray(inputs[name])
        if a.ndim == 0:
            a = a.reshape(1)
        arrays[f"in_{name}_dram"] = a
        args.append(nc.dram_tensor(f"in_{name}_dram", a.shape, _mybir.dt.from_np(a.dtype), kind="ExternalInput").ap())
    for i, (shape, dtype) in enumerate(_OUTS):
        dt = _mybir.dt.from_np(_np.dtype(dtype))
        args.append(nc.dram_tensor(f"out_{i}_dram", shape, dt, kind="ExternalOutput").ap())
    build(nc, *args)
    r = _run(nc, [arrays], core_ids=[0])
    got = tuple(r.results[0][f"out_{i}_dram"] for i in range(len(_OUTS)))
    return got[0]
```
